# Optimizing a Trainium2 kernel written in Bass

```python
import numpy as np
import jax
import jax.numpy as jnp

def _softmax(x, axis=-1):
    return jax.nn.softmax(x, axis=axis)

def _gelu(x):
    return jax.nn.gelu(x, approximate=True)

def _silu(x):
    return jax.nn.silu(x)

def _sigmoid(x):
    return jax.nn.sigmoid(x)

def _layernorm(x, axis=-1, eps=1e-05):
    m = jnp.mean(x, axis=axis, keepdims=True)
    v = jnp.var(x, axis=axis, keepdims=True)
    return (x - m) / jnp.sqrt(v + eps)

def _scatter_add(tgt, idx, src, axis=0):
    return tgt.at[idx].add(src)

def _segment_sum(src, seg, n):
    return jax.ops.segment_sum(src, seg, n)
kernel_name = 'mk_gnn_resnorm_d4_gnn_r32_2af194'

def setup_inputs(seed: int=0):
    np.random.seed(seed)
    _w = jnp.asarray

    def _rec_inputs():
        import jax
        import jax.numpy as jnp
        _gk = jax.random.key(seed)
        x = -0.0003713 + 1 * jax.random.normal(jax.random.fold_in(_gk, 1), (3125, 128), jnp.float32)
        src = jax.random.randint(jax.random.fold_in(_gk, 2), (50000,), 0, 3125, jnp.int32)
        dst = jnp.minimum((3125 * jax.random.uniform(jax.random.fold_in(_gk, 3), (50000,)) ** 2.0).astype(jnp.int32), 99999)
        _o = jnp.argsort(dst, stable=True)
        src = src[_o]
        dst = dst[_o]
        edge_type_8 = jax.random.randint(jax.random.fold_in(_gk, 13), (50000,), 0, 8, jnp.int32)
        return (x, src, dst, edge_type_8)
    x, src, dst, edge_type_8 = _rec_inputs()

    def _L0_gnn_setup():
        import jax, jax.numpy as jnp
        import numpy as np
        N_NODES = 3125
        N_EDGES = 100000
        N_REL = 8
        EMB = 128
        key = jax.random.key(seed)
        k1, k2, k3, k4, k5 = jax.random.split(key, 5)
        node_emb = jax.random.normal(k1, (N_NODES, EMB), dtype=jnp.float32)
        weights = jax.random.normal(k2, (N_REL, EMB, EMB), dtype=jnp.float32)
        src = jax.random.randint(k3, (N_EDGES,), 0, N_NODES, dtype=jnp.int64 if jax.config.jax_enable_x64 else jnp.int32).astype(jnp.int64)
        rel = jax.random.randint(k4, (N_EDGES,), 0, N_REL).astype(jnp.int64)
        dst = jax.random.randint(k5, (N_EDGES,), 0, N_NODES).astype(jnp.int64)
        return {'node_emb': node_emb, 'weights': weights, 'src': src, 'rel': rel, 'dst': dst}
    _L0_gnn_all = _L0_gnn_setup()
    _L0_gnn_in = {k: v for k, v in _L0_gnn_all.items() if k in ('weights',)}
    del _L0_gnn_all

    def _L1_gnn_setup():
        import jax, jax.numpy as jnp
        import numpy as np
        N_NODES = 3125
        N_EDGES = 20000
        D_IN = 128
        D_OUT = 128
        BN_EPS = 1e-05
        LEAKY_SLOPE = 0.01
        key = jax.random.key(seed)
        k1, k2, k3, k4, k5, k6 = jax.random.split(key, 6)
        x = jax.random.normal(k1, (N_NODES, D_IN), dtype=jnp.float32)
        edge_index = jax.random.randint(k2, (2, N_EDGES), 0, N_NODES, dtype=jnp.int64)
        W = jax.random.normal(k3, (D_IN, D_OUT), dtype=jnp.float32) * (1.0 / np.sqrt(D_IN))
        b = jax.random.normal(k4, (D_OUT,), dtype=jnp.float32) * 0.01
        gamma = jnp.ones((D_OUT,), dtype=jnp.float32) + 0.1 * jax.random.normal(k5, (D_OUT,), dtype=jnp.float32)
        beta = 0.1 * jax.random.normal(k6, (D_OUT,), dtype=jnp.float32)
        return {'x': x, 'edge_index': edge_index, 'W': W, 'b': b, 'gamma': gamma, 'beta': beta}
    _L1_gnn_all = _L1_gnn_setup()
    _L1_gnn_in = {k: v for k, v in _L1_gnn_all.items() if k in ('W', 'b', 'gamma', 'beta')}
    del _L1_gnn_all

    def _L2_gnn_setup():
        import jax, jax.numpy as jnp
        import numpy as np
        HEADS = 4
        NEG_SLOPE = 0.2
        LN_EPS = 1e-05

        def _gatv2(x, src, dst, W_l, b_l, W_r, b_r, att, gat_bias, N):
            D = x.shape[1]
            H, C = (HEADS, D)
            xl = (x @ W_l + b_l).reshape(N, H, C)
            xr = (x @ W_r + b_r).reshape(N, H, C)
            e = jax.nn.leaky_relu(xl[src] + xr[dst], NEG_SLOPE)
            alpha = jnp.einsum('ehc,hc->eh', e, att)
            amax = jax.ops.segment_max(alpha, dst, num_segments=N)
            ex = jnp.exp(alpha - amax[dst])
            denom = jax.ops.segment_sum(ex, dst, num_segments=N)
            w = ex / (denom[dst] + 1e-16)
            msg = xl[src] * w[:, :, None]
            out = jax.ops.segment_sum(msg, dst, num_segments=N)
            return out.mean(axis=1) + gat_bias
        key = jax.random.key(seed)
        ks = jax.random.split(key, 12)
        N, D, E = (50000, 128, 12500)
        H, C = (HEADS, D)
        s = 0.05
        x = jax.random.normal(ks[0], (N, D), dtype=jnp.float32)
        edge_index = jax.random.randint(ks[1], (2, E), 0, N, dtype=jnp.int64)
        return {'x': x, 'edge_index': edge_index, 'W_l': jax.random.normal(ks[2], (D, H * C), dtype=jnp.float32) * s, 'b_l': jnp.zeros((H * C,), jnp.float32), 'W_r': jax.random.normal(ks[3], (D, H * C), dtype=jnp.float32) * s, 'b_r': jnp.zeros((H * C,), jnp.float32), 'att': jax.random.normal(ks[4], (H, C), dtype=jnp.float32) * s, 'gat_bias': jnp.zeros((C,), jnp.float32), 'ln_g': jnp.ones((D,), jnp.float32), 'ln_b': jnp.zeros((D,), jnp.float32), 'W1': jax.random.normal(ks[5], (D, 2 * D), dtype=jnp.float32) * s, 'b1': jnp.zeros((2 * D,), jnp.float32), 'W2': jax.random.normal(ks[6], (2 * D, D), dtype=jnp.float32) * s, 'b2': jnp.zeros((D,), jnp.float32)}
    _L2_gnn_all = _L2_gnn_setup()
    _L2_gnn_in = {k: v for k, v in _L2_gnn_all.items() if k in ('W_l', 'b_l', 'W_r', 'b_r', 'att', 'gat_bias', 'ln_g', 'ln_b', 'W1', 'b1', 'W2', 'b2')}
    del _L2_gnn_all

    def _L3_gnn_setup():
        import jax, jax.numpy as jnp
        import numpy as np
        N_NODES = 625
        N_EDGES = 20000
        IN_CH = 128
        HID = 32
        HEADS = 4

        def _linear_params(key, fan_in, fan_out):
            kw, kb = jax.random.split(key)
            s = 1.0 / np.sqrt(fan_in)
            W = jax.random.uniform(kw, (fan_in, fan_out), jnp.float32, -s, s)
            b = jax.random.uniform(kb, (fan_out,), jnp.float32, -s, s)
            return (W, b)

        def transformer_conv(x, edge_index, Wq, bq, Wk, bk, Wv, bv, Ws, bs):
            N = x.shape[0]
            H, C = (HEADS, HID)
            src, dst = (edge_index[0], edge_index[1])
            q = (x @ Wq + bq).reshape(N, H, C)
            k = (x @ Wk + bk).reshape(N, H, C)
            v = (x @ Wv + bv).reshape(N, H, C)
            alpha = jnp.einsum('ehc,ehc->eh', q[dst], k[src]) / jnp.sqrt(jnp.float32(C))
            amax = jax.ops.segment_max(alpha, dst, num_segments=N)
            ealpha = jnp.exp(alpha - amax[dst])
            denom = jax.ops.segment_sum(ealpha, dst, num_segments=N)
            attn = ealpha / denom[dst]
            out = jax.ops.segment_sum(attn[..., None] * v[src], dst, num_segments=N)
            return out.reshape(N, H * C) + x @ Ws + bs
        key = jax.random.key(seed)
        keys = jax.random.split(key, 10)
        x = jax.random.normal(keys[0], (N_NODES, IN_CH), jnp.float32)
        edge_index = jax.random.randint(keys[1], (2, N_EDGES), 0, N_NODES, jnp.int64)
        HC = HEADS * HID
        inp = {'x': x, 'edge_index': edge_index}
        names = ['q', 'k', 'v', 's']
        for li, in_dim in ((1, IN_CH), (2, HC)):
            for j, nm in enumerate(names):
                W, b = _linear_params(keys[2 + (li - 1) * 4 + j], in_dim, HC)
                inp[f'W{nm}{li}'] = W
                inp[f'b{nm}{li}'] = b
        return inp
    _L3_gnn_all = _L3_gnn_setup()
    _L3_gnn_in = {k: v for k, v in _L3_gnn_all.items() if k in ('Wq1', 'bq1', 'Wk1', 'bk1', 'Wv1', 'bv1', 'Ws1', 'bs1', 'Wq2', 'bq2', 'Wk2', 'bk2', 'Wv2', 'bv2', 'Ws2', 'bs2')}
    del _L3_gnn_all
    return {'x': x, 'src': src, 'dst': dst, 'edge_type_8': edge_type_8, 'L0_gnn_weights': _L0_gnn_in['weights'], 'L1_gnn_W': _L1_gnn_in['W'], 'L1_gnn_b': _L1_gnn_in['b'], 'L1_gnn_gamma': _L1_gnn_in['gamma'], 'L1_gnn_beta': _L1_gnn_in['beta'], 'L2_gnn_W_l': _L2_gnn_in['W_l'], 'L2_gnn_b_l': _L2_gnn_in['b_l'], 'L2_gnn_W_r': _L2_gnn_in['W_r'], 'L2_gnn_b_r': _L2_gnn_in['b_r'], 'L2_gnn_att': _L2_gnn_in['att'], 'L2_gnn_gat_bias': _L2_gnn_in['gat_bias'], 'L2_gnn_ln_g': _L2_gnn_in['ln_g'], 'L2_gnn_ln_b': _L2_gnn_in['ln_b'], 'L2_gnn_W1': _L2_gnn_in['W1'], 'L2_gnn_b1': _L2_gnn_in['b1'], 'L2_gnn_W2': _L2_gnn_in['W2'], 'L2_gnn_b2': _L2_gnn_in['b2'], 'L3_gnn_Wq1': _L3_gnn_in['Wq1'], 'L3_gnn_bq1': _L3_gnn_in['bq1'], 'L3_gnn_Wk1': _L3_gnn_in['Wk1'], 'L3_gnn_bk1': _L3_gnn_in['bk1'], 'L3_gnn_Wv1': _L3_gnn_in['Wv1'], 'L3_gnn_bv1': _L3_gnn_in['bv1'], 'L3_gnn_Ws1': _L3_gnn_in['Ws1'], 'L3_gnn_bs1': _L3_gnn_in['bs1'], 'L3_gnn_Wq2': _L3_gnn_in['Wq2'], 'L3_gnn_bq2': _L3_gnn_in['bq2'], 'L3_gnn_Wk2': _L3_gnn_in['Wk2'], 'L3_gnn_bk2': _L3_gnn_in['bk2'], 'L3_gnn_Wv2': _L3_gnn_in['Wv2'], 'L3_gnn_bv2': _L3_gnn_in['bv2'], 'L3_gnn_Ws2': _L3_gnn_in['Ws2'], 'L3_gnn_bs2': _L3_gnn_in['bs2']}

def reference(x, src, dst, edge_type_8, L0_gnn_weights, L1_gnn_W, L1_gnn_b, L1_gnn_gamma, L1_gnn_beta, L2_gnn_W_l, L2_gnn_b_l, L2_gnn_W_r, L2_gnn_b_r, L2_gnn_att, L2_gnn_gat_bias, L2_gnn_ln_g, L2_gnn_ln_b, L2_gnn_W1, L2_gnn_b1, L2_gnn_W2, L2_gnn_b2, L3_gnn_Wq1, L3_gnn_bq1, L3_gnn_Wk1, L3_gnn_bk1, L3_gnn_Wv1, L3_gnn_bv1, L3_gnn_Ws1, L3_gnn_bs1, L3_gnn_Wq2, L3_gnn_bq2, L3_gnn_Wk2, L3_gnn_bk2, L3_gnn_Wv2, L3_gnn_bv2, L3_gnn_Ws2, L3_gnn_bs2):
    import jax
    import jax.numpy as jnp

    def _L0_gnn_ref(node_emb, weights, src, rel, dst):
        import jax, jax.numpy as jnp
        import numpy as np
        N_NODES = 3125
        N_EDGES = 100000
        N_REL = 8
        EMB = 128
        n, e = node_emb.shape
        r = weights.shape[0]
        row = src + n * rel
        ones = jnp.ones(row.shape, dtype=node_emb.dtype)
        deg = jax.ops.segment_sum(ones, row, num_segments=r * n)
        inv = 1.0 / deg
        msg = node_emb[dst] * inv[row][:, None]
        agg = jax.ops.segment_sum(msg, row, num_segments=r * n)
        agg = agg.reshape(r, n, e)
        out = jnp.einsum('rij,rnj->ni', weights, agg)
        return jax.nn.relu(out)

    def _L1_gnn_ref(x, edge_index, W, b, gamma, beta):
        import jax, jax.numpy as jnp
        import numpy as np
        N_NODES = 3125
        N_EDGES = 20000
        D_IN = 128
        D_OUT = 128
        BN_EPS = 1e-05
        LEAKY_SLOPE = 0.01
        N = x.shape[0]
        src, dst = (edge_index[0], edge_index[1])
        deg = 1.0 + jax.ops.segment_sum(jnp.ones_like(src, dtype=x.dtype), dst, num_segments=N)
        dinv = jax.lax.rsqrt(deg)
        h = x @ W
        msgs = (dinv[src] * dinv[dst])[:, None] * h[src]
        agg = jax.ops.segment_sum(msgs, dst, num_segments=N)
        agg = agg + h / deg[:, None]
        out = agg + b
        out = jnp.where(out >= 0, out, LEAKY_SLOPE * out)
        mean = out.mean(axis=0)
        var = out.var(axis=0)
        out = (out - mean) * jax.lax.rsqrt(var + BN_EPS) * gamma + beta
        return out

    def _L2_gnn_ref(x, edge_index, W_l, b_l, W_r, b_r, att, gat_bias, ln_g, ln_b, W1, b1, W2, b2):
        import jax, jax.numpy as jnp
        import numpy as np
        HEADS = 4
        NEG_SLOPE = 0.2
        LN_EPS = 1e-05

        def _gatv2(x, src, dst, W_l, b_l, W_r, b_r, att, gat_bias, N):
            D = x.shape[1]
            H, C = (HEADS, D)
            xl = (x @ W_l + b_l).reshape(N, H, C)
            xr = (x @ W_r + b_r).reshape(N, H, C)
            e = jax.nn.leaky_relu(xl[src] + xr[dst], NEG_SLOPE)
            alpha = jnp.einsum('ehc,hc->eh', e, att)
            amax = jax.ops.segment_max(alpha, dst, num_segments=N)
            ex = jnp.exp(alpha - amax[dst])
            denom = jax.ops.segment_sum(ex, dst, num_segments=N)
            w = ex / (denom[dst] + 1e-16)
            msg = xl[src] * w[:, :, None]
            out = jax.ops.segment_sum(msg, dst, num_segments=N)
            return out.mean(axis=1) + gat_bias
        N = x.shape[0]
        loops = jnp.arange(N, dtype=edge_index.dtype)
        src = jnp.concatenate([edge_index[0], loops])
        dst = jnp.concatenate([edge_index[1], loops])
        h = x + _gatv2(x, src, dst, W_l, b_l, W_r, b_r, att, gat_bias, N)
        mu = h.mean(-1, keepdims=True)
        var = ((h - mu) ** 2).mean(-1, keepdims=True)
        hn = (h - mu) * jax.lax.rsqrt(var + LN_EPS) * ln_g + ln_b
        ffn = jax.nn.leaky_relu(hn @ W1 + b1, NEG_SLOPE) @ W2 + b2
        return hn + ffn

    def _L3_gnn_ref(x, edge_index, Wq1, bq1, Wk1, bk1, Wv1, bv1, Ws1, bs1, Wq2, bq2, Wk2, bk2, Wv2, bv2, Ws2, bs2):
        import jax, jax.numpy as jnp
        import numpy as np
        N_NODES = 625
        N_EDGES = 20000
        IN_CH = 128
        HID = 32
        HEADS = 4

        def _linear_params(key, fan_in, fan_out):
            kw, kb = jax.random.split(key)
            s = 1.0 / np.sqrt(fan_in)
            W = jax.random.uniform(kw, (fan_in, fan_out), jnp.float32, -s, s)
            b = jax.random.uniform(kb, (fan_out,), jnp.float32, -s, s)
            return (W, b)

        def transformer_conv(x, edge_index, Wq, bq, Wk, bk, Wv, bv, Ws, bs):
            N = x.shape[0]
            H, C = (HEADS, HID)
            src, dst = (edge_index[0], edge_index[1])
            q = (x @ Wq + bq).reshape(N, H, C)
            k = (x @ Wk + bk).reshape(N, H, C)
            v = (x @ Wv + bv).reshape(N, H, C)
            alpha = jnp.einsum('ehc,ehc->eh', q[dst], k[src]) / jnp.sqrt(jnp.float32(C))
            amax = jax.ops.segment_max(alpha, dst, num_segments=N)
            ealpha = jnp.exp(alpha - amax[dst])
            denom = jax.ops.segment_sum(ealpha, dst, num_segments=N)
            attn = ealpha / denom[dst]
            out = jax.ops.segment_sum(attn[..., None] * v[src], dst, num_segments=N)
            return out.reshape(N, H * C) + x @ Ws + bs
        h = transformer_conv(x, edge_index, Wq1, bq1, Wk1, bk1, Wv1, bv1, Ws1, bs1)
        h = jax.nn.relu(h)
        out = transformer_conv(h, edge_index, Wq2, bq2, Wk2, bk2, Wv2, bv2, Ws2, bs2)
        return out
    edge_index = jnp.stack([src, dst])
    x = _layernorm(x + _L0_gnn_ref(x, L0_gnn_weights, src, edge_type_8, dst), axis=-1)
    x = _layernorm(x + _L1_gnn_ref(x, edge_index, L1_gnn_W, L1_gnn_b, L1_gnn_gamma, L1_gnn_beta), axis=-1)
    x = _layernorm(x + _L2_gnn_ref(x, edge_index, L2_gnn_W_l, L2_gnn_b_l, L2_gnn_W_r, L2_gnn_b_r, L2_gnn_att, L2_gnn_gat_bias, L2_gnn_ln_g, L2_gnn_ln_b, L2_gnn_W1, L2_gnn_b1, L2_gnn_W2, L2_gnn_b2), axis=-1)
    x = _layernorm(x + _L3_gnn_ref(x, edge_index, L3_gnn_Wq1, L3_gnn_bq1, L3_gnn_Wk1, L3_gnn_bk1, L3_gnn_Wv1, L3_gnn_bv1, L3_gnn_Ws1, L3_gnn_bs1, L3_gnn_Wq2, L3_gnn_bq2, L3_gnn_Wk2, L3_gnn_bk2, L3_gnn_Wv2, L3_gnn_bv2, L3_gnn_Ws2, L3_gnn_bs2), axis=-1)
    return x

_drawn_inputs = setup_inputs


def setup_inputs(seed=0):
    import zlib

    import numpy as np

    out = dict(_drawn_inputs(seed))
    spreads = {'L2_gnn_b_l': (0.0, 0.1),
     'L2_gnn_b_r': (0.0, 0.8),
     'L2_gnn_gat_bias': (0.0, 0.1),
     'L2_gnn_ln_g': (1.0, 0.2),
     'L2_gnn_ln_b': (0.0, 0.1),
     'L2_gnn_b1': (0.0, 0.311),
     'L2_gnn_b2': (0.0, 0.1)}
    factors = {'L1_gnn_b': 4.12,
     'L2_gnn_W_r': 8.0,
     'L2_gnn_att': 6.314,
     'L3_gnn_bq1': 8.0,
     'L3_gnn_bk1': 8.0,
     'L3_gnn_Wq2': 8.0,
     'L3_gnn_bq2': 8.0,
     'L3_gnn_Wk2': 8.0,
     'L3_gnn_bk2': 8.0}
    for name, (base, spread) in spreads.items():
        noise = np.random.default_rng([zlib.crc32(name.encode()), seed]).standard_normal(out[name].shape)
        drawn = base * np.exp(spread * noise) if base else spread * noise
        out[name] = jnp.asarray(drawn.astype(out[name].dtype))
    for name, factor in factors.items():
        out[name] = (out[name] * factor).astype(out[name].dtype)
    return out
```

```python
import itertools
import numpy as np
import concourse.bass as bass
import concourse.mybir as mybir
from contextlib import ExitStack

F32, BF16, I32, U32 = mybir.dt.float32, mybir.dt.bfloat16, mybir.dt.int32, mybir.dt.uint32
ALU, ACT, AX = mybir.AluOpType, mybir.ActivationFunctionType, mybir.AxisListType.X

N, E, D, R, H = 3125, 50000, 128, 8, 4
Q, W = 125, 25
P = 128
C = 32
TILES = 392
CH = 98
NCH = TILES // CH
FULL, REST = E // P, E % P
PAIRS = 416
G = 4
PAD_DST, PAD_SRC = 4000, 3200
ROWLO, ROWHI = 128, 196
ACCROWS = 27 * P
DUMP = 26 * P
BIG = 1.0e30
EPS = 1e-5
SLOTPAD = PAIRS + 4 * G
BLOCKS = H * PAIRS // P
assert TILES * P >= E and FULL + W <= PAIRS and Q * W == N and R * N <= ROWLO * ROWHI


PHASE = itertools.count()


class Mem:
    pass


def scope(nc, ctx):
    n = next(PHASE)
    sems = []

    def clear_semaphores():
        if sems:
            with nc.Block() as block:
                @block.gpsimd
                def _(pool):
                    for s in sems:
                        pool.sem_clear(s)

    ctx.callback(clear_semaphores)

    def sb(name, shape, dt=F32):
        return ctx.enter_context(nc.sbuf_tensor(f"{name}_{n}", shape, dt))

    def sem(name):
        sems.append(ctx.enter_context(nc.semaphore(f"{name}_{n}")))
        return sems[-1]

    def bank(name, shape=(P, 512), dt=F32):
        return ctx.enter_context(nc.psum_tensor(f"{name}_{n}", list(shape), dt))

    return sb, sem, bank

def bc_mid(ap, n):
    return ap.unsqueeze(1).broadcast_to([ap.shape[0], n, ap.shape[1]])


def bc_last(ap, n):
    return ap.unsqueeze(2).broadcast_to([ap.shape[0], ap.shape[1], n])


def row_bc(ap, n):
    return ap.rearrange("(o n) -> o n", o=1).broadcast_to([n, ap.shape[0]])


def nodes(ap):
    return ap.rearrange("(w q) d -> q w d", q=Q)


def setup_phase(nc, m, ins):
    with ExitStack() as ctx:
        sb, sem, bank = scope(nc, ctx)

        nat_i = sb("nat_i", [CH, 3, NCH, P], I32)
        row_i = sb("row_i", [CH, 3, NCH, P], I32)
        nat = sb("nat", [CH, 2, NCH, P])
        win = sb("win", [CH, NCH, P])
        quant = sb("quant", [CH, 5, NCH, P])
        edge_flags = sb("edge_flags", [CH, 2, NCH, P])
        below = sb("below", [CH, NCH, W])
        thresholds = sb("thresholds", [P, W])
        tile_no = sb("tile_no", [P, NCH])
        pick = sb("pick", [CH, NCH, PAIRS])
        ones = sb("ones", [P, P])
        ends = sb("ends", [P, W])
        pair_tile = sb("pair_tile", [P, PAIRS])
        last0 = sb("last0", [P, 2, PAIRS])
        same = sb("same", [P, 4, PAIRS])
        io = sb("io", [P, 512], I32)
        io2 = sb("io2", [P, NCH], I32)
        ps = [bank(f"ps{i}") for i in range(8)]
        loaded, consts, chain = sem("edges_loaded"), sem("consts"), sem("dve_chain")
        padded, quant_ready, lanes_done = sem("padded"), sem("quant_ready"), sem("lanes_done")
        lanes_read, below_ready, ends_done = sem("lanes_read"), sem("below_ready"), sem("ends_done")
        pick_ready, slots_done, slots_read = sem("pick_ready"), sem("slots_done"), sem("slots_read")
        pens_ready, pens_turned = sem("pens_ready"), sem("pens_turned")
        start_pen = sb("start_pen", [P, H, PAIRS])
        end_pen = sb("end_pen", [P, H, PAIRS])
        block = ctx.enter_context(nc.Block())

        @block.sync
        def _(sp):
            sp.wait_ge(padded, 1)
            for k, name in enumerate(("src", "dst", "edge_type_8")):
                a = ins[name]
                for c in range(NCH):
                    rows = min(CH, FULL - CH * c)
                    sp.dma_start(nat_i[0:rows, k, c, :],
                                 a[c * CH * P:(c * CH + rows) * P].rearrange("(t l) -> t l", l=P)).then_inc(loaded, 16)
                    if rows < CH:
                        sp.dma_start(nat_i[rows:rows + 1, k, c, 0:REST],
                                     a[FULL * P:E].rearrange("(o l) -> o l", o=1)).then_inc(loaded, 16)
            sp.dma_start(m.x[:, :, :], nodes(ins["x"])).then_inc(loaded, 16)
            sp.wait_ge(loaded, 16 * (3 * (NCH + 1) + 1))

        @block.gpsimd
        def _(pool):
            pool.memset(nat_i[:, 0, :, :], PAD_SRC).then_inc(consts, 1)
            pool.memset(nat_i[:, 1, :, :], PAD_DST).then_inc(consts, 1)
            pool.memset(nat_i[:, 2, :, :], 0).then_inc(consts, 1)
            pool.wait_ge(consts, 3)
            pool.sem_inc(padded, 1)
            pool.memset(m.ident[:, :], 0.0).then_inc(consts, 1)
            pool.memset(m.rows_before[:, :], 1.0).then_inc(consts, 1)
            pool.memset(m.only0[:, :], 0.0).then_inc(consts, 1)
            pool.memset(m.only127[:, :], 0.0).then_inc(consts, 1)
            pool.memset(ones[:, :], 1.0).then_inc(consts, 1)
            pool.iota(io[:, :], [[1, 512]], base=0, channel_multiplier=0).then_inc(consts, 1)
            pool.iota(io2[:, :], [[CH, NCH]], base=0, channel_multiplier=1).then_inc(consts, 1)
            pool.wait_ge(consts, 10)
            pool.affine_select(out=m.ident[:, :], in_=m.ident[:, :], compare_op=ALU.not_equal, fill=1.0,
                               base=0, pattern=[[-1, P]], channel_multiplier=1).then_inc(consts, 1)
            pool.affine_select(out=m.rows_before[:, :], in_=m.rows_before[:, :], compare_op=ALU.is_gt, fill=0.0,
                               base=0, pattern=[[-1, P]], channel_multiplier=1).then_inc(consts, 1)
            pool.affine_select(out=m.only0[:, :], in_=m.only0[:, :], compare_op=ALU.not_equal, fill=1.0,
                               base=0, pattern=[[0, P]], channel_multiplier=1).then_inc(consts, 1)
            pool.affine_select(out=m.only127[:, :], in_=m.only127[:, :], compare_op=ALU.not_equal, fill=1.0,
                               base=-(P - 1), pattern=[[0, P]], channel_multiplier=1).then_inc(consts, 1)

        @block.vector
        def _(dve):
            v, count = nc.vector, [0]

            def link(op):
                count[0] += 1
                op.then_inc(chain, 1)
                dve.wait_ge(chain, count[0])

            dve.wait_ge(consts, 14)
            v.tensor_copy(m.iota[:, :], io[:, :]).then_inc(chain, 1)
            v.tensor_copy(tile_no[:, :], io2[:, :]).then_inc(chain, 1)
            v.tensor_copy(m.lane[:, :], io2[:, 0:1]).then_inc(chain, 1)
            v.tensor_copy(m.ident_b[:, :], m.ident[:, :]).then_inc(chain, 1)
            v.memset(m.pair_src[:, PAIRS:SLOTPAD], 0).then_inc(chain, 1)
            v.memset(m.y_row[:, TILES:TILES + 8], 0).then_inc(chain, 1)
            v.memset(m.src_lane[:, TILES:TILES + 8], 0.0).then_inc(chain, 1)
            v.memset(m.pair_dst[:, PAIRS:PAIRS + G], -1.0).then_inc(chain, 1)
            v.memset(m.small[:, PAIRS:PAIRS + G, :], 0.0).then_inc(chain, 1)
            count[0] = 9
            dve.wait_ge(chain, 9)
            link(v.tensor_copy(m.iota_b[:, :], m.iota[:, 0:256]))
            link(v.tensor_scalar(thresholds[:, :], m.iota[:, 0:W], float(Q), float(Q), ALU.mult, ALU.add))
            dve.wait_ge(loaded, 16 * (3 * (NCH + 1) + 1))
            src_i, dst_i, rel_i = nat_i[:, 0, :, :], nat_i[:, 1, :, :], nat_i[:, 2, :, :]
            v.tensor_copy(nat[:, 0, :, :], src_i).then_inc(chain, 1)
            v.tensor_copy(nat[:, 1, :, :], dst_i).then_inc(chain, 1)
            v.scalar_tensor_tensor(row_i[:, 0, :, :], src_i, float(R), rel_i, ALU.mult, ALU.add).then_inc(chain, 1)
            v.scalar_tensor_tensor(quant[:, 1, :, :], dst_i, float(R), rel_i, ALU.mult, ALU.add).then_inc(chain, 1)
            count[0] += 4
            dve.wait_ge(chain, count[0])
            link(v.tensor_tensor(below[:, :, :], nat[:, 1, :, P - 1:P].broadcast_to([CH, NCH, W]),
                                 bc_mid(thresholds[0:CH, :], NCH), ALU.is_lt))
            dve.sem_inc(below_ready, 1)
            link(v.tensor_scalar(quant[:, 1, :, :], quant[:, 1, :, :], float(R * N - 1), None, ALU.min))
            link(v.tensor_copy(quant[:, 0, :, :], nat[:, 0, :, :]))
            link(v.tensor_scalar(row_i[:, 1, :, :], row_i[:, 0, :, :], ROWLO - 1, None, ALU.bitwise_and))
            link(v.tensor_scalar(row_i[:, 2, :, :], row_i[:, 0, :, :], 7, None, ALU.arith_shift_right))
            link(v.tensor_copy(quant[:, 2, :, :], row_i[:, 1, :, :]))
            link(v.tensor_copy(quant[:, 3, :, :], row_i[:, 2, :, :]))
            link(v.tensor_scalar(win[:, :, :], nat[:, 1, :, :], float(Q), None, ALU.is_ge))
            for w in range(2, W):
                link(v.scalar_tensor_tensor(win[:, :, :], nat[:, 1, :, :], float(Q * w), win[:, :, :], ALU.is_ge, ALU.add))
            link(v.scalar_tensor_tensor(quant[:, 4, :, :], win[:, :, :], -float(Q), nat[:, 1, :, :], ALU.mult, ALU.add))
            link(v.memset(edge_flags[:, :, :, :], -BIG))
            v.tensor_tensor(edge_flags[:, 0, :, 1:P], nat[:, 1, :, 1:P], nat[:, 1, :, 0:P - 1], ALU.not_equal).then_inc(chain, 1)
            v.tensor_tensor(edge_flags[:, 1, :, 0:P - 1], nat[:, 1, :, 1:P], nat[:, 1, :, 0:P - 1], ALU.not_equal).then_inc(chain, 1)
            count[0] += 2
            dve.wait_ge(chain, count[0])
            v.tensor_scalar(edge_flags[:, 0, :, 1:P], edge_flags[:, 0, :, 1:P], -BIG, None, ALU.mult).then_inc(chain, 1)
            v.tensor_scalar(edge_flags[:, 1, :, 0:P - 1], edge_flags[:, 1, :, 0:P - 1], -BIG, None, ALU.mult).then_inc(chain, 1)
            count[0] += 2
            dve.wait_ge(chain, count[0])
            dve.sem_inc(quant_ready, 1)
            dve.wait_ge(ends_done, 1)
            link(v.tensor_tensor(ends[:, :], ps[7][:, 0:W], m.iota[:, 0:W], ALU.add))
            link(v.tensor_scalar(m.pair_win[:, :], m.iota[:, 0:PAIRS], ends[:, 0:1], None, ALU.is_gt))
            for w in range(1, W - 1):
                link(v.scalar_tensor_tensor(m.pair_win[:, :], m.iota[:, 0:PAIRS], ends[:, w:w + 1], m.pair_win[:, :],
                                            ALU.is_gt, ALU.add))
            link(v.tensor_copy(m.pair_win_i[:, :], m.pair_win[0:1, :]))
            link(v.tensor_tensor(pair_tile[:, :], m.iota[:, 0:PAIRS], m.pair_win[:, :], ALU.subtract))
            for c in range(NCH):
                link(v.tensor_scalar(pick[:, c, :], pair_tile[0:CH, :], tile_no[0:CH, c:c + 1], None, ALU.is_equal))
            dve.sem_inc(pick_ready, 1)
            dve.wait_ge(lanes_done, 1)
            v.tensor_copy(m.src_lane[:, 0:TILES], ps[0][:, 0:TILES]).then_inc(lanes_read, 1)
            v.tensor_copy(m.y_row[:, 0:TILES], ps[1][:, 0:TILES]).then_inc(lanes_read, 1)
            v.tensor_copy(m.row_lo[:, :], ps[2][:, 0:TILES]).then_inc(lanes_read, 1)
            v.tensor_copy(m.row_hi[:, :], ps[3][:, 0:TILES]).then_inc(lanes_read, 1)
            v.tensor_copy(m.dst_loc[:, :], ps[4][:, 0:TILES]).then_inc(lanes_read, 1)
            v.tensor_copy(m.dst_win[:, :], ps[5][:, 0:TILES]).then_inc(lanes_read, 1)
            dve.wait_ge(slots_done, 1)
            link(v.tensor_scalar(m.pair_src[:, 0:PAIRS], ps[0][:, 0:PAIRS], float(N - 1), None, ALU.min))
            link(v.scalar_tensor_tensor(m.pair_dst[:, 0:PAIRS], m.pair_win[:, :], -float(Q), ps[1][:, 0:PAIRS], ALU.mult, ALU.add))
            for h in range(H):
                link(v.tensor_copy(start_pen[:, h, :], ps[2][:, 0:PAIRS]))
                link(v.tensor_copy(end_pen[:, h, :], ps[3][:, 0:PAIRS]))
            dve.sem_inc(pens_ready, 1)
            link(v.tensor_copy(last0[:, 0, :], ps[4][:, 0:PAIRS]))
            link(v.tensor_copy(last0[:, 1, :], ps[5][:, 0:PAIRS]))
            link(v.tensor_tensor(same[:, 0, :], ps[1][:, 0:PAIRS], last0[:, 1, :], ALU.not_equal))
            link(v.tensor_tensor(same[:, 1, :], ps[1][:, 0:PAIRS], last0[:, 0, :], ALU.not_equal))
            dve.sem_inc(slots_read, 1)
            link(v.tensor_scalar(m.first_pen[:, :], same[:, 0, :], -BIG, None, ALU.mult))
            link(v.tensor_scalar(m.last_pen[:, :], same[:, 1, :], -BIG, None, ALU.mult))
            link(v.memset(same[:, 2:3, :], 0.0))
            link(v.tensor_tensor(same[:, 2, 1:PAIRS], last0[:, 1, 1:PAIRS], last0[:, 0, 0:PAIRS - 1], ALU.is_equal))
            link(v.tensor_tensor(same[:, 3, 1:PAIRS], m.pair_win[:, 1:PAIRS], m.pair_win[:, 0:PAIRS - 1], ALU.is_equal))
            link(v.tensor_tensor(same[:, 2, 1:PAIRS], same[:, 2, 1:PAIRS], same[:, 3, 1:PAIRS], ALU.mult))
            link(v.tensor_tensor(same[:, 3, :], last0[:, 0, :], last0[:, 1, :], ALU.is_equal))
            link(v.tensor_scalar(m.cont_pen[:, :], same[:, 2, :], 1.0, BIG, ALU.subtract, ALU.mult))
            link(v.tensor_tensor(same[:, 0, :], same[:, 2, :], same[:, 3, :], ALU.mult))
            link(v.memset(same[:, 1, :], 0.0))
            link(v.tensor_tensor(same[:, 1, 0:PAIRS - 1], same[:, 2, 1:PAIRS], same[:, 3, 0:PAIRS - 1], ALU.mult))
            for h in range(H):
                link(v.tensor_scalar(m.fwd_pen[:, h, :], same[:, 0, :], 1.0, BIG, ALU.subtract, ALU.mult))
                link(v.tensor_scalar(m.bwd_pen[:, h, :], same[:, 1, :], 1.0, BIG, ALU.subtract, ALU.mult))
            link(v.tensor_scalar(m.leader[:, :], start_pen[:, 0, :], -1.0, None, ALU.is_lt))
            link(v.tensor_scalar(same[:, 1, :], same[:, 2, :], m.only0[:, 0:1], None, ALU.mult))
            link(v.tensor_tensor(m.leader[:, :], m.leader[:, :], same[:, 1, :], ALU.subtract))
            dve.wait_ge(pens_turned, 1)
            for k in range(4):
                cols = min(512, H * PAIRS - 512 * k)
                link(v.tensor_copy(m.start_turned[:, 512 * k:512 * k + cols], ps[k][:, 0:cols]))
                link(v.tensor_copy(m.end_turned[:, 512 * k:512 * k + cols], ps[4 + k][:, 0:cols]))

        @block.tensor
        def _(pe):
            t = nc.tensor
            pe.wait_ge(consts, 14)
            pe.wait_ge(below_ready, 1)
            for c in range(NCH):
                last = t.matmul(ps[7][:, 0:W], ones[0:CH, :], below[:, c, :], start=(c == 0), stop=(c == NCH - 1))
            last.then_inc(ends_done, 1)
            pe.wait_ge(quant_ready, 1)
            for k in range(6):
                for c in range(NCH):
                    a = quant[:, k, c, :] if k < 5 else win[:, c, :]
                    last = t.transpose(ps[k][:, c * CH:(c + 1) * CH], a, m.ident[0:CH, 0:CH])
            last.then_inc(lanes_done, 1)
            pe.wait_ge(pick_ready, 1)
            pe.wait_ge(lanes_read, 6)
            for k in range(6):
                for c in range(NCH):
                    if k < 2:
                        a = nat[:, k, c, :]
                    elif k < 4:
                        a = edge_flags[:, k - 2, c, :]
                    else:
                        lane = P - 1 if k == 4 else 0
                        a = nat[:, 1, c, lane:lane + 1].broadcast_to([CH, P])
                    last = t.matmul(ps[k][:, 0:PAIRS], a, pick[:, c, :], start=(c == 0), stop=(c == NCH - 1))
            last.then_inc(slots_done, 1)
            pe.wait_ge(pens_ready, 1)
            pe.wait_ge(slots_read, 1)
            for base, pen in ((0, start_pen), (4, end_pen)):
                flat = pen[:, :, :].rearrange("l h p -> l (h p)")
                for n in range(BLOCKS):
                    last = t.transpose(ps[base + n // 4][:, (n % 4) * P:(n % 4 + 1) * P], flat[:, n * P:(n + 1) * P],
                                       m.ident[:, :])
            last.then_inc(pens_turned, 1)


def segment_softmax(nc, m):
    with ExitStack() as ctx:
        sb, sem, bank = scope(nc, ctx)

        cols = H * PAIRS
        carried = sb("carried", [P, 2, H, PAIRS])
        fwd, both = (carried[:, k, :, :].rearrange("l h p -> l (h p)") for k in range(2))
        top = sb("top", [P, H, PAIRS])
        ends2 = sb("ends2", [P, 2, cols])
        ps = [bank(f"sg{i}") for i in range(8)]
        turned, scanned, back, top_ready = sem("turned"), sem("scanned"), sem("back"), sem("top_ready")
        ends_ready, chain, shifted, exped = sem("ends_ready"), sem("seg_chain"), sem("shifted"), sem("exped")
        block = ctx.enter_context(nc.Block())
        alpha = m.alpha[:, :, :].rearrange("l h p -> l (h p)")
        topf = top[:, :, :].rearrange("l h p -> l (h p)")

        def width(k):
            return min(512, cols - 512 * k)

        @block.tensor
        def _(pe):
            t = nc.tensor
            for n in range(BLOCKS):
                last = t.transpose(ps[n // 4][:, (n % 4) * P:(n % 4 + 1) * P], alpha[:, n * P:(n + 1) * P], m.ident[:, :])
            last.then_inc(turned, 1)
            pe.wait_ge(scanned, 1)
            for n in range(BLOCKS):
                last = t.transpose(ps[4 + n // 4][:, (n % 4) * P:(n % 4 + 1) * P], both[:, n * P:(n + 1) * P], m.ident[:, :])
            last.then_inc(back, 1)
            pe.wait_ge(top_ready, 1)
            for k in range(4):
                last = t.matmul(ps[k][:, 0:width(k)], m.only0[:, :], topf[:, 512 * k:512 * k + width(k)], start=True, stop=True)
                last = t.matmul(ps[4 + k][:, 0:width(k)], m.only127[:, :], topf[:, 512 * k:512 * k + width(k)],
                                start=True, stop=True)
            last.then_inc(ends_ready, 1)

        @block.scalar
        def _(act):
            act.wait_ge(shifted, 1)
            nc.scalar.activation(m.small[:, 0:PAIRS, 0:H], top[:, :, :].rearrange("l h p -> l p h"), ACT.Exp).then_inc(exped, 1)

        @block.vector
        def _(dve):
            v, count = nc.vector, [0]

            def link(op):
                count[0] += 1
                op.then_inc(chain, 1)
                dve.wait_ge(chain, count[0])

            dve.wait_ge(turned, 1)
            for k in range(4):
                a, b = 512 * k, 512 * k + width(k)
                link(v.tensor_tensor_scan(fwd[:, a:b], m.start_turned[:, a:b], ps[k][:, 0:width(k)], -BIG, ALU.add, ALU.max))
            link(v.tensor_tensor_scan(both[:, ::-1], m.end_turned[:, ::-1], fwd[:, ::-1], -BIG, ALU.add, ALU.max))
            dve.sem_inc(scanned, 1)
            dve.wait_ge(back, 1)
            for k in range(4):
                link(v.tensor_copy(topf[:, 512 * k:512 * k + width(k)], ps[4 + k][:, 0:width(k)]))
            dve.sem_inc(top_ready, 1)
            dve.wait_ge(ends_ready, 1)
            for k in range(4):
                link(v.tensor_copy(ends2[:, 0, 512 * k:512 * k + width(k)], ps[k][:, 0:width(k)]))
                link(v.tensor_copy(ends2[:, 1, 512 * k:512 * k + width(k)], ps[4 + k][:, 0:width(k)]))
            fpen = m.fwd_pen[:, :, :].rearrange("l h p -> l (h p)")
            bpen = m.bwd_pen[:, :, :].rearrange("l h p -> l (h p)")
            link(v.tensor_tensor_scan(fwd, fpen, ends2[:, 1, :], -BIG, ALU.add, ALU.max))
            link(v.tensor_tensor_scan(both[:, ::-1], bpen[:, ::-1], ends2[:, 0, ::-1], -BIG, ALU.add, ALU.max))
            inc = ends2[:, 0, :].rearrange("l (h p) -> l h p", h=H)
            inb = ends2[:, 1, :].rearrange("l (h p) -> l h p", h=H)
            link(v.memset(ends2[:, :, :], -BIG))
            link(v.tensor_tensor(inc[:, :, 1:PAIRS], carried[:, 0, :, 0:PAIRS - 1], bc_mid(m.cont_pen[:, 1:PAIRS], H), ALU.add))
            link(v.tensor_tensor(inb[:, :, 0:PAIRS - 1], carried[:, 1, :, 1:PAIRS], bc_mid(m.cont_pen[:, 1:PAIRS], H), ALU.add))
            link(v.tensor_tensor(inc, inc, bc_mid(m.first_pen[:, :], H), ALU.add))
            link(v.tensor_tensor(inb, inb, bc_mid(m.last_pen[:, :], H), ALU.add))
            link(v.tensor_tensor(inc, inc, inb, ALU.max))
            link(v.tensor_tensor(top[:, :, :], top[:, :, :], inc, ALU.max))
            link(v.tensor_tensor(m.small[:, 0:PAIRS, H:2 * H], top[:, :, :].rearrange("l h p -> l p h"), bc_last(m.leader[:, :], H), ALU.mult))
            link(v.tensor_tensor(top[:, :, :], m.alpha[:, :, :], top[:, :, :], ALU.subtract))
            link(v.tensor_scalar(top[:, :, :], top[:, :, :], 0.0, None, ALU.min))
            dve.sem_inc(shifted, 1)
            dve.wait_ge(exped, 1)

def common(m, sb):
    m.x = sb("x_nodes", [Q, W, D])
    m.ident, m.ident_b = sb("ident", [P, P]), sb("ident_b", [P, P], BF16)
    m.rows_before = sb("rows_before", [P, P])
    m.only0, m.only127 = sb("only0", [P, P]), sb("only127", [P, P])
    m.iota, m.iota_b = sb("iota", [P, 512]), sb("iota_b", [P, 256], BF16)
    m.lane = sb("lane", [P, 1])
    m.pair_src = sb("pair_src", [P, SLOTPAD], U32)
    m.pair_dst = sb("pair_dst", [P, PAIRS + G])
    m.pair_win = sb("pair_win", [P, PAIRS])
    m.pair_win_i = sb("pair_win_i", [1, PAIRS], I32)
    m.y_row = sb("y_row", [P, TILES + 8], U32)
    m.src_lane = sb("src_lane", [P, TILES + 8])
    m.row_lo, m.row_hi = sb("row_lo", [P, TILES], BF16), sb("row_hi", [P, TILES], BF16)
    m.dst_loc, m.dst_win = sb("dst_loc", [P, TILES], BF16), sb("dst_win", [P, TILES], BF16)
    m.start_turned, m.end_turned = sb("start_turned", [P, H * PAIRS]), sb("end_turned", [P, H * PAIRS])
    m.first_pen, m.last_pen, m.cont_pen = (sb(n, [P, PAIRS]) for n in ("first_pen", "last_pen", "cont_pen"))
    m.fwd_pen, m.bwd_pen = sb("fwd_pen", [P, H, PAIRS]), sb("bwd_pen", [P, H, PAIRS])
    m.leader = sb("leader", [P, PAIRS])
    m.alpha = sb("alpha", [P, H, PAIRS])
    m.small = sb("small", [P, PAIRS + G, 2 * H])
    m.row_inv = sb("row_inv", [P, 3, ROWHI], BF16)
    m.deg_inv, m.deg_rsqrt = sb("deg_inv", [Q, W]), sb("deg_rsqrt", [Q, W])



def layer_norm(nc, dve, link, x, y, tmp, stats, eps, var_ready, std_ready, turn):
    v = nc.vector
    mean, var = stats[:, 0, :], stats[:, 1, :]
    link(v.reduce_sum(mean, x, AX))
    link(v.tensor_scalar(mean, mean, 1.0 / D, None, ALU.mult))
    link(v.tensor_tensor(y, x, bc_last(mean, D), ALU.subtract))
    link(v.tensor_tensor(tmp, y, y, ALU.mult))
    link(v.reduce_sum(var, tmp, AX))
    v.tensor_scalar(var, var, 1.0 / D, eps, ALU.mult, ALU.add).then_inc(var_ready, 1)
    dve.wait_ge(std_ready, turn)
    link(v.reciprocal(mean, var))
    link(v.tensor_tensor(y, y, bc_last(mean, D), ALU.mult))


def std_of(nc, act, stats, var_ready, std_ready, turn):
    act.wait_ge(var_ready, turn)
    nc.scalar.activation(stats[:, 1, :], stats[:, 1, :], ACT.Sqrt).then_inc(std_ready, 1)


TG = (W + 3) // 4


def turn_windows_pe(nc, pe, m, src, banks, turned, copied, done=0):
    for g in range(TG):
        n = done + g
        if n >= 2:
            pe.wait_ge(copied, n - 1)
        for w in range(4 * g, min(4 * g + 4, W)):
            last = nc.tensor.transpose(banks[n % 2][:, (w % 4) * Q:(w % 4 + 1) * Q], src[:, w, :], m.ident[0:Q, 0:Q])
        last.then_inc(turned, 1)


def turn_windows_act(nc, act, m, dst, banks, turned, copied, done=0):
    for g in range(TG):
        n = done + g
        act.wait_ge(turned, n + 1)
        k = min(4, W - 4 * g)
        nc.scalar.copy(dst[:, 4 * g:4 * g + k, :].rearrange("d w q -> d (w q)"), banks[n % 2][:, 0:k * Q]).then_inc(copied, 1)


def relation_rows(nc, m, ins, y_table):
    with ExitStack() as ctx:
        sb, sem, bank = scope(nc, ctx)
        w0, w0t = sb("w0", [P, R, D]), sb("w0t", [P, R * D])
        xt = sb("xt0", [P, W, Q])
        stage = sb("y_stage", [Q, 2, R * D])
        tb = [bank(f"tb{i}") for i in range(2)]
        wb = [bank(f"wb{i}") for i in range(2)]
        yb = [bank(f"yb{i}") for i in range(4)]
        loaded, turned, copied, wt, wc = (sem(n) for n in ("w0_loaded", "x_turned", "xt_copied", "w_turned", "wt_copied"))
        y_done, y_left, y_right = sem("y_done"), sem("y_left"), sem("y_right")
        stored = [sem("y_stored0"), sem("y_stored1")]
        block = ctx.enter_context(nc.Block())

        @block.sync
        def _(sp):
            sp.dma_start(w0[:, :, :], ins["L0_gnn_weights"].rearrange("r i j -> i r j")).then_inc(loaded, 16)
            for w in range(W):
                sp.wait_ge(y_left, w + 1)
                sp.wait_ge(y_right, w + 1)
                sp.dma_start(y_table.rearrange("(n r) d -> n (r d)", r=R)[w * Q:(w + 1) * Q, :],
                             stage[:, w % 2, :]).then_inc(stored[w % 2], 16)
            sp.wait_ge(stored[0], 16 * ((W + 1) // 2))
            sp.wait_ge(stored[1], 16 * (W // 2))

        @block.tensor
        def _(pe):
            pe.wait_ge(loaded, 16)
            for r in range(R):
                last = nc.tensor.transpose(wb[r // 4][:, (r % 4) * D:(r % 4 + 1) * D], w0[:, r, :], m.ident[:, :])
            last.then_inc(wt, 1)
            turn_windows_pe(nc, pe, m, m.x, tb, turned, copied)
            pe.wait_ge(wc, 2)
            pe.wait_ge(copied, TG)
            for w in range(W):
                if w >= 2:
                    pe.wait_ge(y_left, w - 1)
                    pe.wait_ge(y_right, w - 1)
                for k in range(2):
                    last = nc.tensor.matmul(yb[2 * (w % 2) + k][0:Q, :], xt[:, w, :], w0t[:, k * 512:(k + 1) * 512],
                                            start=True, stop=True)
                last.then_inc(y_done, 1)

        @block.scalar
        def _(act):
            turn_windows_act(nc, act, m, xt, tb, turned, copied)
            for w in range(W):
                act.wait_ge(y_done, w + 1)
                if w >= 2:
                    act.wait_ge(stored[w % 2], 16 * (w // 2))
                nc.scalar.copy(stage[:, w % 2, 0:512], yb[2 * (w % 2)][0:Q, :]).then_inc(y_left, 1)

        @block.vector
        def _(dve):
            dve.wait_ge(wt, 1)
            nc.vector.tensor_copy(w0t[:, 0:512], wb[0][:, :]).then_inc(wc, 1)
            nc.vector.tensor_copy(w0t[:, 512:1024], wb[1][:, :]).then_inc(wc, 1)
            for w in range(W):
                dve.wait_ge(y_done, w + 1)
                if w >= 2:
                    dve.wait_ge(stored[w % 2], 16 * (w // 2))
                nc.vector.tensor_copy(stage[:, w % 2, 512:1024], yb[2 * (w % 2) + 1][0:Q, :]).then_inc(y_right, 1)


def count_edges(nc, m):
    with ExitStack() as ctx:
        sb, sem, bank = scope(nc, ctx)
        zeros = sb("zeros_b", [P, 512], BF16)
        lo, hi = sb("lo_hot", [P, 2, G, ROWLO], BF16), sb("hi_hot", [P, 2, G, ROWHI], BF16)
        dl, dw = sb("dl_hot", [P, 2, G, Q], BF16), sb("dw_hot", [P, 2, G, W], BF16)
        part = sb("part", [P, ROWHI])
        deg_std = sb("deg_std", [Q, W])
        rows, degs = bank("rows_count"), bank("dst_count")
        start, hots, counted, done = sem("start"), sem("hots"), sem("counted"), sem("all_counted")
        chain, deg_ready, std_ready = sem("count_chain"), sem("deg_ready"), sem("deg_std_ready")
        block = ctx.enter_context(nc.Block())

        @block.tensor
        def _(pe):
            mm = nc.tensor.matmul
            pe.wait_ge(start, 1)
            mm(rows[:, 0:ROWHI], zeros[:, 0:P], zeros[:, 0:ROWHI], start=True, stop=False)
            mm(degs[0:Q, 0:W], zeros[:, 0:Q], zeros[:, 0:W], start=True, stop=False)
            with pe.Fori(0, TILES // (2 * G)) as i:
                for b in range(2):
                    pe.wait_ge(hots, 2 * i + (b + 1))
                    for j in range(G):
                        mm(rows[:, 0:ROWHI], lo[:, b, j, :], hi[:, b, j, :], start=False, stop=False)
                        last = mm(degs[0:Q, 0:W], dl[:, b, j, :], dw[:, b, j, :], start=False, stop=False)
                    last.then_inc(counted, 1)
            mm(rows[:, 0:ROWHI], zeros[:, 0:P], zeros[:, 0:ROWHI], start=False, stop=True)
            mm(degs[0:Q, 0:W], zeros[:, 0:Q], zeros[:, 0:W], start=False, stop=True).then_inc(done, 1)

        @block.scalar
        def _(act):
            act.wait_ge(deg_ready, 1)
            nc.scalar.activation(deg_std[:, :], m.deg_inv[:, :], ACT.Sqrt).then_inc(std_ready, 1)

        @block.vector
        def _(dve):
            v, count = nc.vector, [0]

            def link(op):
                count[0] += 1
                op.then_inc(chain, 1)
                dve.wait_ge(chain, count[0])

            link(v.memset(zeros[:, :], 0.0))
            dve.sem_inc(start, 1)
            dve.sem_inc(counted, 2)
            with dve.Fori(0, TILES // (2 * G)) as i:
                for b in range(2):
                    dve.wait_ge(counted, 2 * i + (b + 1))
                    for hot, col, n in ((lo, m.row_lo, ROWLO), (hi, m.row_hi, ROWHI), (dl, m.dst_loc, Q), (dw, m.dst_win, W)):
                        last = v.tensor_tensor(hot[:, b, :, :], bc_last(col[:, bass.ds(i * (2 * G) + b * G, G)], n),
                                               bc_mid(m.iota_b[:, 0:n], G), ALU.is_equal)
                    last.then_inc(hots, 1)
            dve.wait_ge(done, 1)
            link(v.tensor_scalar(part[:, :], rows[:, 0:ROWHI], 1.0, None, ALU.max))
            link(v.reciprocal(part[:, :], part[:, :]))
            for k in range(3):
                link(v.tensor_copy(m.row_inv[:, k, :], part[:, :]))
                if k < 2:
                    link(v.tensor_tensor(part[:, :], part[:, :], m.row_inv[:, k, :], ALU.subtract))
            link(v.tensor_scalar(m.deg_inv[:, :], degs[0:Q, 0:W], 1.0, None, ALU.add))
            dve.sem_inc(deg_ready, 1)
            dve.wait_ge(std_ready, 1)
            link(v.reciprocal(m.deg_inv[:, :], m.deg_inv[:, :]))
            link(v.reciprocal(m.deg_rsqrt[:, :], deg_std[:, :]))


def relation_edges(nc, m, y_table, tables):
    with ExitStack() as ctx:
        sb, sem, bank = scope(nc, ctx)
        y_idx, s_idx = sb("y_idx", [P, 2, G], U32), sb("s_idx", [P, 2, G], U32)
        src = sb("src_slot", [P, 2, G])
        got = sb("y_got", [P, 2, G, D])
        same = sb("same_src", [P, 2, G, P])
        before = sb("before", [P, G, P])
        lo, hi = sb("lo1", [P, 2, G, ROWLO], BF16), sb("hi1", [P, 2, G, ROWHI], BF16)
        lot = sb("lot", [P, 2, G, P], BF16)
        looked = sb("looked", [P, G, ROWHI])
        inv = sb("inv_e", [P, 2, G])
        msg, total = sb("msg0", [P, 2, G, D]), sb("total", [P, 2, G, D])
        zrow = sb("zrow", [P, D])
        dup, shift, dump = sb("dup", [P, G]), sb("shift", [P, G]), sb("dump_row", [P, 1])
        src_t, lo_t, sums = bank("src_t"), bank("lo_t", (P, G, P), BF16), bank("sums")
        inv_b = [bank("inv_b0"), bank("inv_b1")]
        copied, src_ready, turned, same_ready, lot_ready = (sem(n) for n in (
            "idx_copied", "src_ready", "turned0", "same_ready", "lot_ready"))
        inv_found, inv_ready, msg_ready, sums_ready, tot_ready, s_ready = (sem(n) for n in (
            "inv_found", "inv_ready", "msg_ready", "sums_ready", "tot_ready", "s_ready"))
        tick, chain, dump_ready = sem("pool_tick"), sem("chain0"), sem("dump_ready")
        y_in = m.come.pop()
        steps = TILES // (2 * G)
        K = 22
        block = ctx.enter_context(nc.Block())

        @block.gpsimd
        def _(pool):
            pool.memset(zrow[:, :], 0.0).then_inc(tick, 1)
            pool.wait_ge(tick, 1)
            for a, b in ((0, ACCROWS // P // 2), (ACCROWS // P // 2, ACCROWS // P)):
                for j in range(G):
                    if a:
                        pool.wait_ge(m.added[j], 16)
                    pool.dma_start(tables[j].rearrange("(a p) d -> p a d", p=P)[:, a:b, :],
                                   bc_mid(zrow[:, :], b - a)).then_inc(m.added[j], 16)

            def gather(b):
                for j in range(G):
                    pool.indirect_dma_start(out=got[:, b, j, :], out_offset=None, in_=y_table[:, :],
                                            in_offset=bass.IndirectOffsetOnAxis(ap=y_idx[:, b, j:j + 1], axis=0)
                                            ).then_inc(y_in[b], 16)

            for b in range(2):
                pool.wait_ge(copied, b + 1)
                gather(b)
            with pool.Fori(0, steps) as i:
                for b in range(2):
                    g = 2 * i + b
                    pool.wait_ge(s_ready, g + 1).then_inc(tick, 1)
                    pool.wait_ge(tot_ready, g + 3).then_inc(tick, 1)
                    for j in range(G):
                        pool.wait_ge(m.added[j], 16 * g + 32).then_inc(tick, 1)
                        pool.indirect_dma_start(out=tables[j][:, :],
                                                out_offset=bass.IndirectOffsetOnAxis(ap=s_idx[:, b, j:j + 1], axis=0),
                                                in_=total[:, b, j, :], in_offset=None,
                                                compute_op=ALU.add).then_inc(m.added[j], 16)
                    pool.wait_ge(copied, g + 3).then_inc(tick, 1)
                    pool.wait_ge(msg_ready, g + 1).then_inc(tick, 1)
                    gather(b)
            for j in range(G):
                pool.wait_ge(m.added[j], 16 * (2 * steps) + 32)
            for b in range(2):
                pool.wait_ge(y_in[b], 16 * G * (steps + 1))

        @block.vector
        def _(dve):
            v, n = nc.vector, [0]
            dve.sem_inc(same_ready, 1)
            dve.sem_inc(inv_ready, 1)
            v.tensor_scalar(dump[:, :], m.lane[:, :], float(DUMP), None, ALU.add).then_inc(dump_ready, 1)
            v.tensor_copy(y_idx[:, 0, :], m.y_row[:, 0:G]).then_inc(copied, 1)
            v.tensor_copy(y_idx[:, 1, :], m.y_row[:, G:2 * G]).then_inc(copied, 1)
            dve.wait_ge(dump_ready, 1)
            with dve.Fori(0, steps) as i:
                def link(op):
                    n[0] += 1
                    op.then_inc(chain, 1)
                    dve.wait_ge(chain, K * i + n[0])

                for b in range(2):
                    g, at = 2 * i + b, i * (2 * G) + b * G
                    dve.wait_ge(tot_ready, g + 1)
                    link(v.tensor_copy(src[:, b, :], m.src_lane[:, bass.ds(at, G)]))
                    v.tensor_tensor(lo[:, b, :, :], bc_last(m.row_lo[:, bass.ds(at, G)], ROWLO),
                                    bc_mid(m.iota_b[:, 0:ROWLO], G), ALU.is_equal).then_inc(src_ready, 1)
                    link(v.tensor_tensor(hi[:, b, :, :], bc_last(m.row_hi[:, bass.ds(at, G)], ROWHI),
                                         bc_mid(m.iota_b[:, 0:ROWHI], G), ALU.is_equal))
                    dve.wait_ge(turned, g + 1)
                    link(v.tensor_tensor(same[:, b, :, :], src_t[:, :].rearrange("p (j e) -> p j e", j=G),
                                         bc_last(src[:, b, :], P), ALU.is_equal))
                    dve.sem_inc(same_ready, 1)
                    link(v.tensor_tensor(before[:, :, :], same[:, b, :, :], bc_mid(m.rows_before[:, :], G), ALU.mult))
                    link(v.reduce_sum(dup[:, :], before[:, :, :], AX))
                    link(v.tensor_scalar(dup[:, :], dup[:, :], 1.0, None, ALU.min))
                    link(v.tensor_scalar(shift[:, :], src[:, b, :], -1.0, dump[:, 0:1], ALU.mult, ALU.add))
                    link(v.tensor_tensor(shift[:, :], shift[:, :], dup[:, :], ALU.mult))
                    for j in range(G):
                        dve.wait_ge(m.added[j], 16 * g + 16)
                    link(v.tensor_tensor(s_idx[:, b, :], shift[:, :], src[:, b, :], ALU.add))
                    dve.sem_inc(s_ready, 1)
                    dve.wait_ge(inv_found, g + 1)
                    for k in range(2):
                        op = v.tensor_tensor(looked[:, 2 * k:2 * k + 2, :],
                                             inv_b[k][:, 0:2 * ROWHI].rearrange("p (j e) -> p j e", j=2),
                                             hi[:, b, 2 * k:2 * k + 2, :], ALU.mult)
                        if k:
                            link(op)
                    v.reduce_sum(inv[:, b, :], looked[:, :, :], AX).then_inc(inv_ready, 1)
                    dve.wait_ge(y_in[b], 64 * i + 64)
                    link(v.tensor_copy(y_idx[:, b, :], m.y_row[:, bass.ds(at + 2 * G, G)]))
                    dve.sem_inc(copied, 1)
                assert n[0] == K, n[0]

        @block.tensor
        def _(pe):
            t = nc.tensor
            with pe.Fori(0, steps) as i:
                for b in range(2):
                    g = 2 * i + b
                    pe.wait_ge(src_ready, g + 1)
                    pe.wait_ge(same_ready, g + 1)
                    pe.wait_ge(lot_ready, g + 1)
                    for j in range(G):
                        t.transpose(src_t[:, j * P:(j + 1) * P], src[:, b, j:j + 1].broadcast_to([P, P]), m.ident[:, :])
                    for j in range(G):
                        last = t.transpose(lo_t[:, j, :], lo[:, b, j, :], m.ident_b[:, :])
                    last.then_inc(turned, 1)
                    pe.wait_ge(lot_ready, g + 2)
                    pe.wait_ge(inv_ready, g + 1)
                    for j in range(G):
                        out = inv_b[j // 2][:, (j % 2) * ROWHI:(j % 2 + 1) * ROWHI]
                        for k in range(3):
                            last = t.matmul(out, lot[:, b, j, :], m.row_inv[:, k, :], start=(k == 0), stop=(k == 2))
                    last.then_inc(inv_found, 1)
                    pe.wait_ge(msg_ready, g + 1)
                    pe.wait_ge(tot_ready, g + 2)
                    for j in range(G):
                        last = t.matmul(sums[:, j * D:(j + 1) * D], same[:, b, j, :], msg[:, b, j, :], start=True, stop=True)
                    last.then_inc(sums_ready, 1)

        @block.scalar
        def _(act):
            s = nc.scalar
            act.sem_inc(lot_ready, 1)
            act.sem_inc(tot_ready, 2)
            with act.Fori(0, steps) as i:
                for b in range(2):
                    g = 2 * i + b
                    act.wait_ge(turned, g + 1)
                    s.copy(lot[:, b, :, :], lo_t[:, :, :]).then_inc(lot_ready, 1)
                    act.wait_ge(inv_ready, g + 2)
                    act.wait_ge(y_in[b], 64 * i + 64)
                    for j in range(G):
                        last = s.activation(msg[:, b, j, :], got[:, b, j, :], ACT.Copy, scale=inv[:, b, j:j + 1])
                    last.then_inc(msg_ready, 1)
                    act.wait_ge(sums_ready, g + 1)
                    for j in range(G):
                        act.wait_ge(m.added[j], 16 * g + 16)
                    s.copy(total[:, b, :, :].rearrange("p j d -> p (j d)"), sums[:, :]).then_inc(tot_ready, 1)


def make_link(dve, chain):
    count = [0]

    def link(op):
        count[0] += 1
        op.then_inc(chain, 1)
        dve.wait_ge(chain, count[0])
    return link


def gcn_nodes(nc, m, ins, tables, t_table):
    with ExitStack() as ctx:
        sb, sem, bank = scope(nc, ctx)
        part, tmp, stats = sb("part1", [Q, G, W, D]), sb("tmp1", [Q, W, D]), sb("stats1", [Q, 2, W])
        w1 = sb("gcn_w", [D, D])
        xt = sb("xt1", [P, W, Q])
        tb, hb = [bank(f"t1{i}") for i in range(2)], [bank(f"h1{i}") for i in range(2)]
        loaded, chain, var_ready, std_ready, x_ready = (sem(n) for n in ("loaded1", "chain1", "var1", "std1", "x1_ready"))
        turned, copied, h_done, h_read, t_ready, stored = (sem(n) for n in ("t1", "c1", "h_done", "h_read", "t_ready", "st1"))
        block = ctx.enter_context(nc.Block())

        @block.sync
        def _(sp):
            for j in range(G):
                sp.dma_start(part[:, j, :, :], nodes(tables[j][0:N, :])).then_inc(loaded, 16)
            sp.dma_start(w1[:, :], ins["L1_gnn_W"]).then_inc(loaded, 16)
            sp.wait_ge(t_ready, 1)
            sp.dma_start(nodes(t_table), tmp[:, :, :]).then_inc(stored, 16)
            sp.wait_ge(stored, 16)

        @block.vector
        def _(dve):
            v, link = nc.vector, make_link(dve, chain)
            dve.wait_ge(loaded, 16 * (G + 1))
            link(v.tensor_tensor(part[:, 0, :, :], part[:, 0, :, :], part[:, 1, :, :], ALU.add))
            link(v.tensor_tensor(part[:, 2, :, :], part[:, 2, :, :], part[:, 3, :, :], ALU.add))
            link(v.tensor_tensor(part[:, 0, :, :], part[:, 0, :, :], part[:, 2, :, :], ALU.add))
            link(v.scalar_tensor_tensor(tmp[:, :, :], part[:, 0, :, :], 0.0, m.x[:, :, :], ALU.max, ALU.add))
            layer_norm(nc, dve, link, tmp[:, :, :], m.x[:, :, :], part[:, 0, :, :], stats, EPS, var_ready, std_ready, 1)
            dve.sem_inc(x_ready, 1)
            for w in range(W):
                dve.wait_ge(h_done, w + 1)
                v.tensor_copy(m.h[:, w, :], hb[w % 2][0:Q, 0:D]).then_inc(h_read, 1)
            dve.wait_ge(h_read, W)
            link(v.tensor_tensor(tmp[:, :, :], m.h[:, :, :], bc_last(m.deg_rsqrt[:, :], D), ALU.mult))
            dve.sem_inc(t_ready, 1)

        @block.scalar
        def _(act):
            std_of(nc, act, stats, var_ready, std_ready, 1)
            turn_windows_act(nc, act, m, xt, tb, turned, copied)

        @block.tensor
        def _(pe):
            pe.wait_ge(x_ready, 1)
            turn_windows_pe(nc, pe, m, m.x, tb, turned, copied)
            pe.wait_ge(copied, TG)
            pe.wait_ge(loaded, 16 * (G + 1))
            for w in range(W):
                if w >= 2:
                    pe.wait_ge(h_read, w - 1)
                nc.tensor.matmul(hb[w % 2][0:Q, 0:D], xt[:, w, :], w1[:, :], start=True, stop=True).then_inc(h_done, 1)


STEPS = PAIRS // (2 * G)


class PairLoop:

    def __init__(self, nc, m, ctx, table):
        sb, sem, bank = scope(nc, ctx)
        self.nc, self.m, self.table = nc, m, table
        self.idx = sb("idx", [P, 2, G], U32)
        self.got = sb("got", [P, 2, G, D])
        self.hot = sb("hot", [P, 2, G, Q])
        self.copied, self.hot_ready, self.tick = sem("idx_copied"), sem("hot_ready"), sem("pool_tick")
        self.used = sem("rows_used")
        self.come = m.come.pop()

    def gathers(self, pool):
        def gather(b):
            for j in range(G):
                pool.indirect_dma_start(out=self.got[:, b, j, :], out_offset=None, in_=self.table[:, :],
                                        in_offset=bass.IndirectOffsetOnAxis(ap=self.idx[:, b, j:j + 1], axis=0)
                                        ).then_inc(self.come[b], 16)

        for b in range(2):
            pool.wait_ge(self.copied, b + 1)
            gather(b)
        with pool.Fori(0, STEPS) as i:
            for b in range(2):
                g = 2 * i + b
                pool.wait_ge(self.copied, g + 3).then_inc(self.tick, 1)
                pool.wait_ge(self.used, g + 3).then_inc(self.tick, 1)
                gather(b)
        for b in range(2):
            pool.wait_ge(self.come[b], 16 * G * (STEPS + 1))

    def first_rows(self, dve):
        for b in range(2):
            self.nc.vector.tensor_copy(self.idx[:, b, :], self.m.pair_src[:, b * G:(b + 1) * G]).then_inc(self.copied, 1)

    def one_hots(self, dve, at, b, g, seen):
        v, m = self.nc.vector, self.m
        cols = slice(at, at + G) if isinstance(at, int) else bass.ds(at, G)
        ahead = slice(at + 2 * G, at + 3 * G) if isinstance(at, int) else bass.ds(at + 2 * G, G)
        dve.wait_ge(self.used, g + 1)
        v.tensor_tensor(self.hot[:, b, :, :], bc_last(m.pair_dst[:, cols], Q), bc_mid(m.iota[:, 0:Q], G),
                        ALU.is_equal).then_inc(self.hot_ready, 1)
        dve.wait_ge(self.come[b], 64 * seen)
        v.tensor_copy(self.idx[:, b, :], m.pair_src[:, ahead]).then_inc(self.copied, 1)


def pair_sums(nc, m, table, acc, heads):
    with ExitStack() as ctx:
        sb, sem, bank = scope(nc, ctx)
        loop = PairLoop(nc, m, ctx, table)
        got, hot = loop.got, loop.hot
        tail = {0: 0, 1: H, H: 2 * H}[heads]
        wide = H * D if heads == H else D
        if heads:
            wts = sb("wts", [P, 2, G, 2 * H])
            msg = sb("msg", [P, 2, G, wide])
            tails = [bank(f"tails{b}", (P, G, 2 * H)) for b in range(2)]
        sums = [bank(f"sums{j}") for j in range(G if heads == H else 2)]
        wts_ready, msg_ready, act_ready, read, chain = (sem(n) for n in ("wts_ready", "msg_ready", "act_msg", "sums_read", "chain"))
        per = 2 * G * (2 if heads else 1)
        block = ctx.enter_context(nc.Block())

        @block.gpsimd
        def _(pool):
            loop.gathers(pool)

        @block.vector
        def _(dve):
            v, done = nc.vector, [0]
            dve.sem_inc(read, 1 if heads == H else 2)
            loop.first_rows(dve)

            def produce(at, b, g, seen):
                loop.one_hots(dve, at, b, g, seen)
                if not heads:
                    return
                cols = slice(at, at + G) if isinstance(at, int) else bass.ds(at, G)
                v.tensor_copy(wts[:, b, :, :], m.small[:, cols, :]).then_inc(wts_ready, 1)
                dve.wait_ge(wts_ready, g + 1)
                if heads == 1:
                    v.tensor_tensor(msg[:, b, :, :].rearrange("p j (h c) -> p j h c", h=H),
                                    got[:, b, :, :].rearrange("p j (h c) -> p j h c", h=H),
                                    wts[:, b, :, 0:H].unsqueeze(3).broadcast_to([P, G, H, C]), ALU.mult).then_inc(msg_ready, 1)
                else:
                    for j in range(G):
                        last = v.tensor_tensor(msg[:, b, j, 0:2 * D].rearrange("p (h d) -> p h d", h=2),
                                               bc_mid(got[:, b, j, :], 2), bc_last(wts[:, b, j, 0:2], D), ALU.mult)
                    last.then_inc(msg_ready, 1)

            produce(0, 0, 0, 1)
            with dve.Fori(0, STEPS) as i:
                def add(dst, src):
                    done[0] += 1
                    v.tensor_tensor(dst, dst, src, ALU.add).then_inc(chain, 1)

                for b in range(2):
                    g, at = 2 * i + b, i * (2 * G) + b * G
                    produce(at + G, 1 - b, g + 1, i + 1 + b)
                    dve.wait_ge(loop.used, g + 3)
                    for j in range(G):
                        w = dve.value_load(m.pair_win_i[0:1, bass.ds(at + j, 1)], min_val=0, max_val=W - 1)
                        row = acc[:, bass.ds(w, 1), :].rearrange("q o d -> q (o d)")
                        if j:
                            dve.wait_ge(chain, per * i + done[0])
                        add(row[:, 0:wide], sums[j][0:Q, :] if heads == H else sums[b][0:Q, j * D:(j + 1) * D])
                        if heads:
                            add(row[:, wide:wide + tail], tails[b][0:Q, j, 0:tail])
                    dve.wait_ge(chain, per * i + done[0])
                    dve.sem_inc(read, 1)
                assert done[0] == per

        @block.scalar
        def _(act):
            if heads != H:
                return

            def weigh(b, g, seen):
                act.wait_ge(wts_ready, g + 1)
                act.wait_ge(loop.come[b], 64 * seen)
                for j in range(G):
                    for h in range(2, H):
                        last = nc.scalar.activation(msg[:, b, j, h * D:(h + 1) * D], got[:, b, j, :], ACT.Copy,
                                                    scale=wts[:, b, j, h:h + 1])
                last.then_inc(act_ready, 1)

            with act.Fori(0, STEPS) as i:
                for b in range(2):
                    weigh(b, 2 * i + b, i + 1)

        @block.tensor
        def _(pe):
            t = nc.tensor
            pe.sem_inc(loop.used, 2)
            with pe.Fori(0, STEPS) as i:
                for b in range(2):
                    g = 2 * i + b
                    pe.wait_ge(loop.hot_ready, g + 1)
                    pe.wait_ge(loop.come[b], 64 * i + 64)
                    if heads:
                        pe.wait_ge(msg_ready, g + 1)
                    if heads == H:
                        pe.wait_ge(act_ready, g + 1)
                    pe.wait_ge(read, g + 1)
                    for j in range(G):
                        rows = msg[:, b, j, :] if heads else got[:, b, j, :]
                        out = sums[j][0:Q, :] if heads == H else sums[b][0:Q, j * D:(j + 1) * D]
                        last = t.matmul(out, hot[:, b, j, :], rows, start=True, stop=True)
                        if heads:
                            last = t.matmul(tails[b][0:Q, j, 0:tail], hot[:, b, j, :], wts[:, b, j, 0:tail],
                                            start=True, stop=True)
                    last.then_inc(loop.used, 1)


def batch_norm(nc, m, ins, x_table):
    with ExitStack() as ctx:
        sb, sem, bank = scope(nc, ctx)
        o, sq, stats = sb("gcn_out", [Q, W, D]), sb("gcn_sq", [Q, W, D]), sb("stats2", [Q, 2, W])
        vec = sb("gcn_vec", [P, 3, D])
        mean, rstd = sb("bn_mean", [Q, D]), sb("bn_rstd", [Q, D])
        ones = sb("ones_q", [Q, Q])
        sums = [bank("bn_sum"), bank("bn_sq")]
        loaded, chain, ready, summed, var_ready, std_ready, out_ready, stored = (sem(n) for n in (
            "loaded2", "chain2", "bn_ready", "bn_summed", "var2", "std2", "x2_ready", "stored2"))
        block = ctx.enter_context(nc.Block())

        @block.sync
        def _(sp):
            for k, name in enumerate(("L1_gnn_b", "L1_gnn_gamma", "L1_gnn_beta")):
                sp.dma_start(vec[:, k, :], row_bc(ins[name], P)).then_inc(loaded, 16)
            sp.wait_ge(out_ready, 1)
            sp.dma_start(nodes(x_table), m.x[:, :, :]).then_inc(stored, 16)
            sp.wait_ge(stored, 16)

        @block.tensor
        def _(pe):
            for k, a in enumerate((o, sq)):
                pe.wait_ge(ready, k + 1)
                for w in range(W):
                    last = nc.tensor.matmul(sums[k][0:Q, 0:D], ones[:, :], a[:, w, :], start=(w == 0), stop=(w == W - 1))
                last.then_inc(summed, 1)

        @block.scalar
        def _(act):
            act.wait_ge(var_ready, 1)
            nc.scalar.activation(rstd[:, :], rstd[:, :], ACT.Sqrt).then_inc(std_ready, 1)
            std_of(nc, act, stats, var_ready, std_ready, 2)

        @block.vector
        def _(dve):
            v, link = nc.vector, make_link(dve, chain)
            link(v.memset(ones[:, :], 1.0))
            dve.wait_ge(loaded, 48)
            link(v.tensor_tensor(o[:, :, :], m.acc[:, :, 0:D], bc_last(m.deg_rsqrt[:, :], D), ALU.mult))
            link(v.tensor_tensor(sq[:, :, :], m.h[:, :, :], bc_last(m.deg_inv[:, :], D), ALU.mult))
            link(v.tensor_tensor(o[:, :, :], o[:, :, :], sq[:, :, :], ALU.add))
            link(v.tensor_tensor(o[:, :, :], o[:, :, :], bc_mid(vec[0:Q, 0, :], W), ALU.add))
            link(v.scalar_tensor_tensor(o[:, :, :], o[:, :, :], 0.01, o[:, :, :], ALU.mult, ALU.max))
            dve.sem_inc(ready, 1)
            dve.wait_ge(summed, 1)
            link(v.tensor_scalar(mean[:, :], sums[0][0:Q, 0:D], 1.0 / N, None, ALU.mult))
            link(v.tensor_tensor(o[:, :, :], o[:, :, :], bc_mid(mean[:, :], W), ALU.subtract))
            link(v.tensor_tensor(sq[:, :, :], o[:, :, :], o[:, :, :], ALU.mult))
            dve.sem_inc(ready, 1)
            dve.wait_ge(summed, 2)
            v.tensor_scalar(rstd[:, :], sums[1][0:Q, 0:D], 1.0 / N, EPS, ALU.mult, ALU.add).then_inc(var_ready, 1)
            dve.wait_ge(std_ready, 1)
            link(v.reciprocal(rstd[:, :], rstd[:, :]))
            link(v.tensor_tensor(rstd[:, :], rstd[:, :], vec[0:Q, 1, :], ALU.mult))
            link(v.tensor_tensor(o[:, :, :], o[:, :, :], bc_mid(rstd[:, :], W), ALU.mult))
            link(v.tensor_tensor(o[:, :, :], o[:, :, :], bc_mid(vec[0:Q, 2, :], W), ALU.add))
            link(v.tensor_tensor(o[:, :, :], o[:, :, :], m.x[:, :, :], ALU.add))
            layer_norm(nc, dve, link, o[:, :, :], m.x[:, :, :], sq[:, :, :], stats, EPS, var_ready, std_ready, 2)
            dve.sem_inc(out_ready, 1)


def clear(nc, acc):
    with nc.Block() as block:
        @block.gpsimd
        def _(pool):
            pool.memset(acc, 0.0)


def gat_nodes(nc, m, ins):
    with ExitStack() as ctx:
        sb, sem, bank = scope(nc, ctx)
        wr, bias, two = sb("w_r", [D, H * D]), sb("bias_lr", [P, 2, H * D]), sb("z_self", [Q, 2, H * D])
        wide = sb("wide", [P, H * D])
        xt = sb("xt3", [P, W, Q])
        tb = [bank(f"g_t{i}") for i in range(2)]
        lb, rb = [bank(f"g_l{i}") for i in range(2)], [bank(f"g_r{i}") for i in range(2)]
        loaded, turned, copied, done, zed, chain = (sem(n) for n in ("loaded3", "t3", "c3", "lr_done", "z_ready", "chain3"))
        block = ctx.enter_context(nc.Block())

        @block.sync
        def _(sp):
            sp.dma_start(wr[:, :], ins["L2_gnn_W_r"]).then_inc(loaded, 16)
            sp.dma_start(m.gat_wl[:, :], ins["L2_gnn_W_l"]).then_inc(loaded, 16)
            sp.dma_start(m.att[:, :], row_bc(ins["L2_gnn_att"].rearrange("h d -> (h d)"), P)).then_inc(loaded, 16)
            for k, name in enumerate(("L2_gnn_b_l", "L2_gnn_b_r")):
                sp.dma_start(bias[:, k, :], row_bc(ins[name], P)).then_inc(loaded, 16)
            sp.wait_ge(loaded, 80)

        @block.tensor
        def _(pe):
            turn_windows_pe(nc, pe, m, m.x, tb, turned, copied)
            pe.wait_ge(copied, TG)
            pe.wait_ge(loaded, 80)
            for w in range(W):
                if w >= 2:
                    pe.wait_ge(zed, w - 1)
                nc.tensor.matmul(lb[w % 2][0:Q, :], xt[:, w, :], m.gat_wl[:, :], start=True, stop=True)
                nc.tensor.matmul(rb[w % 2][0:Q, :], xt[:, w, :], wr[:, :], start=True, stop=True).then_inc(done, 1)

        @block.scalar
        def _(act):
            turn_windows_act(nc, act, m, xt, tb, turned, copied)

        @block.vector
        def _(dve):
            v, link = nc.vector, make_link(dve, chain)
            dve.wait_ge(loaded, 80)
            link(v.tensor_tensor(bias[:, 0, :], bias[:, 0, :], bias[:, 1, :], ALU.add))


            def dot(dst, a, part, rows):
                link(v.tensor_tensor(part, a, m.att[0:rows, :], ALU.mult))
                link(v.reduce_sum(dst, part.rearrange("q (h d) -> q h d", h=H), AX))

            dot(m.wl_att[:, :], m.gat_wl[:, :], wide[:, :], D)
            link(v.tensor_scalar(m.wl_att[:, :], m.wl_att[:, :], 0.2, None, ALU.mult))
            for w in range(W):
                dve.wait_ge(done, w + 1)
                link(v.tensor_tensor(m.acc[:, w, 0:H * D], rb[w % 2][0:Q, :], bias[0:Q, 0, :], ALU.add))
                z = two[:, w % 2, :]
                v.tensor_tensor(z, lb[w % 2][0:Q, :], m.acc[:, w, 0:H * D], ALU.add).then_inc(zed, 1)
                dot(m.acc[:, w, H * D:H * D + H], m.acc[:, w, 0:H * D], wide[0:Q, :], Q)
                dve.wait_ge(zed, w + 1)
                link(v.scalar_tensor_tensor(z, z, 0.2, z, ALU.mult, ALU.max))
                dot(m.self_score[:, w, :], z, wide[0:Q, :], Q)
            link(v.tensor_scalar(m.acc[:, :, H * D:H * D + H], m.acc[:, :, H * D:H * D + H], 0.2, None, ALU.mult))


def gat_scores(nc, m, x_table):
    with ExitStack() as ctx:
        sb, sem, bank = scope(nc, ctx)
        loop = PairLoop(nc, m, ctx, x_table)
        got, hot = loop.got, loop.hot
        got_t, hot_t = sb("got_t", [P, 2, G, P]), sb("hot_t", [Q, 2, G, P])
        leaky = sb("leaky", [P, G, H * D])
        score = sb("score", [P, 2, H, G])
        got_b, hot_b = bank("got_b"), bank("hot_b")
        z = [bank(f"z{j}") for j in range(G)]
        lin = [bank(f"lin{b}", (P, H, G)) for b in range(2)]
        copied_t, z_done, z_read, l_read, out = (sem(n) for n in ("copied_t", "z_done", "z_read", "l_read", "alpha_out"))
        block = ctx.enter_context(nc.Block())

        @block.gpsimd
        def _(pool):
            loop.gathers(pool)

        @block.vector
        def _(dve):
            v = nc.vector
            dve.sem_inc(l_read, G)
            dve.sem_inc(out, 2)
            loop.first_rows(dve)
            loop.one_hots(dve, 0, 0, 0, 1)
            with dve.Fori(0, STEPS) as i:
                for b in range(2):
                    g, at = 2 * i + b, i * (2 * G) + b * G
                    loop.one_hots(dve, at + G, 1 - b, g + 1, i + 1 + b)
                    for j in range(G):
                        dve.wait_ge(z_read, 4 * g + (j + 1 + G))
                        for h in range(H):
                            part = leaky[:, j, h * D:(h + 1) * D]
                            last = v.tensor_tensor_reduce(out=part, in0=part,
                                                          in1=m.att[:, h * D:(h + 1) * D], scale=1.0, scalar=0.0,
                                                          op0=ALU.mult, op1=ALU.add, accum_out=score[:, b, h, j:j + 1])
                        last.then_inc(l_read, 1)
                    dve.wait_ge(l_read, 4 * g + 2 * G)
                    v.tensor_tensor(m.alpha[:, :, bass.ds(at, G)], score[:, b, :, :], lin[b][:, :, :], ALU.add).then_inc(out, 1)

        @block.scalar
        def _(act):
            s = nc.scalar
            act.sem_inc(z_read, G)
            act.sem_inc(copied_t, 1)

            def copy(b, g):
                act.wait_ge(loop.used, g + 3)
                s.copy(got_t[:, b, :, :].rearrange("p j e -> p (j e)"), got_b[:, :])
                s.copy(hot_t[:, b, :, :].rearrange("p j e -> p (j e)"), hot_b[0:Q, :]).then_inc(copied_t, 1)

            copy(0, 0)
            with act.Fori(0, STEPS) as i:
                for b in range(2):
                    g = 2 * i + b
                    copy(1 - b, g + 1)
                    for j in range(G):
                        act.wait_ge(z_done, 4 * g + (j + 1))
                        act.wait_ge(l_read, 4 * g + (j + 1))
                        s.activation(leaky[:, j, :], z[j][:, :], ACT.Relu, scale=0.8).then_inc(z_read, 1)

        @block.tensor
        def _(pe):
            t = nc.tensor
            pe.sem_inc(loop.used, 2)

            def turn(b, g, seen):
                pe.wait_ge(loop.hot_ready, g + 1)
                pe.wait_ge(loop.come[b], 64 * seen)
                pe.wait_ge(copied_t, g + 1)
                for j in range(G):
                    t.transpose(got_b[:, j * P:(j + 1) * P], got[:, b, j, :], m.ident[:, :])
                    last = t.transpose(hot_b[0:Q, j * P:(j + 1) * P], hot[:, b, j, :], m.ident[:, :])
                last.then_inc(loop.used, 1)

            turn(0, 0, 1)
            with pe.Fori(0, STEPS) as i:
                for b in range(2):
                    g, at = 2 * i + b, i * (2 * G) + b * G
                    turn(1 - b, g + 1, i + 1 + b)
                    pe.wait_ge(copied_t, g + 2)
                    pe.wait_ge(out, g + 1)
                    for j in range(G):
                        pe.wait_ge(z_read, 4 * g + (j + 1))
                        w = pe.value_load(m.pair_win_i[0:1, bass.ds(at + j, 1)], min_val=0, max_val=W - 1)
                        t.matmul(lin[b][:, :, j], got_t[:, b, j, :], m.wl_att[:, :], start=True, stop=False)
                        t.matmul(lin[b][:, :, j], hot_t[:, b, j, :],
                                 m.acc[:, bass.ds(w, 1), H * D:H * D + H].rearrange("q o d -> q (o d)"), start=False, stop=True)
                        t.matmul(z[j][:, :], got_t[:, b, j, :], m.gat_wl[:, :], start=True, stop=False)
                        last = t.matmul(z[j][:, :], hot_t[:, b, j, :],
                                        m.acc[:, bass.ds(w, 1), 0:H * D].rearrange("q o d -> q (o d)"), start=False, stop=True)
                        last.then_inc(z_done, 1)


def gat_finish(nc, m, ins):
    with ExitStack() as ctx:
        sb, sem, bank = scope(nc, ctx)
        edge, own, inv = (sb(n, [Q, W, H]) for n in ("edge_w", "self_w", "inv_w"))
        tmp, stats = sb("tmp5", [Q, W, D]), sb("stats5", [Q, 2, W])
        vec = sb("vec5", [P, 3, D])
        bl = sb("bl5", [P, H * D])
        at = sb("agg_t", [P, 2, H, Q])
        tb, ob = [bank(f"a_t{i}") for i in range(2)], [bank(f"a_o{i}") for i in range(2)]
        loaded, chain, shifted, exped, ready, turned, copied, done, read, var_ready, std_ready = (sem(n) for n in (
            "loaded5", "chain5", "shifted5", "exped5", "ready5", "t5", "c5", "o5", "r5", "var5", "std5"))
        block = ctx.enter_context(nc.Block())

        @block.sync
        def _(sp):
            for k, name in enumerate(("L2_gnn_gat_bias", "L2_gnn_ln_g", "L2_gnn_ln_b")):
                sp.dma_start(vec[:, k, :], row_bc(ins[name], P)).then_inc(loaded, 16)
            sp.dma_start(bl[:, :], row_bc(ins["L2_gnn_b_l"], P)).then_inc(loaded, 16)
            sp.wait_ge(loaded, 64)

        @block.scalar
        def _(act):
            act.wait_ge(shifted, 1)
            nc.scalar.activation(edge[:, :, :], edge[:, :, :], ACT.Exp)
            nc.scalar.activation(own[:, :, :], own[:, :, :], ACT.Exp).then_inc(exped, 1)
            for w in range(W):
                act.wait_ge(turned, w + 1)
                nc.scalar.copy(at[:, w % 2, :, :].rearrange("p h q -> p (h q)"), tb[w % 2][:, 0:H * Q]).then_inc(copied, 1)
            std_of(nc, act, stats, var_ready, std_ready, 1)

        @block.tensor
        def _(pe):
            pe.wait_ge(ready, 1)

            def turn(w):
                if w >= 2:
                    pe.wait_ge(copied, w - 1)
                for h in range(H):
                    last = nc.tensor.transpose(tb[w % 2][:, h * Q:(h + 1) * Q], m.acc[:, w, h * D:(h + 1) * D], m.ident[0:Q, 0:Q])
                last.then_inc(turned, 1)

            turn(0)
            for w in range(W):
                if w + 1 < W:
                    turn(w + 1)
                pe.wait_ge(copied, w + 1)
                if w >= 2:
                    pe.wait_ge(read, w - 1)
                for h in range(H):
                    last = nc.tensor.matmul(ob[w % 2][0:Q, 0:D], at[:, w % 2, h, :], m.gat_wl[:, h * D:(h + 1) * D],
                                            start=(h == 0), stop=(h == H - 1))
                last.then_inc(done, 1)

        @block.vector
        def _(dve):
            v, link = nc.vector, make_link(dve, chain)
            den, emax = m.acc[:, :, H * D:H * D + H], m.acc[:, :, H * D + H:H * D + 2 * H]
            link(v.tensor_scalar(edge[:, :, :], den, 0.0, None, ALU.is_gt))
            link(v.tensor_scalar(edge[:, :, :], edge[:, :, :], 1.0, BIG, ALU.subtract, ALU.mult))
            link(v.tensor_tensor(edge[:, :, :], edge[:, :, :], emax, ALU.add))
            link(v.tensor_tensor(inv[:, :, :], edge[:, :, :], m.self_score[:, :, :], ALU.max))
            link(v.tensor_tensor(edge[:, :, :], edge[:, :, :], inv[:, :, :], ALU.subtract))
            link(v.tensor_tensor(own[:, :, :], m.self_score[:, :, :], inv[:, :, :], ALU.subtract))
            dve.sem_inc(shifted, 1)
            dve.wait_ge(exped, 1)
            link(v.tensor_tensor(inv[:, :, :], den, edge[:, :, :], ALU.mult))
            link(v.tensor_tensor(inv[:, :, :], inv[:, :, :], own[:, :, :], ALU.add))
            link(v.tensor_scalar(inv[:, :, :], inv[:, :, :], 1e-16, None, ALU.add))
            link(v.reciprocal(inv[:, :, :], inv[:, :, :]))
            link(v.tensor_scalar(inv[:, :, :], inv[:, :, :], 1.0 / H, None, ALU.mult))
            link(v.tensor_tensor(edge[:, :, :], edge[:, :, :], inv[:, :, :], ALU.mult))
            link(v.tensor_tensor(own[:, :, :], own[:, :, :], inv[:, :, :], ALU.mult))
            for h in range(H):
                a = m.acc[:, :, h * D:(h + 1) * D]
                link(v.tensor_tensor(a, a, bc_last(edge[:, :, h], D), ALU.mult))
                link(v.tensor_tensor(tmp[:, :, :], m.x[:, :, :], bc_last(own[:, :, h], D), ALU.mult))
                link(v.tensor_tensor(a, a, tmp[:, :, :], ALU.add))
            dve.sem_inc(ready, 1)
            dve.wait_ge(loaded, 64)
            for h in range(H):
                link(v.scalar_tensor_tensor(vec[:, 0, :], bl[:, h * D:(h + 1) * D], 1.0 / H, vec[:, 0, :], ALU.mult, ALU.add))
            link(v.tensor_tensor(tmp[:, :, :], m.x[:, :, :], bc_mid(vec[0:Q, 0, :], W), ALU.add))
            for w in range(W):
                dve.wait_ge(done, w + 1)
                v.tensor_tensor(tmp[:, w, :], tmp[:, w, :], ob[w % 2][0:Q, 0:D], ALU.add).then_inc(read, 1)
            dve.wait_ge(read, W)
            layer_norm(nc, dve, link, tmp[:, :, :], m.h[:, :, :], m.acc[:, :, 0:D], stats, EPS, var_ready, std_ready, 1)
            link(v.tensor_tensor(m.h[:, :, :], m.h[:, :, :], bc_mid(vec[0:Q, 1, :], W), ALU.mult))
            link(v.tensor_tensor(m.h[:, :, :], m.h[:, :, :], bc_mid(vec[0:Q, 2, :], W), ALU.add))


def feed_forward(nc, m, ins):
    with ExitStack() as ctx:
        sb, sem, bank = scope(nc, ctx)
        w1, w2 = sb("ff_w1", [D, 2 * D]), sb("ff_w2", [D, 2, D])
        b1, b2 = sb("ff_b1", [D, 2]), sb("ff_b2", [P, D])
        ht, ut = sb("ht", [P, W, Q]), sb("ut", [P, 2, W, Q])
        stats = sb("stats6", [Q, 2, W])
        tb, ub, ob = ([bank(f"f_{k}{i}") for i in range(2)] for k in "tuo")
        loaded, chain, turned, copied, u_done, u_read, o_done, o_read, var_ready, std_ready, leaky = (sem(n) for n in (
            "loaded6", "chain6", "t6", "c6", "u6", "ur6", "o6", "or6", "var6", "std6", "leaky6"))
        block = ctx.enter_context(nc.Block())
        tmp = m.acc[:, :, 0:D]

        @block.sync
        def _(sp):
            sp.dma_start(w1[:, :], ins["L2_gnn_W1"]).then_inc(loaded, 16)
            sp.dma_start(w2[:, :, :], ins["L2_gnn_W2"].rearrange("(c f) d -> f c d", c=2)).then_inc(loaded, 16)
            sp.dma_start(b1[:, :], ins["L2_gnn_b1"].rearrange("(c f) -> f c", c=2), allow_slow_non_contiguous=True).then_inc(loaded, 16)
            sp.dma_start(b2[:, :], row_bc(ins["L2_gnn_b2"], P)).then_inc(loaded, 16)
            sp.wait_ge(loaded, 64)

        @block.tensor
        def _(pe):
            turn_windows_pe(nc, pe, m, m.h, tb, turned, copied)
            pe.wait_ge(copied, TG)
            pe.wait_ge(loaded, 64)
            for g in range(TG):
                k = min(4, W - 4 * g)
                for c in range(2):
                    if g:
                        pe.wait_ge(u_read, 2 * (g - 1) + c + 1)
                    nc.tensor.matmul(ub[c][:, 0:k * Q], w1[:, c * D:(c + 1) * D],
                                     ht[:, 4 * g:4 * g + k, :].rearrange("d w q -> d (w q)"), start=True, stop=True).then_inc(u_done, 1)
            pe.wait_ge(leaky, 2 * TG)
            for w in range(W):
                if w >= 2:
                    pe.wait_ge(o_read, w - 1)
                for c in range(2):
                    last = nc.tensor.matmul(ob[w % 2][0:Q, 0:D], ut[:, c, w, :], w2[:, c, :], start=(c == 0), stop=(c == 1))
                last.then_inc(o_done, 1)

        @block.scalar
        def _(act):
            turn_windows_act(nc, act, m, ht, tb, turned, copied)
            act.wait_ge(loaded, 64)
            for g in range(TG):
                k = min(4, W - 4 * g)
                for c in range(2):
                    act.wait_ge(u_done, 2 * g + c + 1)
                    nc.scalar.activation(ut[:, c, 4 * g:4 * g + k, :].rearrange("d w q -> d (w q)"), ub[c][:, 0:k * Q],
                                         ACT.Identity, bias=b1[:, c:c + 1]).then_inc(u_read, 1)
            std_of(nc, act, stats, var_ready, std_ready, 1)

        @block.vector
        def _(dve):
            v, link = nc.vector, make_link(dve, chain)
            dve.wait_ge(loaded, 64)
            link(v.tensor_tensor(tmp, m.h[:, :, :], bc_mid(b2[0:Q, :], W), ALU.add))
            link(v.tensor_tensor(tmp, tmp, m.x[:, :, :], ALU.add))
            for n in range(2 * TG):
                dve.wait_ge(u_read, n + 1)
                u = ut[:, n % 2, 4 * (n // 2):min(4 * (n // 2) + 4, W), :]
                v.scalar_tensor_tensor(u, u, 0.2, u, ALU.mult, ALU.max).then_inc(leaky, 1)
            for w in range(W):
                dve.wait_ge(o_done, w + 1)
                v.tensor_tensor(m.acc[:, w, 0:D], m.acc[:, w, 0:D], ob[w % 2][0:Q, 0:D], ALU.add).then_inc(o_read, 1)
            dve.wait_ge(o_read, W)
            layer_norm(nc, dve, link, tmp, m.x[:, :, :], m.acc[:, :, D:2 * D], stats, EPS, var_ready, std_ready, 1)


def conv_nodes(nc, m, ins, n, src, k_table, v_table):
    with ExitStack() as ctx:
        sb, sem, bank = scope(nc, ctx)
        w4, b4 = sb("w4", [D, 4, D]), sb("b4", [P, 4, D])
        xt = sb("xt7", [P, W, Q])
        tb, ob = [bank(f"q_t{i}") for i in range(2)], [bank(f"q_o{i}") for i in range(2)]
        loaded, turned, copied, done, read, stored = (sem(x) for x in ("loaded7", "t7", "c7", "o7", "r7", "stored7"))
        block = ctx.enter_context(nc.Block())

        @block.sync
        def _(sp):
            for k, x in enumerate("qkvs"):
                sp.dma_start(w4[:, k, :], ins[f"L3_gnn_W{x}{n}"]).then_inc(loaded, 16)
                sp.dma_start(b4[:, k, :], row_bc(ins[f"L3_gnn_b{x}{n}"], P)).then_inc(loaded, 16)
            sp.wait_ge(read, W)
            sp.dma_start(nodes(k_table), m.acc[:, :, D:2 * D]).then_inc(stored, 16)
            sp.dma_start(nodes(v_table), m.acc[:, :, 2 * D:3 * D]).then_inc(stored, 16)
            sp.wait_ge(stored, 32)

        @block.tensor
        def _(pe):
            turn_windows_pe(nc, pe, m, src, tb, turned, copied)
            pe.wait_ge(copied, TG)
            pe.wait_ge(loaded, 128)
            for w in range(W):
                if w >= 2:
                    pe.wait_ge(read, w - 1)
                nc.tensor.matmul(ob[w % 2][0:Q, :], xt[:, w, :], w4[:, :, :].rearrange("d k c -> d (k c)"),
                                 start=True, stop=True).then_inc(done, 1)

        @block.scalar
        def _(act):
            turn_windows_act(nc, act, m, xt, tb, turned, copied)

        @block.vector
        def _(dve):
            dve.wait_ge(loaded, 128)
            for w in range(W):
                dve.wait_ge(done, w + 1)
                nc.vector.tensor_tensor(m.acc[:, w, 0:4 * D], ob[w % 2][0:Q, :], b4[0:Q, :, :].rearrange("q k c -> q (k c)"),
                                        ALU.add).then_inc(read, 1)


def conv_scores(nc, m, k_table):
    with ExitStack() as ctx:
        sb, sem, bank = scope(nc, ctx)
        loop = PairLoop(nc, m, ctx, k_table)
        got, hot = loop.got, loop.hot
        hot_t = sb("hot_t", [Q, 2, G, P])
        prod, score = sb("prod", [P, 2, G, D]), sb("score", [P, 2, G, H])
        hot_b = [bank(f"hot_b{i}") for i in range(2)]
        q_b = [bank(f"q_b{i}") for i in range(2)]
        turned, copied_t, q_done, out, chain = (sem(n) for n in ("turned", "copied_t", "q_done", "alpha_out", "chain8"))
        block = ctx.enter_context(nc.Block())

        @block.gpsimd
        def _(pool):
            loop.gathers(pool)

        @block.vector
        def _(dve):
            v = nc.vector
            dve.sem_inc(loop.used, 2)
            loop.first_rows(dve)
            loop.one_hots(dve, 0, 0, 0, 1)
            with dve.Fori(0, STEPS) as i:
                for b in range(2):
                    g, at = 2 * i + b, i * (2 * G) + b * G
                    loop.one_hots(dve, at + G, 1 - b, g + 1, i + 1 + b)
                    dve.wait_ge(q_done, g + 1)
                    v.tensor_tensor(prod[:, b, :, :].rearrange("p j d -> p (j d)"), q_b[b][:, :],
                                    got[:, b, :, :].rearrange("p j d -> p (j d)"), ALU.mult).then_inc(loop.used, 1)
                    dve.wait_ge(loop.used, g + 3)
                    v.reduce_sum(score[:, b, :, :], prod[:, b, :, :].rearrange("p j (h c) -> p j h c", h=H), AX).then_inc(chain, 1)
                    dve.wait_ge(chain, g + 1)
                    v.tensor_scalar(m.alpha[:, :, bass.ds(at, G)], score[:, b, :, :].rearrange("p j h -> p h j"),
                                    float(C) ** -0.5, None, ALU.mult).then_inc(out, 1)

        @block.scalar
        def _(act):
            def copy(b, g):
                act.wait_ge(turned, g + 1)
                nc.scalar.copy(hot_t[:, b, :, :].rearrange("p j e -> p (j e)"), hot_b[b][0:Q, :]).then_inc(copied_t, 1)

            copy(0, 0)
            with act.Fori(0, STEPS) as i:
                for b in range(2):
                    copy(1 - b, 2 * i + (b + 1))

        @block.tensor
        def _(pe):
            t = nc.tensor

            def turn(b, g):
                pe.wait_ge(loop.hot_ready, g + 1)
                for j in range(G):
                    last = t.transpose(hot_b[b][0:Q, j * P:(j + 1) * P], hot[:, b, j, :], m.ident[:, :])
                last.then_inc(turned, 1)

            turn(0, 0)
            with pe.Fori(0, STEPS) as i:
                for b in range(2):
                    g, at = 2 * i + b, i * (2 * G) + b * G
                    turn(1 - b, g + 1)
                    pe.wait_ge(copied_t, g + 1)
                    pe.wait_ge(loop.used, g + 1)
                    for j in range(G):
                        w = pe.value_load(m.pair_win_i[0:1, bass.ds(at + j, 1)], min_val=0, max_val=W - 1)
                        last = t.matmul(q_b[b][:, j * P:(j + 1) * P], hot_t[:, b, j, :],
                                        m.acc[:, bass.ds(w, 1), 0:D].rearrange("q o d -> q (o d)"), start=True, stop=True)
                    last.then_inc(q_done, 1)


def conv_finish(nc, m, last_layer, out):
    with ExitStack() as ctx:
        sb, sem, bank = scope(nc, ctx)
        inv = sb("inv9", [Q, W, H])
        tmp, stats = sb("tmp9", [Q, W, D]), sb("stats9", [Q, 2, W])
        chain, var_ready, std_ready, ready, stored = (sem(n) for n in ("chain9", "var9", "std9", "ready9", "stored9"))
        block = ctx.enter_context(nc.Block())

        if last_layer:
            @block.sync
            def _(sp):
                sp.wait_ge(ready, 1)
                sp.dma_start(nodes(out), m.h[:, :, :]).then_inc(stored, 16)
                sp.wait_ge(stored, 16)

            @block.scalar
            def _(act):
                std_of(nc, act, stats, var_ready, std_ready, 1)

        @block.vector
        def _(dve):
            v, link = nc.vector, make_link(dve, chain)
            link(v.tensor_scalar(inv[:, :, :], m.sums[:, :, D:D + H], 1e-30, None, ALU.max))
            link(v.reciprocal(inv[:, :, :], inv[:, :, :]))
            link(v.tensor_tensor(tmp[:, :, :].rearrange("q w (h c) -> q w h c", h=H),
                                 m.sums[:, :, 0:D].rearrange("q w (h c) -> q w h c", h=H),
                                 inv[:, :, :].unsqueeze(3).broadcast_to([Q, W, H, C]), ALU.mult))
            link(v.tensor_tensor(tmp[:, :, :], tmp[:, :, :], m.acc[:, :, 3 * D:4 * D], ALU.add))
            if not last_layer:
                link(v.tensor_scalar(m.h[:, :, :], tmp[:, :, :], 0.0, None, ALU.max))
            else:
                link(v.tensor_tensor(tmp[:, :, :], tmp[:, :, :], m.x[:, :, :], ALU.add))
                layer_norm(nc, dve, link, tmp[:, :, :], m.h[:, :, :], m.acc[:, :, 0:D], stats, EPS, var_ready, std_ready, 1)
                dve.sem_inc(ready, 1)


def build(nc, ins, out):
    with ExitStack() as ctx:
        m = Mem()
        sb, sem, bank = scope(nc, ctx)
        common(m, sb)
        m.come = [[sem(f"come{n}_{b}") for b in range(2)] for n in range(8)]
        m.added = [sem(f"added{j}") for j in range(G)]
        y_table = nc.dram_tensor("y_table", [R * N, D], F32, kind="Internal").ap()
        tables = [nc.dram_tensor(f"agg{j}", [ACCROWS, D], F32, kind="Internal").ap() for j in range(G)]
        t_table, x_table, k_table, v_table = (nc.dram_tensor(n, [N, D], F32, kind="Internal").ap()
                                              for n in ("t_table", "x_table", "k_table", "v_table"))
        setup_phase(nc, m, ins)
        relation_rows(nc, m, ins, y_table)
        count_edges(nc, m)
        relation_edges(nc, m, y_table, tables)
        m.h = sb("h", [Q, W, D])
        m.self_score = sb("self_score", [Q, W, H])
        m.gat_wl, m.att, m.wl_att = sb("gat_wl", [D, H * D]), sb("att", [P, H * D]), sb("wl_att", [D, H])
        gcn_nodes(nc, m, ins, tables, t_table)
        m.acc = sb("acc", [Q, W, H * D + 2 * H])
        clear(nc, m.acc[:, :, 0:D])
        pair_sums(nc, m, t_table, m.acc, 0)
        batch_norm(nc, m, ins, x_table)
        gat_nodes(nc, m, ins)
        gat_scores(nc, m, x_table)
        segment_softmax(nc, m)
        clear(nc, m.acc[:, :, :])
        pair_sums(nc, m, x_table, m.acc, H)
        gat_finish(nc, m, ins)
        feed_forward(nc, m, ins)
        m.sums = sb("sums", [Q, W, D + H])
        for n, src in ((1, m.x), (2, m.h)):
            conv_nodes(nc, m, ins, n, src, k_table, v_table)
            conv_scores(nc, m, k_table)
            segment_softmax(nc, m)
            clear(nc, m.sums[:, :, :])
            pair_sums(nc, m, v_table, m.sums, 1)
            conv_finish(nc, m, n == 2, out)


def kernel(**inputs):
    import numpy as _np
    import concourse.bacc as _bacc
    from concourse import mybir as _mybir
    from concourse.bass_utils import run_bass_kernel_spmd as _run

    nc = _bacc.Bacc("TRN2", target_bir_lowering=False, num_devices=1)
    arrays, args = {}, {}
    for name in inputs:
        a = _np.ascontiguousarray(inputs[name])
        arrays[f"in_{name}_dram"] = a
        args[name] = nc.dram_tensor(f"in_{name}_dram", a.shape, _mybir.dt.from_np(a.dtype), kind="ExternalInput").ap()
    out = nc.dram_tensor("out_0_dram", (N, D), F32, kind="ExternalOutput").ap()
    build(nc, args, out)
    r = _run(nc, [arrays], core_ids=[0])
    return r.results[0]["out_0_dram"]
```

```python
import itertools
import numpy as np
import concourse.bass as bass
import concourse.mybir as mybir
from contextlib import ExitStack

F32, BF16, I32, U32 = mybir.dt.float32, mybir.dt.bfloat16, mybir.dt.int32, mybir.dt.uint32
ENG = mybir.EngineType
ALU, ACT, AX = mybir.AluOpType, mybir.ActivationFunctionType, mybir.AxisListType.X

N, E, D, R, H = 3125, 50000, 128, 8, 4
Q, W = 125, 25
P = 128
C = 32
TILES = 392
CH = 98
NCH = TILES // CH
FULL, REST = E // P, E % P
PAIRS = 416
G = 4
PAD_DST, PAD_SRC = 4000, 3200
ROWLO, ROWHI = 128, 196
ACCROWS = 27 * P
DUMP = 26 * P
BIG = 1.0e30
EPS = 1e-5
SLOTPAD = PAIRS + 4 * G
BLOCKS = H * PAIRS // P
assert TILES * P >= E and FULL + W <= PAIRS and Q * W == N and R * N <= ROWLO * ROWHI


PHASE = itertools.count()


class Mem:
    pass


def scope(nc, ctx):
    n = next(PHASE)
    sems = []

    def clear_semaphores(failed, *_):
        if sems and not failed:
            with nc.Block() as block:
                @block.gpsimd
                def _(pool):
                    for s in sems:
                        pool.sem_clear(s)

    ctx.push(clear_semaphores)

    def sb(name, shape, dt=F32):
        return ctx.enter_context(nc.sbuf_tensor(f"{name}_{n}", shape, dt))

    def sem(name):
        sems.append(ctx.enter_context(nc.semaphore(f"{name}_{n}")))
        return sems[-1]

    def bank(name, shape=(P, 512), dt=F32):
        return ctx.enter_context(nc.psum_tensor(f"{name}_{n}", list(shape), dt))

    return sb, sem, bank

def bc_mid(ap, n):
    return ap.unsqueeze(1).broadcast_to([ap.shape[0], n, ap.shape[1]])


def bc_last(ap, n):
    return ap.unsqueeze(2).broadcast_to([ap.shape[0], ap.shape[1], n])


def row_bc(ap, n):
    return ap.rearrange("(o n) -> o n", o=1).broadcast_to([n, ap.shape[0]])


def nodes(ap):
    return ap.rearrange("(w q) d -> q w d", q=Q)


def setup_phase(nc, m, ins):
    with ExitStack() as ctx:
        sb, sem, bank = scope(nc, ctx)

        nat_i = sb("nat_i", [CH, 3, NCH, P], I32)
        row_i = sb("row_i", [CH, 3, NCH, P], I32)
        nat = sb("nat", [CH, 2, NCH, P])
        win = sb("win", [CH, NCH, P])
        quant = sb("quant", [CH, 5, NCH, P])
        edge_flags = sb("edge_flags", [CH, 2, NCH, P])
        below = sb("below", [CH, NCH, W])
        thresholds = sb("thresholds", [P, W])
        tile_no = sb("tile_no", [P, NCH])
        pick = sb("pick", [CH, NCH, PAIRS])
        ones = sb("ones", [P, P])
        ends = sb("ends", [P, W])
        pair_tile = sb("pair_tile", [P, PAIRS])
        last0 = sb("last0", [P, 2, PAIRS])
        same = sb("same", [P, 4, PAIRS])
        io = sb("io", [P, 512], I32)
        io2 = sb("io2", [P, NCH], I32)
        ps = [bank(f"ps{i}") for i in range(8)]
        loaded, consts, chain = sem("edges_loaded"), sem("consts"), sem("dve_chain")
        padded, quant_ready, lanes_done = sem("padded"), sem("quant_ready"), sem("lanes_done")
        lanes_read, below_ready, ends_done = sem("lanes_read"), sem("below_ready"), sem("ends_done")
        pick_ready, slots_done, slots_read = sem("pick_ready"), sem("slots_done"), sem("slots_read")
        pens_ready, pens_turned = sem("pens_ready"), sem("pens_turned")
        start_pen = sb("start_pen", [P, H, PAIRS])
        end_pen = sb("end_pen", [P, H, PAIRS])
        block = ctx.enter_context(nc.Block())

        @block.sync
        def _(sp):
            sp.wait_ge(padded, 1)
            for k, name in enumerate(("src", "dst", "edge_type_8")):
                a = ins[name]
                for c in range(NCH):
                    rows = min(CH, FULL - CH * c)
                    sp.dma_start(nat_i[0:rows, k, c, :],
                                 a[c * CH * P:(c * CH + rows) * P].rearrange("(t l) -> t l", l=P)).then_inc(loaded, 16)
                    if rows < CH:
                        sp.dma_start(nat_i[rows:rows + 1, k, c, 0:REST],
                                     a[FULL * P:E].rearrange("(o l) -> o l", o=1)).then_inc(loaded, 16)
            sp.dma_start(m.x[:, :, :], nodes(ins["x"])).then_inc(loaded, 16)
            sp.wait_ge(loaded, 16 * (3 * (NCH + 1) + 1))

        @block.gpsimd
        def _(pool):
            pool.memset(nat_i[:, 0, :, :], PAD_SRC).then_inc(consts, 1)
            pool.memset(nat_i[:, 1, :, :], PAD_DST).then_inc(consts, 1)
            pool.memset(nat_i[:, 2, :, :], 0).then_inc(consts, 1)
            pool.wait_ge(consts, 3)
            pool.sem_inc(padded, 1)
            pool.memset(m.ident[:, :], 0.0).then_inc(consts, 1)
            pool.memset(m.rows_before[:, :], 1.0).then_inc(consts, 1)
            pool.memset(m.only0[:, :], 0.0).then_inc(consts, 1)
            pool.memset(m.only127[:, :], 0.0).then_inc(consts, 1)
            pool.memset(ones[:, :], 1.0).then_inc(consts, 1)
            pool.iota(io[:, :], [[1, 512]], base=0, channel_multiplier=0).then_inc(consts, 1)
            pool.iota(io2[:, :], [[CH, NCH]], base=0, channel_multiplier=1).then_inc(consts, 1)
            pool.wait_ge(consts, 10)
            pool.affine_select(out=m.ident[:, :], in_=m.ident[:, :], compare_op=ALU.not_equal, fill=1.0,
                               base=0, pattern=[[-1, P]], channel_multiplier=1).then_inc(consts, 1)
            pool.affine_select(out=m.rows_before[:, :], in_=m.rows_before[:, :], compare_op=ALU.is_gt, fill=0.0,
                               base=0, pattern=[[-1, P]], channel_multiplier=1).then_inc(consts, 1)
            pool.affine_select(out=m.only0[:, :], in_=m.only0[:, :], compare_op=ALU.not_equal, fill=1.0,
                               base=0, pattern=[[0, P]], channel_multiplier=1).then_inc(consts, 1)
            pool.affine_select(out=m.only127[:, :], in_=m.only127[:, :], compare_op=ALU.not_equal, fill=1.0,
                               base=-(P - 1), pattern=[[0, P]], channel_multiplier=1).then_inc(consts, 1)

        @block.vector
        def _(dve):
            v, count = nc.vector, [0]

            def link(op):
                count[0] += 1
                op.then_inc(chain, 1)
                dve.wait_ge(chain, count[0])

            dve.wait_ge(consts, 14)
            v.tensor_copy(m.iota[:, :], io[:, :]).then_inc(chain, 1)
            v.tensor_copy(tile_no[:, :], io2[:, :]).then_inc(chain, 1)
            v.tensor_copy(m.lane[:, :], io2[:, 0:1]).then_inc(chain, 1)
            v.tensor_copy(m.ident_b[:, :], m.ident[:, :]).then_inc(chain, 1)
            v.memset(m.pair_src[:, PAIRS:SLOTPAD], 0).then_inc(chain, 1)
            v.memset(m.y_row[:, TILES:TILES + 8], 0).then_inc(chain, 1)
            v.memset(m.src_lane[:, TILES:TILES + 8], 0.0).then_inc(chain, 1)
            v.memset(m.pair_dst[:, PAIRS:PAIRS + 2 * G], -1.0).then_inc(chain, 1)
            v.memset(m.small[:, PAIRS:PAIRS + G, :], 0.0).then_inc(chain, 1)
            count[0] = 9
            dve.wait_ge(chain, 9)
            link(v.tensor_copy(m.iota_b[:, :], m.iota[:, 0:256]))
            link(v.tensor_scalar(thresholds[:, :], m.iota[:, 0:W], float(Q), float(Q), ALU.mult, ALU.add))
            dve.wait_ge(loaded, 16 * (3 * (NCH + 1) + 1))
            src_i, dst_i, rel_i = nat_i[:, 0, :, :], nat_i[:, 1, :, :], nat_i[:, 2, :, :]
            v.tensor_copy(nat[:, 0, :, :], src_i).then_inc(chain, 1)
            v.tensor_copy(nat[:, 1, :, :], dst_i).then_inc(chain, 1)
            v.scalar_tensor_tensor(row_i[:, 0, :, :], src_i, float(R), rel_i, ALU.mult, ALU.add).then_inc(chain, 1)
            v.scalar_tensor_tensor(quant[:, 1, :, :], dst_i, float(R), rel_i, ALU.mult, ALU.add).then_inc(chain, 1)
            count[0] += 4
            dve.wait_ge(chain, count[0])
            link(v.tensor_tensor(below[:, :, :], nat[:, 1, :, P - 1:P].broadcast_to([CH, NCH, W]),
                                 bc_mid(thresholds[0:CH, :], NCH), ALU.is_lt))
            dve.sem_inc(below_ready, 1)
            link(v.tensor_scalar(quant[:, 1, :, :], quant[:, 1, :, :], float(R * N - 1), None, ALU.min))
            link(v.tensor_copy(quant[:, 0, :, :], nat[:, 0, :, :]))
            link(v.tensor_scalar(row_i[:, 1, :, :], row_i[:, 0, :, :], ROWLO - 1, None, ALU.bitwise_and))
            link(v.tensor_scalar(row_i[:, 2, :, :], row_i[:, 0, :, :], 7, None, ALU.arith_shift_right))
            link(v.tensor_copy(quant[:, 2, :, :], row_i[:, 1, :, :]))
            link(v.tensor_copy(quant[:, 3, :, :], row_i[:, 2, :, :]))
            link(v.tensor_scalar(win[:, :, :], nat[:, 1, :, :], float(Q), None, ALU.is_ge))
            for w in range(2, W):
                link(v.scalar_tensor_tensor(win[:, :, :], nat[:, 1, :, :], float(Q * w), win[:, :, :], ALU.is_ge, ALU.add))
            link(v.scalar_tensor_tensor(quant[:, 4, :, :], win[:, :, :], -float(Q), nat[:, 1, :, :], ALU.mult, ALU.add))
            link(v.memset(edge_flags[:, :, :, :], -BIG))
            v.tensor_tensor(edge_flags[:, 0, :, 1:P], nat[:, 1, :, 1:P], nat[:, 1, :, 0:P - 1], ALU.not_equal).then_inc(chain, 1)
            v.tensor_tensor(edge_flags[:, 1, :, 0:P - 1], nat[:, 1, :, 1:P], nat[:, 1, :, 0:P - 1], ALU.not_equal).then_inc(chain, 1)
            count[0] += 2
            dve.wait_ge(chain, count[0])
            v.tensor_scalar(edge_flags[:, 0, :, 1:P], edge_flags[:, 0, :, 1:P], -BIG, None, ALU.mult).then_inc(chain, 1)
            v.tensor_scalar(edge_flags[:, 1, :, 0:P - 1], edge_flags[:, 1, :, 0:P - 1], -BIG, None, ALU.mult).then_inc(chain, 1)
            count[0] += 2
            dve.wait_ge(chain, count[0])
            dve.sem_inc(quant_ready, 1)
            dve.wait_ge(ends_done, 1)
            link(v.tensor_tensor(ends[:, :], ps[7][:, 0:W], m.iota[:, 0:W], ALU.add))
            link(v.tensor_scalar(m.pair_win[:, :], m.iota[:, 0:PAIRS], ends[:, 0:1], None, ALU.is_gt))
            for w in range(1, W - 1):
                link(v.scalar_tensor_tensor(m.pair_win[:, :], m.iota[:, 0:PAIRS], ends[:, w:w + 1], m.pair_win[:, :],
                                            ALU.is_gt, ALU.add))
            link(v.tensor_copy(m.pair_win_i[:, :], m.pair_win[0:1, :]))
            link(v.tensor_tensor(pair_tile[:, :], m.iota[:, 0:PAIRS], m.pair_win[:, :], ALU.subtract))
            for c in range(NCH):
                link(v.tensor_scalar(pick[:, c, :], pair_tile[0:CH, :], tile_no[0:CH, c:c + 1], None, ALU.is_equal))
            dve.sem_inc(pick_ready, 1)
            dve.wait_ge(lanes_done, 1)
            v.tensor_copy(m.src_lane[:, 0:TILES], ps[0][:, 0:TILES]).then_inc(lanes_read, 1)
            v.tensor_copy(m.y_row[:, 0:TILES], ps[1][:, 0:TILES]).then_inc(lanes_read, 1)
            v.tensor_copy(m.row_lo[:, :], ps[2][:, 0:TILES]).then_inc(lanes_read, 1)
            v.tensor_copy(m.row_hi[:, :], ps[3][:, 0:TILES]).then_inc(lanes_read, 1)
            v.tensor_copy(m.dst_loc[:, :], ps[4][:, 0:TILES]).then_inc(lanes_read, 1)
            v.tensor_copy(m.dst_win[:, :], ps[5][:, 0:TILES]).then_inc(lanes_read, 1)
            dve.wait_ge(slots_done, 1)
            link(v.tensor_scalar(m.pair_src[:, 0:PAIRS], ps[0][:, 0:PAIRS], float(N - 1), None, ALU.min))
            link(v.scalar_tensor_tensor(m.pair_dst[:, 0:PAIRS], m.pair_win[:, :], -float(Q), ps[1][:, 0:PAIRS], ALU.mult, ALU.add))
            for h in range(H):
                link(v.tensor_copy(start_pen[:, h, :], ps[2][:, 0:PAIRS]))
                link(v.tensor_copy(end_pen[:, h, :], ps[3][:, 0:PAIRS]))
            dve.sem_inc(pens_ready, 1)
            link(v.tensor_copy(last0[:, 0, :], ps[4][:, 0:PAIRS]))
            link(v.tensor_copy(last0[:, 1, :], ps[5][:, 0:PAIRS]))
            link(v.tensor_tensor(same[:, 0, :], ps[1][:, 0:PAIRS], last0[:, 1, :], ALU.not_equal))
            link(v.tensor_tensor(same[:, 1, :], ps[1][:, 0:PAIRS], last0[:, 0, :], ALU.not_equal))
            dve.sem_inc(slots_read, 1)
            link(v.tensor_scalar(m.first_pen[:, :], same[:, 0, :], -BIG, None, ALU.mult))
            link(v.tensor_scalar(m.last_pen[:, :], same[:, 1, :], -BIG, None, ALU.mult))
            link(v.memset(same[:, 2:3, :], 0.0))
            link(v.tensor_tensor(same[:, 2, 1:PAIRS], last0[:, 1, 1:PAIRS], last0[:, 0, 0:PAIRS - 1], ALU.is_equal))
            link(v.tensor_tensor(same[:, 3, 1:PAIRS], m.pair_win[:, 1:PAIRS], m.pair_win[:, 0:PAIRS - 1], ALU.is_equal))
            link(v.tensor_tensor(same[:, 2, 1:PAIRS], same[:, 2, 1:PAIRS], same[:, 3, 1:PAIRS], ALU.mult))
            link(v.tensor_tensor(same[:, 3, :], last0[:, 0, :], last0[:, 1, :], ALU.is_equal))
            link(v.tensor_scalar(m.cont_pen[:, :], same[:, 2, :], 1.0, BIG, ALU.subtract, ALU.mult))
            link(v.tensor_tensor(same[:, 0, :], same[:, 2, :], same[:, 3, :], ALU.mult))
            link(v.memset(same[:, 1, :], 0.0))
            link(v.tensor_tensor(same[:, 1, 0:PAIRS - 1], same[:, 2, 1:PAIRS], same[:, 3, 0:PAIRS - 1], ALU.mult))
            for h in range(H):
                link(v.tensor_scalar(m.fwd_pen[:, h, :], same[:, 0, :], 1.0, BIG, ALU.subtract, ALU.mult))
                link(v.tensor_scalar(m.bwd_pen[:, h, :], same[:, 1, :], 1.0, BIG, ALU.subtract, ALU.mult))
            link(v.tensor_scalar(m.leader[:, :], start_pen[:, 0, :], -1.0, None, ALU.is_lt))
            link(v.tensor_scalar(same[:, 1, :], same[:, 2, :], m.only0[:, 0:1], None, ALU.mult))
            link(v.tensor_tensor(m.leader[:, :], m.leader[:, :], same[:, 1, :], ALU.subtract))
            dve.wait_ge(pens_turned, 1)
            for k in range(4):
                cols = min(512, H * PAIRS - 512 * k)
                link(v.tensor_copy(m.start_turned[:, 512 * k:512 * k + cols], ps[k][:, 0:cols]))
                link(v.tensor_copy(m.end_turned[:, 512 * k:512 * k + cols], ps[4 + k][:, 0:cols]))

        @block.tensor
        def _(pe):
            t = nc.tensor
            pe.wait_ge(consts, 14)
            pe.wait_ge(below_ready, 1)
            for c in range(NCH):
                last = t.matmul(ps[7][:, 0:W], ones[0:CH, :], below[:, c, :], start=(c == 0), stop=(c == NCH - 1))
            last.then_inc(ends_done, 1)
            pe.wait_ge(quant_ready, 1)
            for k in range(6):
                for c in range(NCH):
                    a = quant[:, k, c, :] if k < 5 else win[:, c, :]
                    last = t.transpose(ps[k][:, c * CH:(c + 1) * CH], a, m.ident[0:CH, 0:CH])
            last.then_inc(lanes_done, 1)
            pe.wait_ge(pick_ready, 1)
            pe.wait_ge(lanes_read, 6)
            for k in range(6):
                for c in range(NCH):
                    if k < 2:
                        a = nat[:, k, c, :]
                    elif k < 4:
                        a = edge_flags[:, k - 2, c, :]
                    else:
                        lane = P - 1 if k == 4 else 0
                        a = nat[:, 1, c, lane:lane + 1].broadcast_to([CH, P])
                    last = t.matmul(ps[k][:, 0:PAIRS], a, pick[:, c, :], start=(c == 0), stop=(c == NCH - 1))
            last.then_inc(slots_done, 1)
            pe.wait_ge(pens_ready, 1)
            pe.wait_ge(slots_read, 1)
            for base, pen in ((0, start_pen), (4, end_pen)):
                flat = pen[:, :, :].rearrange("l h p -> l (h p)")
                for n in range(BLOCKS):
                    last = t.transpose(ps[base + n // 4][:, (n % 4) * P:(n % 4 + 1) * P], flat[:, n * P:(n + 1) * P],
                                       m.ident[:, :])
            last.then_inc(pens_turned, 1)


def segment_softmax(nc, m):
    with ExitStack() as ctx:
        sb, sem, bank = scope(nc, ctx)

        cols = H * PAIRS
        carried = sb("carried", [P, 2, H, PAIRS])
        fwd, both = (carried[:, k, :, :].rearrange("l h p -> l (h p)") for k in range(2))
        top = sb("top", [P, H, PAIRS])
        ends2 = sb("ends2", [P, 2, cols])
        ps = [bank(f"sg{i}") for i in range(8)]
        turned, scanned, back, top_ready = sem("turned"), sem("scanned"), sem("back"), sem("top_ready")
        ends_ready, chain, shifted, exped = sem("ends_ready"), sem("seg_chain"), sem("shifted"), sem("exped")
        block = ctx.enter_context(nc.Block())
        alpha = m.alpha[:, :, :].rearrange("l h p -> l (h p)")
        topf = top[:, :, :].rearrange("l h p -> l (h p)")

        def width(k):
            return min(512, cols - 512 * k)

        @block.tensor
        def _(pe):
            t = nc.tensor
            for n in range(BLOCKS):
                last = t.transpose(ps[n // 4][:, (n % 4) * P:(n % 4 + 1) * P], alpha[:, n * P:(n + 1) * P], m.ident[:, :])
            last.then_inc(turned, 1)
            pe.wait_ge(scanned, 1)
            for n in range(BLOCKS):
                last = t.transpose(ps[4 + n // 4][:, (n % 4) * P:(n % 4 + 1) * P], both[:, n * P:(n + 1) * P], m.ident[:, :])
            last.then_inc(back, 1)
            pe.wait_ge(top_ready, 1)
            for k in range(4):
                last = t.matmul(ps[k][:, 0:width(k)], m.only0[:, :], topf[:, 512 * k:512 * k + width(k)], start=True, stop=True)
                last = t.matmul(ps[4 + k][:, 0:width(k)], m.only127[:, :], topf[:, 512 * k:512 * k + width(k)],
                                start=True, stop=True)
            last.then_inc(ends_ready, 1)

        @block.scalar
        def _(act):
            act.wait_ge(shifted, 1)
            nc.scalar.activation(m.small[:, 0:PAIRS, 0:H], top[:, :, :].rearrange("l h p -> l p h"), ACT.Exp).then_inc(exped, 1)

        @block.vector
        def _(dve):
            v, count = nc.vector, [0]

            def link(op):
                count[0] += 1
                op.then_inc(chain, 1)
                dve.wait_ge(chain, count[0])

            dve.wait_ge(turned, 1)
            for k in range(4):
                a, b = 512 * k, 512 * k + width(k)
                link(v.tensor_tensor_scan(fwd[:, a:b], m.start_turned[:, a:b], ps[k][:, 0:width(k)], -BIG, ALU.add, ALU.max))
            link(v.tensor_tensor_scan(both[:, ::-1], m.end_turned[:, ::-1], fwd[:, ::-1], -BIG, ALU.add, ALU.max))
            dve.sem_inc(scanned, 1)
            dve.wait_ge(back, 1)
            for k in range(4):
                link(v.tensor_copy(topf[:, 512 * k:512 * k + width(k)], ps[4 + k][:, 0:width(k)]))
            dve.sem_inc(top_ready, 1)
            dve.wait_ge(ends_ready, 1)
            for k in range(4):
                link(v.tensor_copy(ends2[:, 0, 512 * k:512 * k + width(k)], ps[k][:, 0:width(k)]))
                link(v.tensor_copy(ends2[:, 1, 512 * k:512 * k + width(k)], ps[4 + k][:, 0:width(k)]))
            fpen = m.fwd_pen[:, :, :].rearrange("l h p -> l (h p)")
            bpen = m.bwd_pen[:, :, :].rearrange("l h p -> l (h p)")
            link(v.tensor_tensor_scan(fwd, fpen, ends2[:, 1, :], -BIG, ALU.add, ALU.max))
            link(v.tensor_tensor_scan(both[:, ::-1], bpen[:, ::-1], ends2[:, 0, ::-1], -BIG, ALU.add, ALU.max))
            inc = ends2[:, 0, :].rearrange("l (h p) -> l h p", h=H)
            inb = ends2[:, 1, :].rearrange("l (h p) -> l h p", h=H)
            link(v.memset(ends2[:, :, :], -BIG))
            link(v.tensor_tensor(inc[:, :, 1:PAIRS], carried[:, 0, :, 0:PAIRS - 1], bc_mid(m.cont_pen[:, 1:PAIRS], H), ALU.add))
            link(v.tensor_tensor(inb[:, :, 0:PAIRS - 1], carried[:, 1, :, 1:PAIRS], bc_mid(m.cont_pen[:, 1:PAIRS], H), ALU.add))
            link(v.tensor_tensor(inc, inc, bc_mid(m.first_pen[:, :], H), ALU.add))
            link(v.tensor_tensor(inb, inb, bc_mid(m.last_pen[:, :], H), ALU.add))
            link(v.tensor_tensor(inc, inc, inb, ALU.max))
            link(v.tensor_tensor(top[:, :, :], top[:, :, :], inc, ALU.max))
            link(v.tensor_tensor(m.small[:, 0:PAIRS, H:2 * H], top[:, :, :].rearrange("l h p -> l p h"), bc_last(m.leader[:, :], H), ALU.mult))
            link(v.tensor_tensor(top[:, :, :], m.alpha[:, :, :], top[:, :, :], ALU.subtract))
            link(v.tensor_scalar(top[:, :, :], top[:, :, :], 0.0, None, ALU.min))
            dve.sem_inc(shifted, 1)
            dve.wait_ge(exped, 1)

def common(m, sb):
    m.x = sb("x_nodes", [Q, W, D])
    m.ident, m.ident_b = sb("ident", [P, P]), sb("ident_b", [P, P], BF16)
    m.rows_before = sb("rows_before", [P, P])
    m.only0, m.only127 = sb("only0", [P, P]), sb("only127", [P, P])
    m.iota, m.iota_b = sb("iota", [P, 512]), sb("iota_b", [P, 256], BF16)
    m.lane = sb("lane", [P, 1])
    m.pair_src = sb("pair_src", [P, SLOTPAD], U32)
    m.pair_dst = sb("pair_dst", [P, PAIRS + 2 * G])
    m.pair_win = sb("pair_win", [P, PAIRS])
    m.pair_win_i = sb("pair_win_i", [1, PAIRS], I32)
    m.y_row = sb("y_row", [P, TILES + 8], U32)
    m.src_lane = sb("src_lane", [P, TILES + 8])
    m.row_lo, m.row_hi = sb("row_lo", [P, TILES], BF16), sb("row_hi", [P, TILES], BF16)
    m.dst_loc, m.dst_win = sb("dst_loc", [P, TILES], BF16), sb("dst_win", [P, TILES], BF16)
    m.start_turned, m.end_turned = sb("start_turned", [P, H * PAIRS]), sb("end_turned", [P, H * PAIRS])
    m.first_pen, m.last_pen, m.cont_pen = (sb(n, [P, PAIRS]) for n in ("first_pen", "last_pen", "cont_pen"))
    m.fwd_pen, m.bwd_pen = sb("fwd_pen", [P, H, PAIRS]), sb("bwd_pen", [P, H, PAIRS])
    m.leader = sb("leader", [P, PAIRS])
    m.alpha = sb("alpha", [P, H, PAIRS])
    m.small = sb("small", [P, PAIRS + G, 2 * H])
    m.row_inv = sb("row_inv", [P, 3, ROWHI], BF16)
    m.deg_inv, m.deg_rsqrt = sb("deg_inv", [Q, W]), sb("deg_rsqrt", [Q, W])



def layer_norm(nc, dve, link, x, y, tmp, stats, eps, var_ready, std_ready, turn):
    v = nc.vector
    mean, var = stats[:, 0, :], stats[:, 1, :]
    link(v.reduce_sum(mean, x, AX))
    link(v.tensor_scalar(mean, mean, 1.0 / D, None, ALU.mult))
    link(v.tensor_tensor(y, x, bc_last(mean, D), ALU.subtract))
    link(v.tensor_tensor(tmp, y, y, ALU.mult))
    link(v.reduce_sum(var, tmp, AX))
    v.tensor_scalar(var, var, 1.0 / D, eps, ALU.mult, ALU.add).then_inc(var_ready, 1)
    dve.wait_ge(std_ready, turn)
    link(v.reciprocal(mean, var))
    link(v.tensor_tensor(y, y, bc_last(mean, D), ALU.mult))


def std_of(nc, act, stats, var_ready, std_ready, turn):
    act.wait_ge(var_ready, turn)
    nc.scalar.activation(stats[:, 1, :], stats[:, 1, :], ACT.Sqrt).then_inc(std_ready, 1)


TG = (W + 3) // 4


def turn_windows_pe(nc, pe, m, src, banks, turned, copied, done=0):
    for g in range(TG):
        n = done + g
        if n >= 2:
            pe.wait_ge(copied, n - 1)
        for w in range(4 * g, min(4 * g + 4, W)):
            last = nc.tensor.transpose(banks[n % 2][:, (w % 4) * Q:(w % 4 + 1) * Q], src[:, w, :], m.ident[0:Q, 0:Q])
        last.then_inc(turned, 1)


def turn_windows_act(nc, act, m, dst, banks, turned, copied, done=0):
    for g in range(TG):
        n = done + g
        act.wait_ge(turned, n + 1)
        k = min(4, W - 4 * g)
        nc.scalar.copy(dst[:, 4 * g:4 * g + k, :].rearrange("d w q -> d (w q)"), banks[n % 2][:, 0:k * Q]).then_inc(copied, 1)


def relation_rows(nc, m, ins, y_table):
    with ExitStack() as ctx:
        sb, sem, bank = scope(nc, ctx)
        w0, w0t = sb("w0", [P, R, D]), sb("w0t", [P, R * D])
        xt = sb("xt0", [P, W, Q])
        stage = sb("y_stage", [Q, 2, R * D])
        tb = [bank(f"tb{i}") for i in range(2)]
        wb = [bank(f"wb{i}") for i in range(2)]
        yb = [bank(f"yb{i}") for i in range(4)]
        loaded, turned, copied, wt, wc = (sem(n) for n in ("w0_loaded", "x_turned", "xt_copied", "w_turned", "wt_copied"))
        y_done, y_left, y_right = sem("y_done"), sem("y_left"), sem("y_right")
        stored = [sem("y_stored0"), sem("y_stored1")]
        block = ctx.enter_context(nc.Block())

        @block.sync
        def _(sp):
            sp.dma_start(w0[:, :, :], ins["L0_gnn_weights"].rearrange("r i j -> i r j")).then_inc(loaded, 16)
            for w in range(W):
                sp.wait_ge(y_left, w + 1)
                sp.wait_ge(y_right, w + 1)
                sp.dma_start(y_table.rearrange("(n r) d -> n (r d)", r=R)[w * Q:(w + 1) * Q, :],
                             stage[:, w % 2, :]).then_inc(stored[w % 2], 16)
            sp.wait_ge(stored[0], 16 * ((W + 1) // 2))
            sp.wait_ge(stored[1], 16 * (W // 2))

        @block.tensor
        def _(pe):
            pe.wait_ge(loaded, 16)
            for r in range(R):
                last = nc.tensor.transpose(wb[r // 4][:, (r % 4) * D:(r % 4 + 1) * D], w0[:, r, :], m.ident[:, :])
            last.then_inc(wt, 1)
            turn_windows_pe(nc, pe, m, m.x, tb, turned, copied)
            pe.wait_ge(wc, 2)
            pe.wait_ge(copied, TG)
            for w in range(W):
                if w >= 2:
                    pe.wait_ge(y_left, w - 1)
                    pe.wait_ge(y_right, w - 1)
                for k in range(2):
                    last = nc.tensor.matmul(yb[2 * (w % 2) + k][0:Q, :], xt[:, w, :], w0t[:, k * 512:(k + 1) * 512],
                                            start=True, stop=True)
                last.then_inc(y_done, 1)

        @block.scalar
        def _(act):
            turn_windows_act(nc, act, m, xt, tb, turned, copied)
            for w in range(W):
                act.wait_ge(y_done, w + 1)
                if w >= 2:
                    act.wait_ge(stored[w % 2], 16 * (w // 2))
                nc.scalar.copy(stage[:, w % 2, 0:512], yb[2 * (w % 2)][0:Q, :]).then_inc(y_left, 1)

        @block.vector
        def _(dve):
            dve.wait_ge(wt, 1)
            nc.vector.tensor_copy(w0t[:, 0:512], wb[0][:, :]).then_inc(wc, 1)
            nc.vector.tensor_copy(w0t[:, 512:1024], wb[1][:, :]).then_inc(wc, 1)
            for w in range(W):
                dve.wait_ge(y_done, w + 1)
                if w >= 2:
                    dve.wait_ge(stored[w % 2], 16 * (w // 2))
                nc.vector.tensor_copy(stage[:, w % 2, 512:1024], yb[2 * (w % 2) + 1][0:Q, :]).then_inc(y_right, 1)


def count_edges(nc, m):
    with ExitStack() as ctx:
        sb, sem, bank = scope(nc, ctx)
        zeros = sb("zeros_b", [P, 512], BF16)
        lo, hi = sb("lo_hot", [P, 2, G, ROWLO], BF16), sb("hi_hot", [P, 2, G, ROWHI], BF16)
        dl, dw = sb("dl_hot", [P, 2, G, Q], BF16), sb("dw_hot", [P, 2, G, W], BF16)
        part = sb("part", [P, ROWHI])
        deg_std = sb("deg_std", [Q, W])
        rows, degs = bank("rows_count"), bank("dst_count")
        start, hots, counted, done = sem("start"), sem("hots"), sem("counted"), sem("all_counted")
        chain, deg_ready, std_ready = sem("count_chain"), sem("deg_ready"), sem("deg_std_ready")
        block = ctx.enter_context(nc.Block())

        @block.tensor
        def _(pe):
            mm = nc.tensor.matmul
            pe.wait_ge(start, 1)
            mm(rows[:, 0:ROWHI], zeros[:, 0:P], zeros[:, 0:ROWHI], start=True, stop=False)
            mm(degs[0:Q, 0:W], zeros[:, 0:Q], zeros[:, 0:W], start=True, stop=False)
            with pe.Fori(0, TILES // (2 * G)) as i:
                for b in range(2):
                    pe.wait_ge(hots, 2 * i + (b + 1))
                    for j in range(G):
                        mm(rows[:, 0:ROWHI], lo[:, b, j, :], hi[:, b, j, :], start=False, stop=False)
                        last = mm(degs[0:Q, 0:W], dl[:, b, j, :], dw[:, b, j, :], start=False, stop=False)
                    last.then_inc(counted, 1)
            mm(rows[:, 0:ROWHI], zeros[:, 0:P], zeros[:, 0:ROWHI], start=False, stop=True)
            mm(degs[0:Q, 0:W], zeros[:, 0:Q], zeros[:, 0:W], start=False, stop=True).then_inc(done, 1)

        @block.scalar
        def _(act):
            act.wait_ge(deg_ready, 1)
            nc.scalar.activation(deg_std[:, :], m.deg_inv[:, :], ACT.Sqrt).then_inc(std_ready, 1)

        @block.vector
        def _(dve):
            v, count = nc.vector, [0]

            def link(op):
                count[0] += 1
                op.then_inc(chain, 1)
                dve.wait_ge(chain, count[0])

            link(v.memset(zeros[:, :], 0.0))
            dve.sem_inc(start, 1)
            dve.sem_inc(counted, 2)
            with dve.Fori(0, TILES // (2 * G)) as i:
                for b in range(2):
                    dve.wait_ge(counted, 2 * i + (b + 1))
                    for hot, col, n in ((lo, m.row_lo, ROWLO), (hi, m.row_hi, ROWHI), (dl, m.dst_loc, Q), (dw, m.dst_win, W)):
                        last = v.tensor_tensor(hot[:, b, :, :], bc_last(col[:, bass.ds(i * (2 * G) + b * G, G)], n),
                                               bc_mid(m.iota_b[:, 0:n], G), ALU.is_equal)
                    last.then_inc(hots, 1)
            dve.wait_ge(done, 1)
            link(v.tensor_scalar(part[:, :], rows[:, 0:ROWHI], 1.0, None, ALU.max))
            link(v.reciprocal(part[:, :], part[:, :]))
            for k in range(3):
                link(v.tensor_copy(m.row_inv[:, k, :], part[:, :]))
                if k < 2:
                    link(v.tensor_tensor(part[:, :], part[:, :], m.row_inv[:, k, :], ALU.subtract))
            link(v.tensor_scalar(m.deg_inv[:, :], degs[0:Q, 0:W], 1.0, None, ALU.add))
            dve.sem_inc(deg_ready, 1)
            dve.wait_ge(std_ready, 1)
            link(v.reciprocal(m.deg_inv[:, :], m.deg_inv[:, :]))
            link(v.reciprocal(m.deg_rsqrt[:, :], deg_std[:, :]))


def relation_edges(nc, m, y_table, tables):
    with ExitStack() as ctx:
        sb, sem, bank = scope(nc, ctx)
        y_idx, s_idx = sb("y_idx", [P, 2, G], U32), sb("s_idx", [P, 2, G], U32)
        src = sb("src_slot", [P, 2, G])
        got = sb("y_got", [P, 2, G, D])
        same = sb("same_src", [P, 2, G, P])
        before = sb("before", [P, G, P])
        lo, hi = sb("lo1", [P, 2, G, ROWLO], BF16), sb("hi1", [P, 2, G, ROWHI], BF16)
        lot = sb("lot", [P, 2, G, P], BF16)
        looked = sb("looked", [P, G, ROWHI])
        inv = sb("inv_e", [P, 2, G])
        msg, total = sb("msg0", [P, 2, G, D]), sb("total", [P, 2, G, D])
        zrow = sb("zrow", [P, D])
        dup, shift, dump = sb("dup", [P, G]), sb("shift", [P, G]), sb("dump_row", [P, 1])
        src_t, lo_t, sums = bank("src_t"), bank("lo_t", (P, G, P), BF16), bank("sums")
        inv_b = [bank("inv_b0"), bank("inv_b1")]
        copied, src_ready, turned, same_ready, lot_ready = (sem(n) for n in (
            "idx_copied", "src_ready", "turned0", "same_ready", "lot_ready"))
        inv_found, inv_ready, msg_ready, sums_ready, tot_ready, s_ready = (sem(n) for n in (
            "inv_found", "inv_ready", "msg_ready", "sums_ready", "tot_ready", "s_ready"))
        tick, chain, dump_ready = sem("pool_tick"), sem("chain0"), sem("dump_ready")
        y_in = m.come.pop()
        steps = TILES // (2 * G)
        K = 22
        block = ctx.enter_context(nc.Block())

        @block.gpsimd
        def _(pool):
            pool.memset(zrow[:, :], 0.0).then_inc(tick, 1)
            pool.wait_ge(tick, 1)
            for a, b in ((0, ACCROWS // P // 2), (ACCROWS // P // 2, ACCROWS // P)):
                for j in range(G):
                    if a:
                        pool.wait_ge(m.added[j], 16)
                    pool.dma_start(tables[j].rearrange("(a p) d -> p a d", p=P)[:, a:b, :],
                                   bc_mid(zrow[:, :], b - a)).then_inc(m.added[j], 16)

            def gather(b):
                for j in range(G):
                    pool.indirect_dma_start(out=got[:, b, j, :], out_offset=None, in_=y_table[:, :],
                                            in_offset=bass.IndirectOffsetOnAxis(ap=y_idx[:, b, j:j + 1], axis=0)
                                            ).then_inc(y_in[b], 16)

            for b in range(2):
                pool.wait_ge(copied, b + 1)
                gather(b)
            with pool.Fori(0, steps) as i:
                for b in range(2):
                    g = 2 * i + b
                    pool.wait_ge(s_ready, g + 1).then_inc(tick, 1)
                    pool.wait_ge(tot_ready, g + 3).then_inc(tick, 1)
                    for j in range(G):
                        pool.wait_ge(m.added[j], 16 * g + 32).then_inc(tick, 1)
                        pool.indirect_dma_start(out=tables[j][:, :],
                                                out_offset=bass.IndirectOffsetOnAxis(ap=s_idx[:, b, j:j + 1], axis=0),
                                                in_=total[:, b, j, :], in_offset=None,
                                                compute_op=ALU.add).then_inc(m.added[j], 16)
                    pool.wait_ge(copied, g + 3).then_inc(tick, 1)
                    pool.wait_ge(msg_ready, g + 1).then_inc(tick, 1)
                    gather(b)
            for j in range(G):
                pool.wait_ge(m.added[j], 16 * (2 * steps) + 32)
            for b in range(2):
                pool.wait_ge(y_in[b], 16 * G * (steps + 1))

        @block.vector
        def _(dve):
            v, n = nc.vector, [0]
            dve.sem_inc(same_ready, 1)
            dve.sem_inc(inv_ready, 1)
            v.tensor_scalar(dump[:, :], m.lane[:, :], float(DUMP), None, ALU.add).then_inc(dump_ready, 1)
            v.tensor_copy(y_idx[:, 0, :], m.y_row[:, 0:G]).then_inc(copied, 1)
            v.tensor_copy(y_idx[:, 1, :], m.y_row[:, G:2 * G]).then_inc(copied, 1)
            dve.wait_ge(dump_ready, 1)
            with dve.Fori(0, steps) as i:
                def link(op):
                    n[0] += 1
                    op.then_inc(chain, 1)
                    dve.wait_ge(chain, K * i + n[0])

                for b in range(2):
                    g, at = 2 * i + b, i * (2 * G) + b * G
                    dve.wait_ge(tot_ready, g + 1)
                    link(v.tensor_copy(src[:, b, :], m.src_lane[:, bass.ds(at, G)]))
                    v.tensor_tensor(lo[:, b, :, :], bc_last(m.row_lo[:, bass.ds(at, G)], ROWLO),
                                    bc_mid(m.iota_b[:, 0:ROWLO], G), ALU.is_equal).then_inc(src_ready, 1)
                    link(v.tensor_tensor(hi[:, b, :, :], bc_last(m.row_hi[:, bass.ds(at, G)], ROWHI),
                                         bc_mid(m.iota_b[:, 0:ROWHI], G), ALU.is_equal))
                    dve.wait_ge(turned, g + 1)
                    link(v.tensor_tensor(same[:, b, :, :], src_t[:, :].rearrange("p (j e) -> p j e", j=G),
                                         bc_last(src[:, b, :], P), ALU.is_equal))
                    dve.sem_inc(same_ready, 1)
                    link(v.tensor_tensor(before[:, :, :], same[:, b, :, :], bc_mid(m.rows_before[:, :], G), ALU.mult))
                    link(v.reduce_sum(dup[:, :], before[:, :, :], AX))
                    link(v.tensor_scalar(dup[:, :], dup[:, :], 1.0, None, ALU.min))
                    link(v.tensor_scalar(shift[:, :], src[:, b, :], -1.0, dump[:, 0:1], ALU.mult, ALU.add))
                    link(v.tensor_tensor(shift[:, :], shift[:, :], dup[:, :], ALU.mult))
                    for j in range(G):
                        dve.wait_ge(m.added[j], 16 * g + 16)
                    link(v.tensor_tensor(s_idx[:, b, :], shift[:, :], src[:, b, :], ALU.add))
                    dve.sem_inc(s_ready, 1)
                    dve.wait_ge(inv_found, g + 1)
                    for k in range(2):
                        op = v.tensor_tensor(looked[:, 2 * k:2 * k + 2, :],
                                             inv_b[k][:, 0:2 * ROWHI].rearrange("p (j e) -> p j e", j=2),
                                             hi[:, b, 2 * k:2 * k + 2, :], ALU.mult)
                        if k:
                            link(op)
                    v.reduce_sum(inv[:, b, :], looked[:, :, :], AX).then_inc(inv_ready, 1)
                    dve.wait_ge(y_in[b], 64 * i + 64)
                    link(v.tensor_copy(y_idx[:, b, :], m.y_row[:, bass.ds(at + 2 * G, G)]))
                    dve.sem_inc(copied, 1)
                assert n[0] == K, n[0]

        @block.tensor
        def _(pe):
            t = nc.tensor
            with pe.Fori(0, steps) as i:
                for b in range(2):
                    g = 2 * i + b
                    pe.wait_ge(src_ready, g + 1)
                    pe.wait_ge(same_ready, g + 1)
                    pe.wait_ge(lot_ready, g + 1)
                    for j in range(G):
                        t.transpose(src_t[:, j * P:(j + 1) * P], src[:, b, j:j + 1].broadcast_to([P, P]), m.ident[:, :])
                    for j in range(G):
                        last = t.transpose(lo_t[:, j, :], lo[:, b, j, :], m.ident_b[:, :])
                    last.then_inc(turned, 1)
                    pe.wait_ge(lot_ready, g + 2)
                    pe.wait_ge(inv_ready, g + 1)
                    for j in range(G):
                        out = inv_b[j // 2][:, (j % 2) * ROWHI:(j % 2 + 1) * ROWHI]
                        for k in range(3):
                            last = t.matmul(out, lot[:, b, j, :], m.row_inv[:, k, :], start=(k == 0), stop=(k == 2))
                    last.then_inc(inv_found, 1)
                    pe.wait_ge(msg_ready, g + 1)
                    pe.wait_ge(tot_ready, g + 2)
                    for j in range(G):
                        last = t.matmul(sums[:, j * D:(j + 1) * D], same[:, b, j, :], msg[:, b, j, :], start=True, stop=True)
                    last.then_inc(sums_ready, 1)

        @block.scalar
        def _(act):
            s = nc.scalar
            act.sem_inc(lot_ready, 1)
            act.sem_inc(tot_ready, 2)
            with act.Fori(0, steps) as i:
                for b in range(2):
                    g = 2 * i + b
                    act.wait_ge(turned, g + 1)
                    s.copy(lot[:, b, :, :], lo_t[:, :, :]).then_inc(lot_ready, 1)
                    act.wait_ge(inv_ready, g + 2)
                    act.wait_ge(y_in[b], 64 * i + 64)
                    for j in range(G):
                        last = s.activation(msg[:, b, j, :], got[:, b, j, :], ACT.Copy, scale=inv[:, b, j:j + 1])
                    last.then_inc(msg_ready, 1)
                    act.wait_ge(sums_ready, g + 1)
                    for j in range(G):
                        act.wait_ge(m.added[j], 16 * g + 16)
                    s.copy(total[:, b, :, :].rearrange("p j d -> p (j d)"), sums[:, :]).then_inc(tot_ready, 1)


def make_link(dve, chain):
    count = [0]

    def link(op):
        count[0] += 1
        op.then_inc(chain, 1)
        dve.wait_ge(chain, count[0])
    return link


def gcn_nodes(nc, m, ins, tables, t_table):
    with ExitStack() as ctx:
        sb, sem, bank = scope(nc, ctx)
        part, tmp, stats = sb("part1", [Q, G, W, D]), sb("tmp1", [Q, W, D]), sb("stats1", [Q, 2, W])
        w1 = sb("gcn_w", [D, D])
        xt = sb("xt1", [P, W, Q])
        tb, hb = [bank(f"t1{i}") for i in range(2)], [bank(f"h1{i}") for i in range(2)]
        loaded, chain, var_ready, std_ready, x_ready = (sem(n) for n in ("loaded1", "chain1", "var1", "std1", "x1_ready"))
        turned, copied, h_done, h_read, t_ready, stored = (sem(n) for n in ("t1", "c1", "h_done", "h_read", "t_ready", "st1"))
        block = ctx.enter_context(nc.Block())

        @block.sync
        def _(sp):
            for j in range(G):
                sp.dma_start(part[:, j, :, :], nodes(tables[j][0:N, :])).then_inc(loaded, 16)
            sp.dma_start(w1[:, :], ins["L1_gnn_W"]).then_inc(loaded, 16)
            sp.wait_ge(t_ready, 1)
            sp.dma_start(nodes(t_table), tmp[:, :, :]).then_inc(stored, 16)
            sp.wait_ge(stored, 16)

        @block.vector
        def _(dve):
            v, link = nc.vector, make_link(dve, chain)
            dve.wait_ge(loaded, 16 * (G + 1))
            link(v.tensor_tensor(part[:, 0, :, :], part[:, 0, :, :], part[:, 1, :, :], ALU.add))
            link(v.tensor_tensor(part[:, 2, :, :], part[:, 2, :, :], part[:, 3, :, :], ALU.add))
            link(v.tensor_tensor(part[:, 0, :, :], part[:, 0, :, :], part[:, 2, :, :], ALU.add))
            link(v.scalar_tensor_tensor(tmp[:, :, :], part[:, 0, :, :], 0.0, m.x[:, :, :], ALU.max, ALU.add))
            layer_norm(nc, dve, link, tmp[:, :, :], m.x[:, :, :], part[:, 0, :, :], stats, EPS, var_ready, std_ready, 1)
            dve.sem_inc(x_ready, 1)
            for w in range(W):
                dve.wait_ge(h_done, w + 1)
                v.tensor_copy(m.h[:, w, :], hb[w % 2][0:Q, 0:D]).then_inc(h_read, 1)
            dve.wait_ge(h_read, W)
            link(v.tensor_tensor(tmp[:, :, :], m.h[:, :, :], bc_last(m.deg_rsqrt[:, :], D), ALU.mult))
            dve.sem_inc(t_ready, 1)

        @block.scalar
        def _(act):
            std_of(nc, act, stats, var_ready, std_ready, 1)
            turn_windows_act(nc, act, m, xt, tb, turned, copied)

        @block.tensor
        def _(pe):
            pe.wait_ge(x_ready, 1)
            turn_windows_pe(nc, pe, m, m.x, tb, turned, copied)
            pe.wait_ge(copied, TG)
            pe.wait_ge(loaded, 16 * (G + 1))
            for w in range(W):
                if w >= 2:
                    pe.wait_ge(h_read, w - 1)
                nc.tensor.matmul(hb[w % 2][0:Q, 0:D], xt[:, w, :], w1[:, :], start=True, stop=True).then_inc(h_done, 1)


STEPS = PAIRS // (2 * G)
WG = 2 * G


def windows(nc, m, engine, at, n):
    _, values = nc.values_load_multi_w_load_instructions(
        m.pair_win_i[0:1, bass.ds(at, n)], engines=[engine], min_val=0, max_val=W - 1, skip_runtime_bounds_check_because="a pair's window is a count of 24 comparisons")
    return values


class PairLoop:

    def __init__(self, nc, m, ctx, table, width=D, hot_dt=F32):
        sb, sem, bank = scope(nc, ctx)
        self.nc, self.m, self.table = nc, m, table
        self.idx = sb("idx", [P, 2, G], U32)
        self.got = sb("got", [P, 2, G, width])
        self.hot = sb("hot", [P, 2, G, Q], hot_dt)
        self.copied, self.hot_ready, self.tick = sem("idx_copied"), sem("hot_ready"), sem("pool_tick")
        self.come = m.come.pop()

    def gathers(self, pool, wait_free):
        def gather(b):
            for j in range(G):
                pool.indirect_dma_start(out=self.got[:, b, j, :], out_offset=None, in_=self.table[:, :],
                                        in_offset=bass.IndirectOffsetOnAxis(ap=self.idx[:, b, j:j + 1], axis=0)
                                        ).then_inc(self.come[b], 16)

        for b in range(2):
            pool.wait_ge(self.copied, b + 1)
            gather(b)
        with pool.Fori(0, STEPS) as i:
            for b in range(2):
                g = 2 * i + b
                pool.wait_ge(self.copied, g + 3).then_inc(self.tick, 1)
                wait_free(i, b, g)
                gather(b)
        for b in range(2):
            pool.wait_ge(self.come[b], 16 * G * (STEPS + 1))

    def first_rows(self, dve):
        for b in range(2):
            self.nc.vector.tensor_copy(self.idx[:, b, :], self.m.pair_src[:, b * G:(b + 1) * G]).then_inc(self.copied, 1)

    def one_hots(self, at, b):
        v, m = self.nc.vector, self.m
        cols = slice(at, at + G) if isinstance(at, int) else bass.ds(at, G)
        v.tensor_tensor(self.hot[:, b, :, :], bc_last(m.pair_dst[:, cols], Q), bc_mid(m.iota[:, 0:Q], G),
                        ALU.is_equal).then_inc(self.hot_ready, 1)

    def next_rows(self, dve, at, b, seen):
        cols = slice(at, at + G) if isinstance(at, int) else bass.ds(at, G)
        dve.wait_ge(self.come[b], 64 * seen)
        self.nc.vector.tensor_copy(self.idx[:, b, :], self.m.pair_src[:, cols]).then_inc(self.copied, 1)


def clear_banks(t, zeros, sums, stop):
    for k in range(8):
        last = t.matmul(sums[0:Q, k * 512:(k + 1) * 512], zeros[:, 0:Q], zeros[:, :], start=not stop, stop=stop)
    return last


def gcn_sums(nc, m, table):
    with ExitStack() as ctx:
        sb, sem, bank = scope(nc, ctx)
        loop = PairLoop(nc, m, ctx, table)
        zeros = sb("zeros", [P, 512], BF16)
        sums = bank("sums", (P, 8 * 512))
        used, zeroed, done, agg_ready = sem("used"), sem("zeroed"), sem("all_summed"), sem("agg_ready")
        block = ctx.enter_context(nc.Block())

        @block.gpsimd
        def _(pool):
            loop.gathers(pool, lambda i, b, g: pool.wait_ge(used, g + 1).then_inc(loop.tick, 1))

        @block.vector
        def _(dve):
            nc.vector.memset(zeros[:, :], 0.0).then_inc(zeroed, 1)
            loop.first_rows(dve)
            for b in range(2):
                loop.one_hots(b * G, b)
            with dve.Fori(0, STEPS) as i:
                for b in range(2):
                    g, at = 2 * i + b, i * (2 * G) + b * G
                    loop.next_rows(dve, at + 2 * G, b, i + 1)
                    dve.wait_ge(used, g + 1)
                    loop.one_hots(at + 2 * G, b)
            dve.wait_ge(done, 1)
            nc.vector.tensor_copy(m.agg[:, :, :].rearrange("q w d -> q (w d)"), sums[0:Q, 0:W * D])

        @block.tensor
        def _(pe):
            t = nc.tensor
            pe.wait_ge(zeroed, 1)
            clear_banks(t, zeros, sums, False)
            with pe.Fori(0, STEPS) as i:
                for b in range(2):
                    g, at = 2 * i + b, i * (2 * G) + b * G
                    ws = windows(nc, m, ENG.PE, at, G)
                    pe.wait_ge(loop.hot_ready, g + 1)
                    pe.wait_ge(loop.come[b], 64 * i + 64)
                    for j in range(G):
                        last = t.matmul(sums[0:Q, bass.ds(ws[j] * D, D)], loop.hot[:, b, j, :], loop.got[:, b, j, :],
                                        start=False, stop=False)
                    last.then_inc(used, 1)
            clear_banks(t, zeros, sums, True).then_inc(done, 1)


def conv_sums(nc, m, v_rows):
    with ExitStack() as ctx:
        sb, sem, bank = scope(nc, ctx)
        zeros = sb("zeros", [P, 512], BF16)
        rows = sb("rows", [P, 2, WG, D])
        hot = sb("hot", [P, 2, WG, Q])
        msg = sb("msg", [P, 2, WG, D])
        wts = sb("wts", [P, 2, WG, H])
        sums = bank("sums", (P, 8 * 512))
        dens = 7 * 512
        used, zeroed, done, hot_ready, wts_ready, msg_ready = (sem(n) for n in (
            "used", "zeroed", "all_summed", "hot_ready", "wts_ready", "msg_ready"))
        come = [sem("come0"), sem("come1")]
        steps = PAIRS // (2 * WG)
        block = ctx.enter_context(nc.Block())

        @block.sync
        def _(sp):
            with sp.Fori(0, steps) as i:
                for b in range(2):
                    sp.wait_ge(msg_ready, 2 * i + (b + 1))
                    sp.dma_start(rows[:, b, :, :].rearrange("l (a j) d -> l a (j d)", a=2),
                                 v_rows[bass.ds(i * 4 + 2 * b, 2), :, :].rearrange("a l n -> l a n")).then_inc(come[b], 16)

        @block.vector
        def _(dve):
            v = nc.vector
            v.memset(zeros[:, :], 0.0).then_inc(zeroed, 1)
            dve.sem_inc(msg_ready, 2)
            with dve.Fori(0, steps) as i:
                for b in range(2):
                    g, cols = 2 * i + b, bass.ds(i * (2 * WG) + b * WG, WG)
                    dve.wait_ge(used, g + 1)
                    v.tensor_copy(wts[:, b, :, :], m.small[:, cols, 0:H]).then_inc(wts_ready, 1)
                    v.tensor_tensor(hot[:, b, :, :], bc_last(m.pair_dst[:, cols], Q), bc_mid(m.iota[:, 0:Q], WG),
                                    ALU.is_equal).then_inc(hot_ready, 1)
                    dve.wait_ge(wts_ready, g + 1)
                    dve.wait_ge(come[b], 16 * i + 16)
                    v.tensor_tensor(msg[:, b, :, :].rearrange("p j (h c) -> p (j h) c", h=H),
                                    rows[:, b, :, :].rearrange("p j (h c) -> p (j h) c", h=H),
                                    bc_last(wts[:, b, :, :].rearrange("p j h -> p (j h)"), C), ALU.mult).then_inc(msg_ready, 1)
            dve.wait_ge(done, 1)
            v.tensor_copy(m.sums[:, :, :].rearrange("q w d -> q (w d)"), sums[0:Q, 0:W * D])
            v.tensor_copy(m.dens[:, :, :].rearrange("q w h -> q (w h)"), sums[0:Q, dens:dens + W * H])

        @block.tensor
        def _(pe):
            t = nc.tensor
            pe.sem_inc(used, 2)
            pe.wait_ge(zeroed, 1)
            clear_banks(t, zeros, sums, False)
            with pe.Fori(0, steps) as i:
                for b in range(2):
                    g, at = 2 * i + b, i * (2 * WG) + b * WG
                    ws = windows(nc, m, ENG.PE, at, WG)
                    pe.wait_ge(hot_ready, g + 1)
                    pe.wait_ge(msg_ready, g + 3)
                    for j in range(WG):
                        t.matmul(sums[0:Q, bass.ds(ws[j] * D, D)], hot[:, b, j, :], msg[:, b, j, :], start=False, stop=False)
                        last = t.matmul(sums[0:Q, bass.ds(ws[j] * H + dens, H)], hot[:, b, j, :], wts[:, b, j, :],
                                        start=False, stop=False)
                    last.then_inc(used, 1)
            clear_banks(t, zeros, sums, True).then_inc(done, 1)


def gat_sums(nc, m, table):
    with ExitStack() as ctx:
        sb, sem, bank = scope(nc, ctx)
        loop = PairLoop(nc, m, ctx, table)
        got, hot = loop.got, loop.hot
        wts = sb("wts", [P, 2, G, 2 * H])
        msg = sb("msg", [P, 2, G, H * D])
        sums = [bank(f"sums{j}") for j in range(G)]
        tails = [bank(f"tails{j}") for j in range(G)]
        wts_ready, msg_ready, act_ready, summed, read, chain = (sem(n) for n in (
            "wts_ready", "msg_ready", "act_msg", "summed", "sums_read", "chain"))
        block = ctx.enter_context(nc.Block())

        @block.gpsimd
        def _(pool):
            def wait_free(i, b, g):
                pool.wait_ge(msg_ready, g + 1).then_inc(loop.tick, 1)
                pool.wait_ge(act_ready, g + 1).then_inc(loop.tick, 1)

            loop.gathers(pool, wait_free)

        @block.vector
        def _(dve):
            v = nc.vector
            dve.sem_inc(read, G)
            loop.first_rows(dve)

            def produce(at, b, g, seen):
                dve.wait_ge(summed, 4 * g + 4)
                cols = slice(at, at + G) if isinstance(at, int) else bass.ds(at, G)
                v.tensor_copy(wts[:, b, :, :], m.small[:, cols, :]).then_inc(wts_ready, 1)
                loop.one_hots(at, b)
                loop.next_rows(dve, at + 2 * G, b, seen)
                dve.wait_ge(wts_ready, g + 1)
                v.tensor_tensor(msg[:, b, :, 0:D], got[:, b, :, :], wts[:, b, :, 0:1].broadcast_to([P, G, D]),
                                ALU.mult).then_inc(msg_ready, 1)

            produce(0, 0, 0, 1)
            with dve.Fori(0, STEPS) as i:
                for b in range(2):
                    g, at = 2 * i + b, i * (2 * G) + b * G
                    ws = windows(nc, m, ENG.DVE, at, G)
                    produce(at + G, 1 - b, g + 1, i + 1 + b)
                    for j in range(G):
                        row = m.acc[:, bass.ds(ws[j], 1), :].rearrange("q o d -> q (o d)")
                        dve.wait_ge(summed, 4 * g + (j + 9))
                        dve.wait_ge(read, 4 * g + (j + 4))
                        v.tensor_tensor(row[:, H * D:], row[:, H * D:], tails[j][0:Q, 0:2 * H], ALU.add)
                        v.tensor_tensor(row[:, 0:H * D], row[:, 0:H * D], sums[j][0:Q, :], ALU.add).then_inc(read, 1)

        @block.scalar
        def _(act):
            with act.Fori(0, STEPS) as i:
                for b in range(2):
                    g = 2 * i + b
                    act.wait_ge(wts_ready, g + 1)
                    act.wait_ge(loop.come[b], 64 * i + 64)
                    for j in range(G):
                        for h in range(1, H):
                            last = nc.scalar.activation(msg[:, b, j, h * D:(h + 1) * D], got[:, b, j, :], ACT.Copy,
                                                        scale=wts[:, b, j, h:h + 1])
                    last.then_inc(act_ready, 1)

        @block.tensor
        def _(pe):
            pe.sem_inc(summed, 2 * G)
            t = nc.tensor
            with pe.Fori(0, STEPS) as i:
                for b in range(2):
                    g = 2 * i + b
                    pe.wait_ge(loop.hot_ready, g + 1)
                    pe.wait_ge(msg_ready, g + 1)
                    pe.wait_ge(act_ready, g + 1)
                    for j in range(G):
                        pe.wait_ge(read, 4 * g + (j + 1))
                        t.matmul(sums[j][0:Q, :], hot[:, b, j, :], msg[:, b, j, :], start=True, stop=True)
                        t.matmul(tails[j][0:Q, 0:2 * H], hot[:, b, j, :], wts[:, b, j, :],
                                 start=True, stop=True).then_inc(summed, 1)


def batch_norm(nc, m, ins, x_table):
    with ExitStack() as ctx:
        sb, sem, bank = scope(nc, ctx)
        o, sq, stats = sb("gcn_out", [Q, W, D]), sb("gcn_sq", [Q, W, D]), sb("stats2", [Q, 2, W])
        vec = sb("gcn_vec", [P, 3, D])
        mean, rstd = sb("bn_mean", [Q, D]), sb("bn_rstd", [Q, D])
        ones = sb("ones_q", [Q, Q])
        sums = [bank("bn_sum"), bank("bn_sq")]
        loaded, chain, ready, summed, var_ready, std_ready, out_ready, stored = (sem(n) for n in (
            "loaded2", "chain2", "bn_ready", "bn_summed", "var2", "std2", "x2_ready", "stored2"))
        block = ctx.enter_context(nc.Block())

        @block.sync
        def _(sp):
            for k, name in enumerate(("L1_gnn_b", "L1_gnn_gamma", "L1_gnn_beta")):
                sp.dma_start(vec[:, k, :], row_bc(ins[name], P)).then_inc(loaded, 16)
            sp.wait_ge(out_ready, 1)
            sp.dma_start(nodes(x_table), m.x[:, :, :]).then_inc(stored, 16)
            sp.wait_ge(stored, 16)

        @block.tensor
        def _(pe):
            for k, a in enumerate((o, sq)):
                pe.wait_ge(ready, k + 1)
                for w in range(W):
                    last = nc.tensor.matmul(sums[k][0:Q, 0:D], ones[:, :], a[:, w, :], start=(w == 0), stop=(w == W - 1))
                last.then_inc(summed, 1)

        @block.scalar
        def _(act):
            act.wait_ge(var_ready, 1)
            nc.scalar.activation(rstd[:, :], rstd[:, :], ACT.Sqrt).then_inc(std_ready, 1)
            std_of(nc, act, stats, var_ready, std_ready, 2)

        @block.vector
        def _(dve):
            v, link = nc.vector, make_link(dve, chain)
            link(v.memset(ones[:, :], 1.0))
            dve.wait_ge(loaded, 48)
            link(v.tensor_tensor(o[:, :, :], m.agg[:, :, :], bc_last(m.deg_rsqrt[:, :], D), ALU.mult))
            link(v.tensor_tensor(sq[:, :, :], m.h[:, :, :], bc_last(m.deg_inv[:, :], D), ALU.mult))
            link(v.tensor_tensor(o[:, :, :], o[:, :, :], sq[:, :, :], ALU.add))
            link(v.tensor_tensor(o[:, :, :], o[:, :, :], bc_mid(vec[0:Q, 0, :], W), ALU.add))
            link(v.scalar_tensor_tensor(o[:, :, :], o[:, :, :], 0.01, o[:, :, :], ALU.mult, ALU.max))
            dve.sem_inc(ready, 1)
            dve.wait_ge(summed, 1)
            link(v.tensor_scalar(mean[:, :], sums[0][0:Q, 0:D], 1.0 / N, None, ALU.mult))
            link(v.tensor_tensor(o[:, :, :], o[:, :, :], bc_mid(mean[:, :], W), ALU.subtract))
            link(v.tensor_tensor(sq[:, :, :], o[:, :, :], o[:, :, :], ALU.mult))
            dve.sem_inc(ready, 1)
            dve.wait_ge(summed, 2)
            v.tensor_scalar(rstd[:, :], sums[1][0:Q, 0:D], 1.0 / N, EPS, ALU.mult, ALU.add).then_inc(var_ready, 1)
            dve.wait_ge(std_ready, 1)
            link(v.reciprocal(rstd[:, :], rstd[:, :]))
            link(v.tensor_tensor(rstd[:, :], rstd[:, :], vec[0:Q, 1, :], ALU.mult))
            link(v.tensor_tensor(o[:, :, :], o[:, :, :], bc_mid(rstd[:, :], W), ALU.mult))
            link(v.tensor_tensor(o[:, :, :], o[:, :, :], bc_mid(vec[0:Q, 2, :], W), ALU.add))
            link(v.tensor_tensor(o[:, :, :], o[:, :, :], m.x[:, :, :], ALU.add))
            layer_norm(nc, dve, link, o[:, :, :], m.x[:, :, :], sq[:, :, :], stats, EPS, var_ready, std_ready, 2)
            dve.sem_inc(out_ready, 1)


def clear(nc, acc):
    with nc.Block() as block:
        @block.gpsimd
        def _(pool):
            pool.memset(acc, 0.0)


def gat_nodes(nc, m, ins):
    with ExitStack() as ctx:
        sb, sem, bank = scope(nc, ctx)
        wr, bias, two = sb("w_r", [D, H * D]), sb("bias_lr", [P, 2, H * D]), sb("z_self", [Q, 2, H * D])
        wide = sb("wide", [P, H * D])
        xt = sb("xt3", [P, W, Q])
        tb = [bank(f"g_t{i}") for i in range(2)]
        lb, rb = [bank(f"g_l{i}") for i in range(2)], [bank(f"g_r{i}") for i in range(2)]
        loaded, turned, copied, done, zed, chain = (sem(n) for n in ("loaded3", "t3", "c3", "lr_done", "z_ready", "chain3"))
        block = ctx.enter_context(nc.Block())

        @block.sync
        def _(sp):
            sp.dma_start(wr[:, :], ins["L2_gnn_W_r"]).then_inc(loaded, 16)
            sp.dma_start(m.gat_wl[:, :], ins["L2_gnn_W_l"]).then_inc(loaded, 16)
            sp.dma_start(m.att[:, :], row_bc(ins["L2_gnn_att"].rearrange("h d -> (h d)"), P)).then_inc(loaded, 16)
            for k, name in enumerate(("L2_gnn_b_l", "L2_gnn_b_r")):
                sp.dma_start(bias[:, k, :], row_bc(ins[name], P)).then_inc(loaded, 16)
            sp.wait_ge(loaded, 80)

        @block.tensor
        def _(pe):
            turn_windows_pe(nc, pe, m, m.x, tb, turned, copied)
            pe.wait_ge(copied, TG)
            pe.wait_ge(loaded, 80)
            for w in range(W):
                if w >= 2:
                    pe.wait_ge(zed, w - 1)
                nc.tensor.matmul(lb[w % 2][0:Q, :], xt[:, w, :], m.gat_wl[:, :], start=True, stop=True)
                nc.tensor.matmul(rb[w % 2][0:Q, :], xt[:, w, :], wr[:, :], start=True, stop=True).then_inc(done, 1)

        @block.scalar
        def _(act):
            turn_windows_act(nc, act, m, xt, tb, turned, copied)

        @block.vector
        def _(dve):
            v, link = nc.vector, make_link(dve, chain)
            dve.wait_ge(loaded, 80)
            link(v.tensor_tensor(bias[:, 0, :], bias[:, 0, :], bias[:, 1, :], ALU.add))


            def dot(dst, a, part, rows):
                link(v.tensor_tensor(part, a, m.att[0:rows, :], ALU.mult))
                link(v.reduce_sum(dst, part.rearrange("q (h d) -> q h d", h=H), AX))

            dot(m.wl_att[:, :], m.gat_wl[:, :], wide[:, :], D)
            link(v.tensor_scalar(m.wl_att[:, :], m.wl_att[:, :], 0.2, None, ALU.mult))
            for w in range(W):
                dve.wait_ge(done, w + 1)
                link(v.tensor_tensor(m.acc[:, w, 0:H * D], rb[w % 2][0:Q, :], bias[0:Q, 0, :], ALU.add))
                z = two[:, w % 2, :]
                v.tensor_tensor(z, lb[w % 2][0:Q, :], m.acc[:, w, 0:H * D], ALU.add).then_inc(zed, 1)
                dot(m.acc[:, w, H * D:H * D + H], m.acc[:, w, 0:H * D], wide[0:Q, :], Q)
                dve.wait_ge(zed, w + 1)
                link(v.scalar_tensor_tensor(z, z, 0.2, z, ALU.mult, ALU.max))
                dot(m.self_score[:, w, :], z, wide[0:Q, :], Q)
            link(v.tensor_scalar(m.acc[:, :, H * D:H * D + H], m.acc[:, :, H * D:H * D + H], 0.2, None, ALU.mult))


def gat_scores(nc, m, x_table):
    with ExitStack() as ctx:
        sb, sem, bank = scope(nc, ctx)
        loop = PairLoop(nc, m, ctx, x_table)
        got, hot = loop.got, loop.hot
        got_t, hot_t = sb("got_t", [P, 2, G, P]), sb("hot_t", [Q, 2, G, P])
        leaky = sb("leaky", [P, G, H * D])
        score = sb("score", [P, 2, H, G])
        got_b, hot_b = bank("got_b"), bank("hot_b")
        z = [bank(f"z{j}") for j in range(G)]
        lin = [bank(f"lin{b}", (P, H, G)) for b in range(2)]
        turned, copied_t, z_done, z_read, l_read, out = (sem(n) for n in ("turned", "copied_t", "z_done", "z_read", "l_read", "alpha_out"))
        block = ctx.enter_context(nc.Block())

        @block.gpsimd
        def _(pool):
            loop.gathers(pool, lambda i, b, g: pool.wait_ge(turned, g + 1).then_inc(loop.tick, 1))

        @block.vector
        def _(dve):
            v = nc.vector
            dve.sem_inc(l_read, G)
            dve.sem_inc(out, 2)
            loop.first_rows(dve)
            for b in range(2):
                loop.one_hots(b * G, b)
            with dve.Fori(0, STEPS) as i:
                for b in range(2):
                    g, at = 2 * i + b, i * (2 * G) + b * G
                    loop.next_rows(dve, at + 2 * G, b, i + 1)
                    dve.wait_ge(turned, g + 1)
                    loop.one_hots(at + 2 * G, b)
                    for j in range(G):
                        dve.wait_ge(z_read, 4 * g + (j + 1 + G))
                        for h in range(H):
                            part = leaky[:, j, h * D:(h + 1) * D]
                            last = v.tensor_tensor_reduce(out=part, in0=part,
                                                          in1=m.att[:, h * D:(h + 1) * D], scale=1.0, scalar=0.0,
                                                          op0=ALU.mult, op1=ALU.add, accum_out=score[:, b, h, j:j + 1])
                        last.then_inc(l_read, 1)
                    dve.wait_ge(l_read, 4 * g + 2 * G)
                    v.tensor_tensor(m.alpha[:, :, bass.ds(at, G)], score[:, b, :, :], lin[b][:, :, :], ALU.add).then_inc(out, 1)

        @block.scalar
        def _(act):
            s = nc.scalar
            act.sem_inc(z_read, G)
            act.sem_inc(copied_t, 1)

            def copy(b, g):
                act.wait_ge(turned, g + 1)
                s.copy(got_t[:, b, :, :].rearrange("p j e -> p (j e)"), got_b[:, :])
                s.copy(hot_t[:, b, :, :].rearrange("p j e -> p (j e)"), hot_b[0:Q, :]).then_inc(copied_t, 1)

            copy(0, 0)
            with act.Fori(0, STEPS) as i:
                for b in range(2):
                    g = 2 * i + b
                    copy(1 - b, g + 1)
                    for j in range(G):
                        act.wait_ge(z_done, 4 * g + (j + 1))
                        act.wait_ge(l_read, 4 * g + (j + 1))
                        s.activation(leaky[:, j, :], z[j][:, :], ACT.Relu, scale=0.8).then_inc(z_read, 1)

        @block.tensor
        def _(pe):
            t = nc.tensor

            def turn(b, g, seen):
                pe.wait_ge(loop.hot_ready, g + 1)
                pe.wait_ge(loop.come[b], 64 * seen)
                pe.wait_ge(copied_t, g + 1)
                for j in range(G):
                    t.transpose(got_b[:, j * P:(j + 1) * P], got[:, b, j, :], m.ident[:, :])
                    last = t.transpose(hot_b[0:Q, j * P:(j + 1) * P], hot[:, b, j, :], m.ident[:, :])
                last.then_inc(turned, 1)

            turn(0, 0, 1)
            with pe.Fori(0, STEPS) as i:
                for b in range(2):
                    g, at = 2 * i + b, i * (2 * G) + b * G
                    ws = windows(nc, m, ENG.PE, at, G)
                    turn(1 - b, g + 1, i + 1 + b)
                    pe.wait_ge(copied_t, g + 2)
                    pe.wait_ge(out, g + 1)
                    for j in range(G):
                        pe.wait_ge(z_read, 4 * g + (j + 1))
                        w = ws[j]
                        t.matmul(lin[b][:, :, j], got_t[:, b, j, :], m.wl_att[:, :], start=True, stop=False)
                        t.matmul(lin[b][:, :, j], hot_t[:, b, j, :],
                                 m.acc[:, bass.ds(w, 1), H * D:H * D + H].rearrange("q o d -> q (o d)"), start=False, stop=True)
                        t.matmul(z[j][:, :], got_t[:, b, j, :], m.gat_wl[:, :], start=True, stop=False)
                        last = t.matmul(z[j][:, :], hot_t[:, b, j, :],
                                        m.acc[:, bass.ds(w, 1), 0:H * D].rearrange("q o d -> q (o d)"), start=False, stop=True)
                        last.then_inc(z_done, 1)


def gat_finish(nc, m, ins):
    with ExitStack() as ctx:
        sb, sem, bank = scope(nc, ctx)
        edge, own, inv = (sb(n, [Q, W, H]) for n in ("edge_w", "self_w", "inv_w"))
        tmp, stats = sb("tmp5", [Q, W, D]), sb("stats5", [Q, 2, W])
        vec = sb("vec5", [P, 3, D])
        bl = sb("bl5", [P, H * D])
        at = sb("agg_t", [P, 2, H, Q])
        tb, ob = [bank(f"a_t{i}") for i in range(2)], [bank(f"a_o{i}") for i in range(2)]
        loaded, chain, shifted, exped, ready, turned, copied, done, read, var_ready, std_ready = (sem(n) for n in (
            "loaded5", "chain5", "shifted5", "exped5", "ready5", "t5", "c5", "o5", "r5", "var5", "std5"))
        block = ctx.enter_context(nc.Block())

        @block.sync
        def _(sp):
            for k, name in enumerate(("L2_gnn_gat_bias", "L2_gnn_ln_g", "L2_gnn_ln_b")):
                sp.dma_start(vec[:, k, :], row_bc(ins[name], P)).then_inc(loaded, 16)
            sp.dma_start(bl[:, :], row_bc(ins["L2_gnn_b_l"], P)).then_inc(loaded, 16)
            sp.wait_ge(loaded, 64)

        @block.scalar
        def _(act):
            act.wait_ge(shifted, 1)
            nc.scalar.activation(edge[:, :, :], edge[:, :, :], ACT.Exp)
            nc.scalar.activation(own[:, :, :], own[:, :, :], ACT.Exp).then_inc(exped, 1)
            for w in range(W):
                act.wait_ge(turned, w + 1)
                nc.scalar.copy(at[:, w % 2, :, :].rearrange("p h q -> p (h q)"), tb[w % 2][:, 0:H * Q]).then_inc(copied, 1)
            std_of(nc, act, stats, var_ready, std_ready, 1)

        @block.tensor
        def _(pe):
            pe.wait_ge(ready, 1)

            def turn(w):
                if w >= 2:
                    pe.wait_ge(copied, w - 1)
                for h in range(H):
                    last = nc.tensor.transpose(tb[w % 2][:, h * Q:(h + 1) * Q], m.acc[:, w, h * D:(h + 1) * D], m.ident[0:Q, 0:Q])
                last.then_inc(turned, 1)

            turn(0)
            for w in range(W):
                if w + 1 < W:
                    turn(w + 1)
                pe.wait_ge(copied, w + 1)
                if w >= 2:
                    pe.wait_ge(read, w - 1)
                for h in range(H):
                    last = nc.tensor.matmul(ob[w % 2][0:Q, 0:D], at[:, w % 2, h, :], m.gat_wl[:, h * D:(h + 1) * D],
                                            start=(h == 0), stop=(h == H - 1))
                last.then_inc(done, 1)

        @block.vector
        def _(dve):
            v, link = nc.vector, make_link(dve, chain)
            den, emax = m.acc[:, :, H * D:H * D + H], m.acc[:, :, H * D + H:H * D + 2 * H]
            link(v.tensor_scalar(edge[:, :, :], den, 0.0, None, ALU.is_gt))
            link(v.tensor_scalar(edge[:, :, :], edge[:, :, :], 1.0, BIG, ALU.subtract, ALU.mult))
            link(v.tensor_tensor(edge[:, :, :], edge[:, :, :], emax, ALU.add))
            link(v.tensor_tensor(inv[:, :, :], edge[:, :, :], m.self_score[:, :, :], ALU.max))
            link(v.tensor_tensor(edge[:, :, :], edge[:, :, :], inv[:, :, :], ALU.subtract))
            link(v.tensor_tensor(own[:, :, :], m.self_score[:, :, :], inv[:, :, :], ALU.subtract))
            dve.sem_inc(shifted, 1)
            dve.wait_ge(exped, 1)
            link(v.tensor_tensor(inv[:, :, :], den, edge[:, :, :], ALU.mult))
            link(v.tensor_tensor(inv[:, :, :], inv[:, :, :], own[:, :, :], ALU.add))
            link(v.tensor_scalar(inv[:, :, :], inv[:, :, :], 1e-16, None, ALU.add))
            link(v.reciprocal(inv[:, :, :], inv[:, :, :]))
            link(v.tensor_scalar(inv[:, :, :], inv[:, :, :], 1.0 / H, None, ALU.mult))
            link(v.tensor_tensor(edge[:, :, :], edge[:, :, :], inv[:, :, :], ALU.mult))
            link(v.tensor_tensor(own[:, :, :], own[:, :, :], inv[:, :, :], ALU.mult))
            for h in range(H):
                a = m.acc[:, :, h * D:(h + 1) * D]
                link(v.tensor_tensor(a, a, bc_last(edge[:, :, h], D), ALU.mult))
                link(v.tensor_tensor(tmp[:, :, :], m.x[:, :, :], bc_last(own[:, :, h], D), ALU.mult))
                link(v.tensor_tensor(a, a, tmp[:, :, :], ALU.add))
            dve.sem_inc(ready, 1)
            dve.wait_ge(loaded, 64)
            for h in range(H):
                link(v.scalar_tensor_tensor(vec[:, 0, :], bl[:, h * D:(h + 1) * D], 1.0 / H, vec[:, 0, :], ALU.mult, ALU.add))
            link(v.tensor_tensor(tmp[:, :, :], m.x[:, :, :], bc_mid(vec[0:Q, 0, :], W), ALU.add))
            for w in range(W):
                dve.wait_ge(done, w + 1)
                v.tensor_tensor(tmp[:, w, :], tmp[:, w, :], ob[w % 2][0:Q, 0:D], ALU.add).then_inc(read, 1)
            dve.wait_ge(read, W)
            layer_norm(nc, dve, link, tmp[:, :, :], m.h[:, :, :], m.acc[:, :, 0:D], stats, EPS, var_ready, std_ready, 1)
            link(v.tensor_tensor(m.h[:, :, :], m.h[:, :, :], bc_mid(vec[0:Q, 1, :], W), ALU.mult))
            link(v.tensor_tensor(m.h[:, :, :], m.h[:, :, :], bc_mid(vec[0:Q, 2, :], W), ALU.add))


def feed_forward(nc, m, ins):
    with ExitStack() as ctx:
        sb, sem, bank = scope(nc, ctx)
        w1, w2 = sb("ff_w1", [D, 2 * D]), sb("ff_w2", [D, 2, D])
        b1, b2 = sb("ff_b1", [D, 2]), sb("ff_b2", [P, D])
        ht, ut = sb("ht", [P, W, Q]), sb("ut", [P, 2, W, Q])
        stats = sb("stats6", [Q, 2, W])
        tb, ub, ob = ([bank(f"f_{k}{i}") for i in range(2)] for k in "tuo")
        loaded, chain, turned, copied, u_done, u_read, o_done, o_read, var_ready, std_ready, leaky = (sem(n) for n in (
            "loaded6", "chain6", "t6", "c6", "u6", "ur6", "o6", "or6", "var6", "std6", "leaky6"))
        block = ctx.enter_context(nc.Block())
        tmp = m.acc[:, :, 0:D]

        @block.sync
        def _(sp):
            sp.dma_start(w1[:, :], ins["L2_gnn_W1"]).then_inc(loaded, 16)
            sp.dma_start(w2[:, :, :], ins["L2_gnn_W2"].rearrange("(c f) d -> f c d", c=2)).then_inc(loaded, 16)
            sp.dma_start(b1[:, :], ins["L2_gnn_b1"].rearrange("(c f) -> f c", c=2), allow_slow_non_contiguous=True).then_inc(loaded, 16)
            sp.dma_start(b2[:, :], row_bc(ins["L2_gnn_b2"], P)).then_inc(loaded, 16)
            sp.wait_ge(loaded, 64)

        @block.tensor
        def _(pe):
            turn_windows_pe(nc, pe, m, m.h, tb, turned, copied)
            pe.wait_ge(copied, TG)
            pe.wait_ge(loaded, 64)
            for g in range(TG):
                k = min(4, W - 4 * g)
                for c in range(2):
                    if g:
                        pe.wait_ge(u_read, 2 * (g - 1) + c + 1)
                    nc.tensor.matmul(ub[c][:, 0:k * Q], w1[:, c * D:(c + 1) * D],
                                     ht[:, 4 * g:4 * g + k, :].rearrange("d w q -> d (w q)"), start=True, stop=True).then_inc(u_done, 1)
            pe.wait_ge(leaky, 2 * TG)
            for w in range(W):
                if w >= 2:
                    pe.wait_ge(o_read, w - 1)
                for c in range(2):
                    last = nc.tensor.matmul(ob[w % 2][0:Q, 0:D], ut[:, c, w, :], w2[:, c, :], start=(c == 0), stop=(c == 1))
                last.then_inc(o_done, 1)

        @block.scalar
        def _(act):
            turn_windows_act(nc, act, m, ht, tb, turned, copied)
            act.wait_ge(loaded, 64)
            for g in range(TG):
                k = min(4, W - 4 * g)
                for c in range(2):
                    act.wait_ge(u_done, 2 * g + c + 1)
                    nc.scalar.activation(ut[:, c, 4 * g:4 * g + k, :].rearrange("d w q -> d (w q)"), ub[c][:, 0:k * Q],
                                         ACT.Identity, bias=b1[:, c:c + 1]).then_inc(u_read, 1)
            std_of(nc, act, stats, var_ready, std_ready, 1)

        @block.vector
        def _(dve):
            v, link = nc.vector, make_link(dve, chain)
            dve.wait_ge(loaded, 64)
            link(v.tensor_tensor(tmp, m.h[:, :, :], bc_mid(b2[0:Q, :], W), ALU.add))
            link(v.tensor_tensor(tmp, tmp, m.x[:, :, :], ALU.add))
            for n in range(2 * TG):
                dve.wait_ge(u_read, n + 1)
                u = ut[:, n % 2, 4 * (n // 2):min(4 * (n // 2) + 4, W), :]
                v.scalar_tensor_tensor(u, u, 0.2, u, ALU.mult, ALU.max).then_inc(leaky, 1)
            for w in range(W):
                dve.wait_ge(o_done, w + 1)
                v.tensor_tensor(m.acc[:, w, 0:D], m.acc[:, w, 0:D], ob[w % 2][0:Q, 0:D], ALU.add).then_inc(o_read, 1)
            dve.wait_ge(o_read, W)
            layer_norm(nc, dve, link, tmp, m.x[:, :, :], m.acc[:, :, D:2 * D], stats, EPS, var_ready, std_ready, 1)


def conv_nodes(nc, m, ins, n, src, kv_table):
    with ExitStack() as ctx:
        sb, sem, bank = scope(nc, ctx)
        w4, b4 = sb("w4", [D, 4, D]), sb("b4", [P, 4, D])
        xt = sb("xt7", [P, W, Q])
        tb, ob = [bank(f"q_t{i}") for i in range(2)], [bank(f"q_o{i}") for i in range(2)]
        loaded, turned, copied, done, read, stored = (sem(x) for x in ("loaded7", "t7", "c7", "o7", "r7", "stored7"))
        block = ctx.enter_context(nc.Block())

        @block.sync
        def _(sp):
            for k, x in enumerate("qkvs"):
                sp.dma_start(w4[:, k, :], ins[f"L3_gnn_W{x}{n}"]).then_inc(loaded, 16)
                sp.dma_start(b4[:, k, :], row_bc(ins[f"L3_gnn_b{x}{n}"], P)).then_inc(loaded, 16)
            sp.wait_ge(read, W)
            sp.dma_start(nodes(kv_table), m.acc[:, :, D:3 * D]).then_inc(stored, 16)
            sp.wait_ge(stored, 16)

        @block.tensor
        def _(pe):
            turn_windows_pe(nc, pe, m, src, tb, turned, copied)
            pe.wait_ge(copied, TG)
            pe.wait_ge(loaded, 128)
            for w in range(W):
                if w >= 2:
                    pe.wait_ge(read, w - 1)
                nc.tensor.matmul(ob[w % 2][0:Q, :], xt[:, w, :], w4[:, :, :].rearrange("d k c -> d (k c)"),
                                 start=True, stop=True).then_inc(done, 1)

        @block.scalar
        def _(act):
            turn_windows_act(nc, act, m, xt, tb, turned, copied)

        @block.vector
        def _(dve):
            dve.wait_ge(loaded, 128)
            for w in range(W):
                dve.wait_ge(done, w + 1)
                nc.vector.tensor_tensor(m.acc[:, w, 0:4 * D], ob[w % 2][0:Q, :], b4[0:Q, :, :].rearrange("q k c -> q (k c)"),
                                        ALU.add).then_inc(read, 1)


def conv_scores(nc, m, kv_table, v_rows):
    with ExitStack() as ctx:
        sb, sem, bank = scope(nc, ctx)
        loop = PairLoop(nc, m, ctx, kv_table, width=2 * D)
        got, hot = loop.got, loop.hot
        hot_t = sb("hot_t", [Q, 2, G, P])
        prod, score = sb("prod", [P, 2, G, D]), sb("score", [P, 2, G, H])
        hot_b = [bank(f"hot_b{i}") for i in range(2)]
        q_b = [bank(f"q_b{i}") for i in range(2)]
        turned, copied_t, q_done, out, chain, used = (sem(n) for n in (
            "turned", "copied_t", "q_done", "alpha_out", "chain8", "used"))
        aside = [sem("aside0"), sem("aside1")]
        block = ctx.enter_context(nc.Block())

        @block.sync
        def _(sp):
            with sp.Fori(0, STEPS) as i:
                for b in range(2):
                    sp.wait_ge(loop.come[b], 64 * i + 64)
                    sp.dma_start(v_rows[bass.ds(2 * i + b, 1), :, :].rearrange("a l (j d) -> (a l) j d", j=G),
                                 got[:, b, :, D:2 * D]).then_inc(aside[b], 16)
            for b in range(2):
                sp.wait_ge(aside[b], 16 * STEPS)

        @block.gpsimd
        def _(pool):
            def wait_free(i, b, g):
                pool.wait_ge(used, g + 3).then_inc(loop.tick, 1)
                pool.wait_ge(aside[b], 16 * i + 16).then_inc(loop.tick, 1)

            loop.gathers(pool, wait_free)

        @block.vector
        def _(dve):
            v = nc.vector
            dve.sem_inc(used, 2)
            loop.first_rows(dve)
            for b in range(2):
                loop.one_hots(b * G, b)
            with dve.Fori(0, STEPS) as i:
                for b in range(2):
                    g, at = 2 * i + b, i * (2 * G) + b * G
                    loop.next_rows(dve, at + 2 * G, b, i + 1)
                    dve.wait_ge(turned, g + 1)
                    loop.one_hots(at + 2 * G, b)
                    dve.wait_ge(q_done, g + 1)
                    v.tensor_tensor(prod[:, b, :, :], q_b[b][:, :].rearrange("p (j d) -> p j d", j=G),
                                    got[:, b, :, 0:D], ALU.mult).then_inc(used, 1)
                    dve.wait_ge(used, g + 3)
                    v.reduce_sum(score[:, b, :, :], prod[:, b, :, :].rearrange("p j (h c) -> p j h c", h=H), AX).then_inc(chain, 1)
                    dve.wait_ge(chain, g + 1)
                    v.tensor_scalar(m.alpha[:, :, bass.ds(at, G)], score[:, b, :, :].rearrange("p j h -> p h j"),
                                    float(C) ** -0.5, None, ALU.mult).then_inc(out, 1)

        @block.scalar
        def _(act):
            def copy(b, g):
                act.wait_ge(turned, g + 1)
                nc.scalar.copy(hot_t[:, b, :, :].rearrange("p j e -> p (j e)"), hot_b[b][0:Q, :]).then_inc(copied_t, 1)

            copy(0, 0)
            with act.Fori(0, STEPS) as i:
                for b in range(2):
                    copy(1 - b, 2 * i + (b + 1))

        @block.tensor
        def _(pe):
            t = nc.tensor

            def turn(b, g):
                pe.wait_ge(loop.hot_ready, g + 1)
                for j in range(G):
                    last = t.transpose(hot_b[b][0:Q, j * P:(j + 1) * P], hot[:, b, j, :], m.ident[:, :])
                last.then_inc(turned, 1)

            turn(0, 0)
            with pe.Fori(0, STEPS) as i:
                for b in range(2):
                    g, at = 2 * i + b, i * (2 * G) + b * G
                    ws = windows(nc, m, ENG.PE, at, G)
                    turn(1 - b, g + 1)
                    pe.wait_ge(copied_t, g + 1)
                    pe.wait_ge(used, g + 1)
                    for j in range(G):
                        w = ws[j]
                        last = t.matmul(q_b[b][:, j * P:(j + 1) * P], hot_t[:, b, j, :],
                                        m.acc[:, bass.ds(w, 1), 0:D].rearrange("q o d -> q (o d)"), start=True, stop=True)
                    last.then_inc(q_done, 1)


def conv_finish(nc, m, last_layer, out):
    with ExitStack() as ctx:
        sb, sem, bank = scope(nc, ctx)
        inv = sb("inv9", [Q, W, H])
        tmp, stats = sb("tmp9", [Q, W, D]), sb("stats9", [Q, 2, W])
        chain, var_ready, std_ready, ready, stored = (sem(n) for n in ("chain9", "var9", "std9", "ready9", "stored9"))
        block = ctx.enter_context(nc.Block())

        if last_layer:
            @block.sync
            def _(sp):
                sp.wait_ge(ready, 1)
                sp.dma_start(nodes(out), m.h[:, :, :]).then_inc(stored, 16)
                sp.wait_ge(stored, 16)

            @block.scalar
            def _(act):
                std_of(nc, act, stats, var_ready, std_ready, 1)

        @block.vector
        def _(dve):
            v, link = nc.vector, make_link(dve, chain)
            link(v.tensor_scalar(inv[:, :, :], m.dens[:, :, :], 1e-30, None, ALU.max))
            link(v.reciprocal(inv[:, :, :], inv[:, :, :]))
            link(v.tensor_tensor(tmp[:, :, :].rearrange("q w (h c) -> q w h c", h=H),
                                 m.sums[:, :, :].rearrange("q w (h c) -> q w h c", h=H),
                                 inv[:, :, :].unsqueeze(3).broadcast_to([Q, W, H, C]), ALU.mult))
            link(v.tensor_tensor(tmp[:, :, :], tmp[:, :, :], m.acc[:, :, 3 * D:4 * D], ALU.add))
            if not last_layer:
                link(v.tensor_scalar(m.h[:, :, :], tmp[:, :, :], 0.0, None, ALU.max))
            else:
                link(v.tensor_tensor(tmp[:, :, :], tmp[:, :, :], m.x[:, :, :], ALU.add))
                layer_norm(nc, dve, link, tmp[:, :, :], m.h[:, :, :], m.acc[:, :, 0:D], stats, EPS, var_ready, std_ready, 1)
                dve.sem_inc(ready, 1)


def build(nc, ins, out):
    with ExitStack() as ctx:
        m = Mem()
        sb, sem, bank = scope(nc, ctx)
        common(m, sb)
        m.come = [[sem(f"come{n}_{b}") for b in range(2)] for n in range(6)]
        m.added = [sem(f"added{j}") for j in range(G)]
        y_table = nc.dram_tensor("y_table", [R * N, D], F32, kind="Internal").ap()
        tables = [nc.dram_tensor(f"agg{j}", [ACCROWS, D], F32, kind="Internal").ap() for j in range(G)]
        t_table, x_table = (nc.dram_tensor(n, [N, D], F32, kind="Internal").ap() for n in ("t_table", "x_table"))
        kv_table = nc.dram_tensor("kv_table", [N, 2 * D], F32, kind="Internal").ap()
        v_rows = nc.dram_tensor("v_rows", [PAIRS // G, P, G * D], F32, kind="Internal").ap()
        setup_phase(nc, m, ins)
        relation_rows(nc, m, ins, y_table)
        count_edges(nc, m)
        relation_edges(nc, m, y_table, tables)
        m.h = sb("h", [Q, W, D])
        m.self_score = sb("self_score", [Q, W, H])
        m.gat_wl, m.att, m.wl_att = sb("gat_wl", [D, H * D]), sb("att", [P, H * D]), sb("wl_att", [D, H])
        gcn_nodes(nc, m, ins, tables, t_table)
        m.agg = sb("agg", [Q, W, D])
        gcn_sums(nc, m, t_table)
        batch_norm(nc, m, ins, x_table)
        m.acc = sb("acc", [Q, W, H * D + 2 * H])
        gat_nodes(nc, m, ins)
        gat_scores(nc, m, x_table)
        segment_softmax(nc, m)
        clear(nc, m.acc[:, :, :])
        gat_sums(nc, m, x_table)
        gat_finish(nc, m, ins)
        feed_forward(nc, m, ins)
        m.sums, m.dens = m.agg, sb("dens", [Q, W, H])
        for n, src in ((1, m.x), (2, m.h)):
            conv_nodes(nc, m, ins, n, src, kv_table)
            conv_scores(nc, m, kv_table, v_rows)
            segment_softmax(nc, m)
            conv_sums(nc, m, v_rows)
            conv_finish(nc, m, n == 2, out)


def kernel(**inputs):
    import numpy as _np
    import concourse.bacc as _bacc
    from concourse import mybir as _mybir
    from concourse.bass_utils import run_bass_kernel_spmd as _run

    nc = _bacc.Bacc("TRN2", target_bir_lowering=False, num_devices=1)
    arrays, args = {}, {}
    for name in inputs:
        a = _np.ascontiguousarray(inputs[name])
        arrays[f"in_{name}_dram"] = a
        args[name] = nc.dram_tensor(f"in_{name}_dram", a.shape, _mybir.dt.from_np(a.dtype), kind="ExternalInput").ap()
    out = nc.dram_tensor("out_0_dram", (N, D), F32, kind="ExternalOutput").ap()
    build(nc, args, out)
    r = _run(nc, [arrays], core_ids=[0])
    return r.results[0]["out_0_dram"]
```

```python
import itertools
import numpy as np
import concourse.bass as bass
import concourse.mybir as mybir
from contextlib import ExitStack

F32, BF16, I32, U32 = mybir.dt.float32, mybir.dt.bfloat16, mybir.dt.int32, mybir.dt.uint32
ENG = mybir.EngineType
ALU, ACT, AX = mybir.AluOpType, mybir.ActivationFunctionType, mybir.AxisListType.X

N, E, D, R, H = 3125, 50000, 128, 8, 4
Q, W = 125, 25
P = 128
C = 32
TILES = 392
CH = 98
NCH = TILES // CH
FULL, REST = E // P, E % P
PAIRS = 416
G = 4
PAD_DST, PAD_SRC = 4000, 3200
ROWLO, ROWHI = 128, 196
ACCROWS = 27 * P
DUMP = 26 * P
BIG = 1.0e30
ROUND = 1.5 * 2.0 ** 23
EPS = 1e-5
SLOTPAD = PAIRS + 4 * G
BLOCKS = H * PAIRS // P
assert TILES * P >= E and FULL + W <= PAIRS and Q * W == N and R * N <= ROWLO * ROWHI


PHASE = itertools.count()


class Mem:
    pass


def scope(nc, ctx):
    n = next(PHASE)
    sems = []

    def clear_semaphores(failed, *_):
        if sems and not failed:
            with nc.Block() as block:
                @block.gpsimd
                def _(pool):
                    for s in sems:
                        pool.sem_clear(s)

    ctx.push(clear_semaphores)

    def sb(name, shape, dt=F32):
        return ctx.enter_context(nc.sbuf_tensor(f"{name}_{n}", shape, dt))

    def sem(name):
        sems.append(ctx.enter_context(nc.semaphore(f"{name}_{n}")))
        return sems[-1]

    def bank(name, shape=(P, 512), dt=F32):
        return ctx.enter_context(nc.psum_tensor(f"{name}_{n}", list(shape), dt))

    return sb, sem, bank

def bc_mid(ap, n):
    return ap.unsqueeze(1).broadcast_to([ap.shape[0], n, ap.shape[1]])


def bc_last(ap, n):
    return ap.unsqueeze(2).broadcast_to([ap.shape[0], ap.shape[1], n])


def row_bc(ap, n):
    return ap.rearrange("(o n) -> o n", o=1).broadcast_to([n, ap.shape[0]])


def nodes(ap):
    return ap.rearrange("(w q) d -> q w d", q=Q)


def setup_phase(nc, m, ins):
    with ExitStack() as ctx:
        sb, sem, bank = scope(nc, ctx)

        nat_i = sb("nat_i", [CH, 3, NCH, P], I32)
        row_i = sb("row_i", [CH, 3, NCH, P], I32)
        nat = sb("nat", [CH, 2, NCH, P])
        win = sb("win", [CH, NCH, P])
        quant = sb("quant", [CH, 5, NCH, P])
        edge_flags = sb("edge_flags", [CH, 2, NCH, P])
        below = sb("below", [CH, NCH, W])
        thresholds = sb("thresholds", [P, W])
        tile_no = sb("tile_no", [P, NCH])
        pick = sb("pick", [CH, NCH, PAIRS])
        ones = sb("ones", [P, P])
        ends, past = sb("ends", [W - 1, 1]), sb("past", [W - 1, PAIRS])
        pair_tile = sb("pair_tile", [P, PAIRS])
        last0 = sb("last0", [P, 2, PAIRS])
        same = sb("same", [P, 4, PAIRS])
        io = sb("io", [P, 512], I32)
        io2 = sb("io2", [P, NCH], I32)
        ps = [bank(f"ps{i}") for i in range(8)]
        loaded, consts, chain = sem("edges_loaded"), sem("consts"), sem("dve_chain")
        padded, quant_ready, lanes_done = sem("padded"), sem("quant_ready"), sem("lanes_done")
        lanes_read, below_ready, ends_done = sem("lanes_read"), sem("below_ready"), sem("ends_done")
        pick_ready, slots_done, slots_read = sem("pick_ready"), sem("slots_done"), sem("slots_read")
        past_ready, wins_done = sem("past_ready"), sem("wins_done")
        pens_ready, pens_turned = sem("pens_ready"), sem("pens_turned")
        start_pen = sb("start_pen", [P, H, PAIRS])
        end_pen = sb("end_pen", [P, H, PAIRS])
        block = ctx.enter_context(nc.Block())

        @block.sync
        def _(sp):
            sp.wait_ge(padded, 1)
            for k, name in enumerate(("src", "dst", "edge_type_8")):
                a = ins[name]
                for c in range(NCH):
                    rows = min(CH, FULL - CH * c)
                    sp.dma_start(nat_i[0:rows, k, c, :],
                                 a[c * CH * P:(c * CH + rows) * P].rearrange("(t l) -> t l", l=P)).then_inc(loaded, 16)
                    if rows < CH:
                        sp.dma_start(nat_i[rows:rows + 1, k, c, 0:REST],
                                     a[FULL * P:E].rearrange("(o l) -> o l", o=1)).then_inc(loaded, 16)
            sp.dma_start(m.x[:, :, :], nodes(ins["x"])).then_inc(loaded, 16)
            sp.wait_ge(loaded, 16 * (3 * (NCH + 1) + 1))

        @block.gpsimd
        def _(pool):
            pool.memset(nat_i[:, 0, :, :], PAD_SRC).then_inc(consts, 1)
            pool.memset(nat_i[:, 1, :, :], PAD_DST).then_inc(consts, 1)
            pool.memset(nat_i[:, 2, :, :], 0).then_inc(consts, 1)
            pool.wait_ge(consts, 3)
            pool.sem_inc(padded, 1)
            pool.memset(m.ident[:, :], 0.0).then_inc(consts, 1)
            pool.memset(m.rows_before[:, :], 1.0).then_inc(consts, 1)
            pool.memset(m.only0[:, :], 0.0).then_inc(consts, 1)
            pool.memset(m.only127[:, :], 0.0).then_inc(consts, 1)
            pool.memset(ones[:, :], 1.0).then_inc(consts, 1)
            pool.iota(io[:, :], [[1, 512]], base=0, channel_multiplier=0).then_inc(consts, 1)
            pool.iota(io2[:, :], [[CH, NCH]], base=0, channel_multiplier=1).then_inc(consts, 1)
            pool.wait_ge(consts, 10)
            pool.affine_select(out=m.ident[:, :], in_=m.ident[:, :], compare_op=ALU.not_equal, fill=1.0,
                               base=0, pattern=[[-1, P]], channel_multiplier=1).then_inc(consts, 1)
            pool.affine_select(out=m.rows_before[:, :], in_=m.rows_before[:, :], compare_op=ALU.is_gt, fill=0.0,
                               base=0, pattern=[[-1, P]], channel_multiplier=1).then_inc(consts, 1)
            pool.affine_select(out=m.only0[:, :], in_=m.only0[:, :], compare_op=ALU.not_equal, fill=1.0,
                               base=0, pattern=[[0, P]], channel_multiplier=1).then_inc(consts, 1)
            pool.affine_select(out=m.only127[:, :], in_=m.only127[:, :], compare_op=ALU.not_equal, fill=1.0,
                               base=-(P - 1), pattern=[[0, P]], channel_multiplier=1).then_inc(consts, 1)

        @block.vector
        def _(dve):
            v, count = nc.vector, [0]

            def link(op):
                count[0] += 1
                op.then_inc(chain, 1)
                dve.wait_ge(chain, count[0])

            dve.wait_ge(consts, 14)
            v.tensor_copy(m.iota[:, :], io[:, :]).then_inc(chain, 1)
            v.tensor_copy(tile_no[:, :], io2[:, :]).then_inc(chain, 1)
            v.tensor_copy(m.lane[:, :], io2[:, 0:1]).then_inc(chain, 1)
            v.tensor_copy(m.ident_b[:, :], m.ident[:, :]).then_inc(chain, 1)
            v.memset(m.pair_src[:, PAIRS:SLOTPAD], 0).then_inc(chain, 1)
            v.memset(m.y_row[:, TILES:TILES + 8], 0).then_inc(chain, 1)
            v.memset(m.src_lane[:, TILES:TILES + 3 * G], 0.0).then_inc(chain, 1)
            v.memset(m.row_lo[:, TILES:TILES + 3 * G], 0.0).then_inc(chain, 1)
            v.memset(m.row_hi_f[:, TILES:TILES + G], 0.0).then_inc(chain, 1)
            v.memset(m.pair_dst[:, PAIRS:PAIRS + 2 * G], -1.0).then_inc(chain, 1)
            v.memset(m.small[:, PAIRS:PAIRS + 2 * G, :], 0.0).then_inc(chain, 1)
            count[0] = 11
            dve.wait_ge(chain, 11)
            link(v.tensor_copy(m.iota_b[:, :], m.iota[:, 0:256]))
            link(v.tensor_scalar(thresholds[:, :], m.iota[:, 0:W], float(Q), float(Q), ALU.mult, ALU.add))
            dve.wait_ge(loaded, 16 * (3 * (NCH + 1) + 1))
            src_i, dst_i, rel_i = nat_i[:, 0, :, :], nat_i[:, 1, :, :], nat_i[:, 2, :, :]
            v.tensor_copy(nat[:, 0, :, :], src_i).then_inc(chain, 1)
            v.tensor_copy(nat[:, 1, :, :], dst_i).then_inc(chain, 1)
            v.scalar_tensor_tensor(row_i[:, 0, :, :], src_i, float(R), rel_i, ALU.mult, ALU.add).then_inc(chain, 1)
            v.scalar_tensor_tensor(quant[:, 1, :, :], dst_i, float(R), rel_i, ALU.mult, ALU.add).then_inc(chain, 1)
            count[0] += 4
            dve.wait_ge(chain, count[0])
            link(v.tensor_tensor(below[:, :, :], nat[:, 1, :, P - 1:P].broadcast_to([CH, NCH, W]),
                                 bc_mid(thresholds[0:CH, :], NCH), ALU.is_lt))
            dve.sem_inc(below_ready, 1)
            link(v.tensor_scalar(quant[:, 1, :, :], quant[:, 1, :, :], float(R * N - 1), None, ALU.min))
            link(v.tensor_copy(quant[:, 0, :, :], nat[:, 0, :, :]))
            link(v.tensor_scalar(row_i[:, 1, :, :], row_i[:, 0, :, :], ROWLO - 1, None, ALU.bitwise_and))
            link(v.tensor_scalar(row_i[:, 2, :, :], row_i[:, 0, :, :], 7, None, ALU.arith_shift_right))
            link(v.tensor_copy(quant[:, 2, :, :], row_i[:, 1, :, :]))
            link(v.tensor_copy(quant[:, 3, :, :], row_i[:, 2, :, :]))
            link(v.tensor_scalar(win[:, :, :], nat[:, 1, :, :], 1.0 / Q, 0.5 / Q - 0.5, ALU.mult, ALU.add))
            link(v.tensor_scalar(win[:, :, :], win[:, :, :], ROUND, None, ALU.add))
            link(v.tensor_scalar(win[:, :, :], win[:, :, :], ROUND, None, ALU.subtract))
            link(v.scalar_tensor_tensor(quant[:, 4, :, :], win[:, :, :], -float(Q), nat[:, 1, :, :], ALU.mult, ALU.add))
            link(v.memset(edge_flags[:, :, :, :], -BIG))
            v.tensor_tensor(edge_flags[:, 0, :, 1:P], nat[:, 1, :, 1:P], nat[:, 1, :, 0:P - 1], ALU.not_equal).then_inc(chain, 1)
            v.tensor_tensor(edge_flags[:, 1, :, 0:P - 1], nat[:, 1, :, 1:P], nat[:, 1, :, 0:P - 1], ALU.not_equal).then_inc(chain, 1)
            count[0] += 2
            dve.wait_ge(chain, count[0])
            v.tensor_scalar(edge_flags[:, 0, :, 1:P], edge_flags[:, 0, :, 1:P], -BIG, None, ALU.mult).then_inc(chain, 1)
            v.tensor_scalar(edge_flags[:, 1, :, 0:P - 1], edge_flags[:, 1, :, 0:P - 1], -BIG, None, ALU.mult).then_inc(chain, 1)
            count[0] += 2
            dve.wait_ge(chain, count[0])
            dve.sem_inc(quant_ready, 1)
            dve.wait_ge(ends_done, 1)
            link(v.tensor_tensor(ends[:, :], ps[7][0:W - 1, 0:1], m.lane[0:W - 1, :], ALU.add))
            link(v.tensor_scalar(past[:, :], m.iota[0:W - 1, 0:PAIRS], ends[:, :], None, ALU.is_gt))
            dve.sem_inc(past_ready, 1)
            dve.wait_ge(wins_done, 1)
            link(v.tensor_copy(m.pair_win[:, :], ps[6][:, 0:PAIRS]))
            link(v.tensor_copy(m.pair_win_i[:, :], m.pair_win[0:1, :]))
            link(v.tensor_tensor(pair_tile[:, :], m.iota[:, 0:PAIRS], m.pair_win[:, :], ALU.subtract))
            for c in range(NCH):
                link(v.tensor_scalar(pick[:, c, :], pair_tile[0:CH, :], tile_no[0:CH, c:c + 1], None, ALU.is_equal))
            dve.sem_inc(pick_ready, 1)
            dve.wait_ge(lanes_done, 1)
            v.tensor_copy(m.src_lane[:, 0:TILES], ps[0][:, 0:TILES]).then_inc(lanes_read, 1)
            v.tensor_copy(m.y_row[:, 0:TILES], ps[1][:, 0:TILES]).then_inc(lanes_read, 1)
            v.tensor_copy(m.row_lo[:, 0:TILES], ps[2][:, 0:TILES]).then_inc(lanes_read, 1)
            v.tensor_copy(m.row_hi_f[:, 0:TILES], ps[3][:, 0:TILES])
            v.tensor_copy(m.row_hi[:, :], ps[3][:, 0:TILES]).then_inc(lanes_read, 1)
            v.tensor_copy(m.dst_loc[:, :], ps[4][:, 0:TILES]).then_inc(lanes_read, 1)
            v.tensor_copy(m.dst_win[:, :], ps[5][:, 0:TILES]).then_inc(lanes_read, 1)
            dve.wait_ge(slots_done, 1)
            link(v.tensor_scalar(m.pair_src[:, 0:PAIRS], ps[0][:, 0:PAIRS], float(N - 1), None, ALU.min))
            link(v.scalar_tensor_tensor(m.pair_dst[:, 0:PAIRS], m.pair_win[:, :], -float(Q), ps[1][:, 0:PAIRS], ALU.mult, ALU.add))
            for h in range(H):
                link(v.tensor_copy(start_pen[:, h, :], ps[2][:, 0:PAIRS]))
                link(v.tensor_copy(end_pen[:, h, :], ps[3][:, 0:PAIRS]))
            dve.sem_inc(pens_ready, 1)
            link(v.tensor_copy(last0[:, 0, :], ps[4][:, 0:PAIRS]))
            link(v.tensor_copy(last0[:, 1, :], ps[5][:, 0:PAIRS]))
            link(v.tensor_tensor(same[:, 0, :], ps[1][:, 0:PAIRS], last0[:, 1, :], ALU.not_equal))
            link(v.tensor_tensor(same[:, 1, :], ps[1][:, 0:PAIRS], last0[:, 0, :], ALU.not_equal))
            dve.sem_inc(slots_read, 1)
            link(v.tensor_scalar(m.first_pen[:, :], same[:, 0, :], -BIG, None, ALU.mult))
            link(v.tensor_scalar(m.last_pen[:, :], same[:, 1, :], -BIG, None, ALU.mult))
            link(v.memset(same[:, 2:3, :], 0.0))
            link(v.tensor_tensor(same[:, 2, 1:PAIRS], last0[:, 1, 1:PAIRS], last0[:, 0, 0:PAIRS - 1], ALU.is_equal))
            link(v.tensor_tensor(same[:, 3, 1:PAIRS], m.pair_win[:, 1:PAIRS], m.pair_win[:, 0:PAIRS - 1], ALU.is_equal))
            link(v.tensor_tensor(same[:, 2, 1:PAIRS], same[:, 2, 1:PAIRS], same[:, 3, 1:PAIRS], ALU.mult))
            link(v.tensor_tensor(same[:, 3, :], last0[:, 0, :], last0[:, 1, :], ALU.is_equal))
            link(v.tensor_scalar(m.cont_pen[:, :], same[:, 2, :], 1.0, BIG, ALU.subtract, ALU.mult))
            link(v.tensor_tensor(same[:, 0, :], same[:, 2, :], same[:, 3, :], ALU.mult))
            link(v.memset(same[:, 1, :], 0.0))
            link(v.tensor_tensor(same[:, 1, 0:PAIRS - 1], same[:, 2, 1:PAIRS], same[:, 3, 0:PAIRS - 1], ALU.mult))
            for h in range(H):
                link(v.tensor_scalar(m.fwd_pen[:, h, :], same[:, 0, :], 1.0, BIG, ALU.subtract, ALU.mult))
                link(v.tensor_scalar(m.bwd_pen[:, h, :], same[:, 1, :], 1.0, BIG, ALU.subtract, ALU.mult))
            link(v.tensor_scalar(m.leader[:, :], start_pen[:, 0, :], -1.0, None, ALU.is_lt))
            link(v.tensor_scalar(same[:, 1, :], same[:, 2, :], m.only0[:, 0:1], None, ALU.mult))
            link(v.tensor_tensor(m.leader[:, :], m.leader[:, :], same[:, 1, :], ALU.subtract))
            dve.wait_ge(pens_turned, 1)
            for k in range(4):
                cols = min(512, H * PAIRS - 512 * k)
                link(v.tensor_copy(m.start_turned[:, 512 * k:512 * k + cols], ps[k][:, 0:cols]))
                link(v.tensor_copy(m.end_turned[:, 512 * k:512 * k + cols], ps[4 + k][:, 0:cols]))

        @block.tensor
        def _(pe):
            t = nc.tensor
            pe.wait_ge(consts, 14)
            pe.wait_ge(below_ready, 1)
            for c in range(NCH):
                last = t.matmul(ps[7][0:W - 1, 0:1], below[:, c, 0:W - 1], ones[0:CH, 0:1], start=(c == 0), stop=(c == NCH - 1))
            last.then_inc(ends_done, 1)
            pe.wait_ge(quant_ready, 1)
            for k in range(6):
                for c in range(NCH):
                    a = quant[:, k, c, :] if k < 5 else win[:, c, :]
                    last = t.transpose(ps[k][:, c * CH:(c + 1) * CH], a, m.ident[0:CH, 0:CH])
            last.then_inc(lanes_done, 1)
            pe.wait_ge(past_ready, 1)
            t.matmul(ps[6][:, 0:PAIRS], ones[0:W - 1, :], past[:, :], start=True, stop=True).then_inc(wins_done, 1)
            pe.wait_ge(pick_ready, 1)
            pe.wait_ge(lanes_read, 6)
            for k in range(6):
                for c in range(NCH):
                    if k < 2:
                        a = nat[:, k, c, :]
                    elif k < 4:
                        a = edge_flags[:, k - 2, c, :]
                    else:
                        lane = P - 1 if k == 4 else 0
                        a = nat[:, 1, c, lane:lane + 1].broadcast_to([CH, P])
                    last = t.matmul(ps[k][:, 0:PAIRS], a, pick[:, c, :], start=(c == 0), stop=(c == NCH - 1))
            last.then_inc(slots_done, 1)
            pe.wait_ge(pens_ready, 1)
            pe.wait_ge(slots_read, 1)
            for base, pen in ((0, start_pen), (4, end_pen)):
                flat = pen[:, :, :].rearrange("l h p -> l (h p)")
                for n in range(BLOCKS):
                    last = t.transpose(ps[base + n // 4][:, (n % 4) * P:(n % 4 + 1) * P], flat[:, n * P:(n + 1) * P],
                                       m.ident[:, :])
            last.then_inc(pens_turned, 1)


def segment_softmax(nc, m, acc=None):
    with ExitStack() as ctx:
        sb, sem, bank = scope(nc, ctx)

        cols = H * PAIRS
        carried = sb("carried", [P, 2, H, PAIRS])
        fwd, both = (carried[:, k, :, :].rearrange("l h p -> l (h p)") for k in range(2))
        top = sb("top", [P, H, PAIRS])
        ends2 = sb("ends2", [P, 2, cols])
        low, high = bank("sg_low", (P, 2048)), bank("sg_high", (P, 2048))
        turned, scanned, back, top_ready = sem("turned"), sem("scanned"), sem("back"), sem("top_ready")
        ends_ready, chain, shifted, exped = sem("ends_ready"), sem("seg_chain"), sem("shifted"), sem("exped")
        block = ctx.enter_context(nc.Block())
        alpha = m.alpha[:, :, :].rearrange("l h p -> l (h p)")
        less = carried[:, 0, :, :]
        topf = top[:, :, :].rearrange("l h p -> l (h p)")

        def width(k):
            return min(512, cols - 512 * k)

        @block.tensor
        def _(pe):
            t = nc.tensor
            for n in range(BLOCKS):
                last = t.transpose(low[:, n * P:(n + 1) * P], alpha[:, n * P:(n + 1) * P], m.ident[:, :])
            last.then_inc(turned, 1)
            pe.wait_ge(scanned, 1)
            for n in range(BLOCKS):
                last = t.transpose(high[:, n * P:(n + 1) * P], both[:, n * P:(n + 1) * P], m.ident[:, :])
            last.then_inc(back, 1)
            pe.wait_ge(top_ready, 1)
            for sums, lane in ((high, m.only127), (low, m.only0)):
                for k in range(4):
                    last = t.matmul(sums[:, 512 * k:512 * k + width(k)], lane[:, :], topf[:, 512 * k:512 * k + width(k)],
                                    start=True, stop=True)
                last.then_inc(ends_ready, 1)

        if acc is not None:
            @block.gpsimd
            def _(pool):
                pool.memset(acc[:, :, :], 0.0)

        @block.scalar
        def _(act):
            act.wait_ge(shifted, 1)
            nc.scalar.activation(m.small[:, 0:PAIRS, 0:H], less.rearrange("l h p -> l p h"), ACT.Exp).then_inc(exped, 1)

        @block.vector
        def _(dve):
            v, count = nc.vector, [0]

            def link(op):
                count[0] += 1
                op.then_inc(chain, 1)
                dve.wait_ge(chain, count[0])

            dve.wait_ge(turned, 1)
            link(v.tensor_tensor_scan(fwd, m.start_turned[:, :], low[:, 0:cols], -BIG, ALU.add, ALU.max))
            link(v.tensor_tensor_scan(both[:, ::-1], m.end_turned[:, ::-1], fwd[:, ::-1], -BIG, ALU.add, ALU.max))
            dve.sem_inc(scanned, 1)
            dve.wait_ge(back, 1)
            link(v.tensor_copy(topf, high[:, 0:cols]))
            dve.sem_inc(top_ready, 1)
            fpen = m.fwd_pen[:, :, :].rearrange("l h p -> l (h p)")
            bpen = m.bwd_pen[:, :, :].rearrange("l h p -> l (h p)")
            dve.wait_ge(ends_ready, 1)
            link(v.tensor_tensor_scan(fwd, fpen, high[:, 0:cols], -BIG, ALU.add, ALU.max))
            dve.wait_ge(ends_ready, 2)
            link(v.tensor_tensor_scan(both[:, ::-1], bpen[:, ::-1], low[:, 0:cols][:, ::-1], -BIG, ALU.add, ALU.max))
            inc = ends2[:, 0, :].rearrange("l (h p) -> l h p", h=H)
            inb = ends2[:, 1, :].rearrange("l (h p) -> l h p", h=H)
            link(v.memset(inc[:, :, 0:1], -BIG))
            link(v.memset(inb[:, :, PAIRS - 1:PAIRS], -BIG))
            link(v.tensor_tensor(inc[:, :, 1:PAIRS], carried[:, 0, :, 0:PAIRS - 1], bc_mid(m.cont_pen[:, 1:PAIRS], H), ALU.add))
            link(v.tensor_tensor(inb[:, :, 0:PAIRS - 1], carried[:, 1, :, 1:PAIRS], bc_mid(m.cont_pen[:, 1:PAIRS], H), ALU.add))
            link(v.tensor_tensor(inc, inc, bc_mid(m.first_pen[:, :], H), ALU.add))
            link(v.tensor_tensor(inb, inb, bc_mid(m.last_pen[:, :], H), ALU.add))
            link(v.tensor_tensor(inc, inc, inb, ALU.max))
            link(v.tensor_tensor(top[:, :, :], top[:, :, :], inc, ALU.max))
            link(v.tensor_tensor(less, m.alpha[:, :, :], top[:, :, :], ALU.subtract))
            link(v.tensor_scalar(less, less, 0.0, None, ALU.min))
            dve.sem_inc(shifted, 1)
            if acc is not None:
                link(v.tensor_tensor(m.small[:, 0:PAIRS, H:2 * H], top[:, :, :].rearrange("l h p -> l p h"),
                                     bc_last(m.leader[:, :], H), ALU.mult))
            dve.wait_ge(exped, 1)

def common(m, sb):
    m.x = sb("x_nodes", [Q, W, D])
    m.ident, m.ident_b = sb("ident", [P, P]), sb("ident_b", [P, P], BF16)
    m.rows_before = sb("rows_before", [P, P])
    m.only0, m.only127 = sb("only0", [P, P]), sb("only127", [P, P])
    m.iota, m.iota_b = sb("iota", [P, 512]), sb("iota_b", [P, 256], BF16)
    m.lane = sb("lane", [P, 1])
    m.pair_src = sb("pair_src", [P, SLOTPAD], U32)
    m.pair_dst = sb("pair_dst", [P, PAIRS + 2 * G])
    m.pair_win = sb("pair_win", [P, PAIRS])
    m.pair_win_i = sb("pair_win_i", [1, PAIRS], I32)
    m.y_row = sb("y_row", [P, TILES + 8], U32)
    m.src_lane = sb("src_lane", [P, TILES + 3 * G])
    m.row_lo, m.row_hi = sb("row_lo", [P, TILES + 3 * G], BF16), sb("row_hi", [P, TILES], BF16)
    m.row_hi_f, m.s_row = sb("row_hi_f", [P, TILES + G]), sb("s_row", [P, TILES], U32)
    m.dst_loc, m.dst_win = sb("dst_loc", [P, TILES], BF16), sb("dst_win", [P, TILES], BF16)
    m.start_turned, m.end_turned = sb("start_turned", [P, H * PAIRS]), sb("end_turned", [P, H * PAIRS])
    m.first_pen, m.last_pen, m.cont_pen = (sb(n, [P, PAIRS]) for n in ("first_pen", "last_pen", "cont_pen"))
    m.fwd_pen, m.bwd_pen = sb("fwd_pen", [P, H, PAIRS]), sb("bwd_pen", [P, H, PAIRS])
    m.leader = sb("leader", [P, PAIRS])
    m.alpha = sb("alpha", [P, H, PAIRS])
    m.small = sb("small", [P, PAIRS + 2 * G, 2 * H])
    m.row_inv = sb("row_inv", [P, 3, ROWHI], BF16)
    m.deg_inv, m.deg_rsqrt = sb("deg_inv", [Q, W]), sb("deg_rsqrt", [Q, W])



def layer_norm(nc, dve, link, x, y, tmp, stats, eps, var_ready, std_ready, turn):
    v = nc.vector
    mean, var = stats[:, 0, :], stats[:, 1, :]
    link(v.reduce_sum(mean, x, AX))
    link(v.tensor_scalar(mean, mean, 1.0 / D, None, ALU.mult))
    link(v.tensor_tensor(y, x, bc_last(mean, D), ALU.subtract))
    for w in range(W):
        last = v.scalar_tensor_tensor(tmp[:, w, :], y[:, w, :], 1.0, y[:, w, :], ALU.mult, ALU.mult, accum_out=var[:, w:w + 1])
    link(last)
    v.tensor_scalar(var, var, 1.0 / D, eps, ALU.mult, ALU.add).then_inc(var_ready, 1)
    dve.wait_ge(std_ready, turn)
    link(v.reciprocal(mean, var))
    link(v.tensor_tensor(y, y, bc_last(mean, D), ALU.mult))


def std_of(nc, act, stats, var_ready, std_ready, turn):
    act.wait_ge(var_ready, turn)
    nc.scalar.activation(stats[:, 1, :], stats[:, 1, :], ACT.Sqrt).then_inc(std_ready, 1)


TG = (W + 3) // 4


def turn_windows_pe(nc, pe, m, src, banks, turned, copied, done=0):
    for g in range(TG):
        n = done + g
        if n >= 2:
            pe.wait_ge(copied, n - 1)
        for w in range(4 * g, min(4 * g + 4, W)):
            last = nc.tensor.transpose(banks[n % 2][:, (w % 4) * Q:(w % 4 + 1) * Q], src[:, w, :], m.ident[0:Q, 0:Q])
        last.then_inc(turned, 1)


def turn_windows_act(nc, act, m, dst, banks, turned, copied, done=0):
    for g in range(TG):
        n = done + g
        act.wait_ge(turned, n + 1)
        k = min(4, W - 4 * g)
        nc.scalar.copy(dst[:, 4 * g:4 * g + k, :].rearrange("d w q -> d (w q)"), banks[n % 2][:, 0:k * Q]).then_inc(copied, 1)


def relation_rows(nc, m, ins, y_table):
    with ExitStack() as ctx:
        sb, sem, bank = scope(nc, ctx)
        w0, w0t = sb("w0", [P, R, D]), sb("w0t", [P, R * D])
        xt = sb("xt0", [P, W, Q])
        stage = sb("y_stage", [Q, 2, R * D])
        tb = [bank(f"tb{i}") for i in range(2)]
        wb = [bank(f"wb{i}") for i in range(2)]
        yb = [bank(f"yb{i}") for i in range(4)]
        loaded, turned, copied, wt, wc = (sem(n) for n in ("w0_loaded", "x_turned", "xt_copied", "w_turned", "wt_copied"))
        y_done, y_left, y_right = sem("y_done"), sem("y_left"), sem("y_right")
        stored = [sem("y_stored0"), sem("y_stored1")]
        block = ctx.enter_context(nc.Block())

        @block.sync
        def _(sp):
            sp.dma_start(w0[:, :, :], ins["L0_gnn_weights"].rearrange("r i j -> i r j")).then_inc(loaded, 16)
            for w in range(W):
                sp.wait_ge(y_left, w + 1)
                sp.wait_ge(y_right, w + 1)
                sp.dma_start(y_table.rearrange("(n r) d -> n (r d)", r=R)[w * Q:(w + 1) * Q, :],
                             stage[:, w % 2, :]).then_inc(stored[w % 2], 16)
            sp.wait_ge(stored[0], 16 * ((W + 1) // 2))
            sp.wait_ge(stored[1], 16 * (W // 2))

        @block.tensor
        def _(pe):
            pe.wait_ge(loaded, 16)
            for r in range(R):
                last = nc.tensor.transpose(wb[r // 4][:, (r % 4) * D:(r % 4 + 1) * D], w0[:, r, :], m.ident[:, :])
            last.then_inc(wt, 1)
            turn_windows_pe(nc, pe, m, m.x, tb, turned, copied)
            pe.wait_ge(wc, 2)
            pe.wait_ge(copied, TG)
            for w in range(W):
                if w >= 2:
                    pe.wait_ge(y_left, w - 1)
                    pe.wait_ge(y_right, w - 1)
                for k in range(2):
                    last = nc.tensor.matmul(yb[2 * (w % 2) + k][0:Q, :], xt[:, w, :], w0t[:, k * 512:(k + 1) * 512],
                                            start=True, stop=True)
                last.then_inc(y_done, 1)

        @block.scalar
        def _(act):
            turn_windows_act(nc, act, m, xt, tb, turned, copied)
            for w in range(W):
                act.wait_ge(y_done, w + 1)
                if w >= 2:
                    act.wait_ge(stored[w % 2], 16 * (w // 2))
                nc.scalar.copy(stage[:, w % 2, 0:512], yb[2 * (w % 2)][0:Q, :]).then_inc(y_left, 1)

        @block.vector
        def _(dve):
            dve.wait_ge(wt, 1)
            nc.vector.tensor_copy(w0t[:, 0:512], wb[0][:, :]).then_inc(wc, 1)
            nc.vector.tensor_copy(w0t[:, 512:1024], wb[1][:, :]).then_inc(wc, 1)
            for w in range(W):
                dve.wait_ge(y_done, w + 1)
                if w >= 2:
                    dve.wait_ge(stored[w % 2], 16 * (w // 2))
                nc.vector.tensor_copy(stage[:, w % 2, 512:1024], yb[2 * (w % 2) + 1][0:Q, :]).then_inc(y_right, 1)


def fetch_and_count(nc, m, y_table, y_rows):
    with ExitStack() as ctx:
        sb, sem, bank = scope(nc, ctx)
        zeros = sb("zeros_b", [P, 512], BF16)
        y_idx, got = sb("y_idx", [P, 2, G], U32), sb("y_got", [P, 2, G, D])
        src, marks = sb("src_slot", [P, 2, G]), sb("marks", [P, G, P])
        dup, shift = sb("dup", [P, TILES]), sb("shift", [P, TILES])
        lo, hi = sb("lo_hot", [P, 2, G, ROWLO], BF16), sb("hi_hot", [P, 2, G, ROWHI], BF16)
        dl, dw = sb("dl_hot", [P, 2, G, Q], BF16), sb("dw_hot", [P, 2, G, W], BF16)
        part = sb("part", [P, ROWHI])
        deg_std = sb("deg_std", [Q, W])
        rows, degs, src_t = bank("rows_count"), bank("dst_count"), bank("src_t")
        start, hots, counted, done, copied, src_ready, turned, dup_ready, tick = (sem(n) for n in (
            "start", "hots", "counted", "all_counted", "idx_copied", "src_ready", "turned", "dup_ready", "tick"))
        chain, deg_ready, std_ready = sem("count_chain"), sem("deg_ready"), sem("deg_std_ready")
        aside = [sem("aside0"), sem("aside1")]
        come = m.come.pop()
        steps = TILES // (2 * G)
        block = ctx.enter_context(nc.Block())

        @block.gpsimd
        def _(pool):
            def gather(b):
                for j in range(G):
                    pool.indirect_dma_start(out=got[:, b, j, :], out_offset=None, in_=y_table[:, :],
                                            in_offset=bass.IndirectOffsetOnAxis(ap=y_idx[:, b, j:j + 1], axis=0)
                                            ).then_inc(come[b], 16)

            for b in range(2):
                pool.wait_ge(copied, b + 1)
                gather(b)
            with pool.Fori(0, steps) as i:
                for b in range(2):
                    pool.wait_ge(copied, 2 * i + (b + 3)).then_inc(tick, 1)
                    pool.wait_ge(aside[b], 16 * i + 16).then_inc(tick, 1)
                    gather(b)
            for b in range(2):
                pool.wait_ge(come[b], 16 * G * (steps + 1))

        @block.sync
        def _(sp):
            with sp.Fori(0, steps) as i:
                for b in range(2):
                    sp.wait_ge(come[b], 64 * i + 64)
                    sp.dma_start(y_rows[bass.ds(2 * i + b, 1), :, :].rearrange("a l n -> (a l) n"),
                                 got[:, b, :, :].rearrange("l j d -> l (j d)")).then_inc(aside[b], 16)
            for b in range(2):
                sp.wait_ge(aside[b], 16 * steps)

        @block.tensor
        def _(pe):
            mm = nc.tensor.matmul
            pe.wait_ge(start, 1)
            mm(rows[:, 0:ROWHI], zeros[:, 0:P], zeros[:, 0:ROWHI], start=True, stop=False)
            mm(degs[0:Q, 0:W], zeros[:, 0:Q], zeros[:, 0:W], start=True, stop=False)
            with pe.Fori(0, steps) as i:
                for b in range(2):
                    g = 2 * i + b
                    pe.wait_ge(src_ready, g + 1)
                    pe.wait_ge(dup_ready, g + 1)
                    for j in range(G):
                        last = nc.tensor.transpose(src_t[:, j * P:(j + 1) * P], src[:, b, j:j + 1].broadcast_to([P, P]),
                                                   m.ident[:, :])
                    last.then_inc(turned, 1)
                    pe.wait_ge(hots, g + 1)
                    for j in range(G):
                        mm(rows[:, 0:ROWHI], lo[:, b, j, :], hi[:, b, j, :], start=False, stop=False)
                        last = mm(degs[0:Q, 0:W], dl[:, b, j, :], dw[:, b, j, :], start=False, stop=False)
                    last.then_inc(counted, 1)
            mm(rows[:, 0:ROWHI], zeros[:, 0:P], zeros[:, 0:ROWHI], start=False, stop=True)
            mm(degs[0:Q, 0:W], zeros[:, 0:Q], zeros[:, 0:W], start=False, stop=True).then_inc(done, 1)

        @block.scalar
        def _(act):
            act.wait_ge(deg_ready, 1)
            nc.scalar.activation(deg_std[:, :], m.deg_inv[:, :], ACT.Sqrt).then_inc(std_ready, 1)

        @block.vector
        def _(dve):
            v, link = nc.vector, make_link(dve, chain)
            link(v.memset(zeros[:, :], 0.0))
            dve.sem_inc(start, 1)
            dve.sem_inc(counted, 2)
            dve.sem_inc(dup_ready, 1)
            for b in range(2):
                v.tensor_copy(y_idx[:, b, :], m.y_row[:, b * G:(b + 1) * G]).then_inc(copied, 1)
            with dve.Fori(0, steps) as i:
                for b in range(2):
                    g, at = 2 * i + b, i * (2 * G) + b * G
                    dve.wait_ge(counted, g + 1)
                    v.tensor_copy(src[:, b, :], m.src_lane[:, bass.ds(at, G)]).then_inc(src_ready, 1)
                    for hot, col, n in ((lo, m.row_lo, ROWLO), (hi, m.row_hi, ROWHI), (dl, m.dst_loc, Q), (dw, m.dst_win, W)):
                        last = v.tensor_tensor(hot[:, b, :, :], bc_last(col[:, bass.ds(at, G)], n),
                                               bc_mid(m.iota_b[:, 0:n], G), ALU.is_equal)
                    last.then_inc(hots, 1)
                    dve.wait_ge(turned, g + 1)
                    dve.wait_ge(dup_ready, g + 1)
                    for j in range(G):
                        last = v.scalar_tensor_tensor(marks[:, j, :], src_t[:, j * P:(j + 1) * P], src[:, b, j:j + 1],
                                                      m.rows_before[:, :], ALU.is_equal, ALU.mult,
                                                      accum_out=dup[:, bass.ds(at + j, 1)])
                    last.then_inc(dup_ready, 1)
                    dve.wait_ge(come[b], 64 * i + 64)
                    v.tensor_copy(y_idx[:, b, :], m.y_row[:, bass.ds(at + 2 * G, G)]).then_inc(copied, 1)
            dve.wait_ge(dup_ready, 2 * steps + 1)
            link(v.tensor_scalar(dup[:, :], dup[:, :], 1.0, None, ALU.min))
            link(v.tensor_scalar(part[:, 0:1], m.lane[:, :], float(DUMP), None, ALU.add))
            link(v.tensor_scalar(shift[:, :], m.src_lane[:, 0:TILES], -1.0, part[:, 0:1], ALU.mult, ALU.add))
            link(v.tensor_tensor(shift[:, :], shift[:, :], dup[:, :], ALU.mult))
            link(v.tensor_tensor(m.s_row[:, :], shift[:, :], m.src_lane[:, 0:TILES], ALU.add))
            dve.wait_ge(done, 1)
            link(v.tensor_scalar(part[:, :], rows[:, 0:ROWHI], 1.0, None, ALU.max))
            link(v.reciprocal(part[:, :], part[:, :]))
            for k in range(3):
                link(v.tensor_copy(m.row_inv[:, k, :], part[:, :]))
                if k < 2:
                    link(v.tensor_tensor(part[:, :], part[:, :], m.row_inv[:, k, :], ALU.subtract))
            link(v.tensor_scalar(m.deg_inv[:, :], degs[0:Q, 0:W], 1.0, None, ALU.add))
            dve.sem_inc(deg_ready, 1)
            dve.wait_ge(std_ready, 1)
            link(v.reciprocal(m.deg_inv[:, :], m.deg_inv[:, :]))
            link(v.reciprocal(m.deg_rsqrt[:, :], deg_std[:, :]))


def relation_edges(nc, m, y_rows, tables):
    with ExitStack() as ctx:
        sb, sem, bank = scope(nc, ctx)
        s_idx, src = sb("s_idx", [P, 2, G], U32), sb("src_slot", [P, 2, G])
        rows = sb("y_in", [P, 2, G, D])
        same, lo = sb("same_src", [P, 2, G, P]), sb("lo1", [P, 2, G, ROWLO], BF16)
        lot = sb("lot", [P, 2, G, P], BF16)
        looked, inv = sb("looked", [P, 2, G, ROWHI]), sb("inv_e", [P, 2, G])
        msg, total = sb("msg0", [P, 2, G, D]), sb("total", [P, 2, G, D])
        zrow = sb("zrow", [P, D])
        src_t = [bank("src_t0"), bank("src_t1")]
        lo_t, sums = bank("lo_t", (P, G, P), BF16), bank("sums")
        inv_b = [[bank(f"inv_b{b}{k}") for k in range(2)] for b in range(2)]
        produced, turned, same_ready, lot_ready, inv_found, inv_ready, msg_ready, sums_ready, tot_ready, s_ready, tick = (
            sem(n) for n in ("produced", "turned", "same_ready", "lot_ready", "inv_found", "inv_ready", "msg_ready",
                             "sums_ready", "tot_ready", "s_ready", "pool_tick"))
        come = [sem("come0"), sem("come1")]
        added = m.added
        steps = TILES // (2 * G)
        block = ctx.enter_context(nc.Block())

        @block.gpsimd
        def _(pool):
            pool.memset(zrow[:, :], 0.0).then_inc(tick, 1)
            pool.wait_ge(tick, 1)
            for a, b in ((0, ACCROWS // P // 2), (ACCROWS // P // 2, ACCROWS // P)):
                for j in range(G):
                    if a:
                        pool.wait_ge(added[j], 16)
                    pool.dma_start(tables[j].rearrange("(a p) d -> p a d", p=P)[:, a:b, :],
                                   bc_mid(zrow[:, :], b - a)).then_inc(added[j], 16)
            with pool.Fori(0, steps) as i:
                for b in range(2):
                    g = 2 * i + b
                    pool.wait_ge(s_ready, g + 1).then_inc(tick, 1)
                    pool.wait_ge(tot_ready, g + 2).then_inc(tick, 1)
                    for j in range(G):
                        pool.wait_ge(added[j], 16 * g + 32).then_inc(tick, 1)
                        pool.indirect_dma_start(out=tables[j][:, :],
                                                out_offset=bass.IndirectOffsetOnAxis(ap=s_idx[:, b, j:j + 1], axis=0),
                                                in_=total[:, b, j, :], in_offset=None,
                                                compute_op=ALU.add).then_inc(added[j], 16)
            for j in range(G):
                pool.wait_ge(added[j], 16 * (2 * steps) + 32)

        @block.sync
        def _(sp):
            with sp.Fori(0, steps) as i:
                for b in range(2):
                    g = 2 * i + b
                    sp.wait_ge(msg_ready, g + 1)
                    sp.dma_start(rows[:, b, :, :].rearrange("l j d -> l (j d)"),
                                 y_rows[bass.ds(g, 1), :, :].rearrange("a l n -> (a l) n")).then_inc(come[b], 16)

        @block.vector
        def _(dve):
            v = nc.vector
            dve.sem_inc(inv_ready, 1)

            def cols(at):
                return slice(at, at + G) if isinstance(at, int) else bass.ds(at, G)

            def produce(at, b):
                v.tensor_copy(src[:, b, :], m.src_lane[:, cols(at)])
                v.tensor_tensor(lo[:, b, :, :], bc_last(m.row_lo[:, cols(at)], ROWLO), bc_mid(m.iota_b[:, 0:ROWLO], G),
                                ALU.is_equal).then_inc(produced, 1)

            def compare(b, n):
                dve.wait_ge(turned, n + 1)
                dve.wait_ge(produced, n + 1)
                v.tensor_tensor(same[:, b, :, :], src_t[b][:, :].rearrange("p (j e) -> p j e", j=G),
                                bc_last(src[:, b, :], P), ALU.is_equal).then_inc(same_ready, 1)

            def look_up(at, b, n):
                dve.wait_ge(inv_found, n + 1)
                for j in range(G):
                    one = slice(at + j, at + j + 1) if isinstance(at, int) else bass.ds(at + j, 1)
                    last = v.scalar_tensor_tensor(looked[:, b, j, :], m.iota[:, 0:ROWHI], m.row_hi_f[:, one],
                                                  inv_b[b][j // 2][:, (j % 2) * ROWHI:(j % 2 + 1) * ROWHI],
                                                  ALU.is_equal, ALU.mult, accum_out=inv[:, b, j:j + 1])
                last.then_inc(inv_ready, 1)

            produce(0, 0)
            produce(G, 1)
            compare(0, 0)
            dve.wait_ge(same_ready, 1)
            produce(2 * G, 0)
            look_up(0, 0, 0)
            with dve.Fori(0, steps) as i:
                for b in range(2):
                    g, at = 2 * i + b, i * (2 * G) + b * G
                    dve.wait_ge(sums_ready, g + 1)
                    compare(1 - b, g + 1)
                    dve.wait_ge(same_ready, g + 2)
                    dve.wait_ge(turned, g + 2)
                    produce(at + 3 * G, 1 - b)
                    dve.wait_ge(msg_ready, g + 2)
                    dve.wait_ge(inv_ready, g + 2)
                    look_up(at + G, 1 - b, g + 1)
                    for j in range(G):
                        dve.wait_ge(added[j], 16 * g + 16)
                    v.tensor_copy(s_idx[:, b, :], m.s_row[:, bass.ds(at, G)]).then_inc(s_ready, 1)

        @block.tensor
        def _(pe):
            t = nc.tensor

            def turn(b, n):
                pe.wait_ge(produced, n + 1)
                for j in range(G):
                    t.transpose(src_t[b][:, j * P:(j + 1) * P], src[:, b, j:j + 1].broadcast_to([P, P]), m.ident[:, :])
                for j in range(G):
                    last = t.transpose(lo_t[:, j, :], lo[:, b, j, :], m.ident_b[:, :])
                last.then_inc(turned, 1)

            def find(b, n):
                pe.wait_ge(lot_ready, n + 1)
                for j in range(G):
                    out = inv_b[b][j // 2][:, (j % 2) * ROWHI:(j % 2 + 1) * ROWHI]
                    for k in range(3):
                        last = t.matmul(out, lot[:, b, j, :], m.row_inv[:, k, :], start=(k == 0), stop=(k == 2))
                last.then_inc(inv_found, 1)

            turn(0, 0)
            find(0, 0)
            turn(1, 1)
            with pe.Fori(0, steps) as i:
                for b in range(2):
                    g = 2 * i + b
                    pe.wait_ge(same_ready, g + 1)
                    pe.wait_ge(lot_ready, g + 2)
                    turn(b, g + 2)
                    pe.wait_ge(inv_ready, g + 1)
                    find(1 - b, g + 1)
                    pe.wait_ge(msg_ready, g + 3)
                    pe.wait_ge(tot_ready, g + 1)
                    for j in range(G):
                        last = t.matmul(sums[:, j * D:(j + 1) * D], same[:, b, j, :], msg[:, b, j, :], start=True, stop=True)
                    last.then_inc(sums_ready, 1)

        @block.scalar
        def _(act):
            s = nc.scalar
            act.sem_inc(tot_ready, 1)
            act.sem_inc(msg_ready, 2)
            act.sem_inc(sums_ready, 1)

            def keep(b, n):
                act.wait_ge(turned, n + 1)
                s.copy(lot[:, b, :, :], lo_t[:, :, :]).then_inc(lot_ready, 1)

            keep(0, 0)
            keep(1, 1)
            with act.Fori(0, steps) as i:
                for b in range(2):
                    g = 2 * i + b
                    act.wait_ge(inv_found, g + 1)
                    keep(b, g + 2)
                    act.wait_ge(inv_ready, g + 2)
                    act.wait_ge(come[b], 16 * i + 16)
                    for j in range(G):
                        last = s.activation(msg[:, b, j, :], rows[:, b, j, :], ACT.Copy, scale=inv[:, b, j:j + 1])
                    last.then_inc(msg_ready, 1)
                    act.wait_ge(sums_ready, g + 2)
                    for j in range(G):
                        act.wait_ge(added[j], 16 * g + 16)
                    s.copy(total[:, b, :, :].rearrange("p j d -> p (j d)"), sums[:, :]).then_inc(tot_ready, 1)


def make_link(dve, chain):
    count = [0]

    def link(op):
        count[0] += 1
        op.then_inc(chain, 1)
        dve.wait_ge(chain, count[0])
    return link


def gcn_nodes(nc, m, ins, tables, t_table):
    with ExitStack() as ctx:
        sb, sem, bank = scope(nc, ctx)
        part, tmp, stats = sb("part1", [Q, G, W, D]), sb("tmp1", [Q, W, D]), sb("stats1", [Q, 2, W])
        w1 = sb("gcn_w", [D, D])
        xt = sb("xt1", [P, W, Q])
        tb, hb = [bank(f"t1{i}") for i in range(2)], [bank(f"h1{i}") for i in range(4)]
        loaded, chain, var_ready, std_ready, x_ready = (sem(n) for n in ("loaded1", "chain1", "var1", "std1", "x1_ready"))
        turned, copied, h_done, h_read, t_ready, stored = (sem(n) for n in ("t1", "c1", "h_done", "h_read", "t_ready", "st1"))
        block = ctx.enter_context(nc.Block())

        @block.sync
        def _(sp):
            for j in range(G):
                sp.dma_start(part[:, j, :, :], nodes(tables[j][0:N, :])).then_inc(loaded, 16)
            sp.dma_start(w1[:, :], ins["L1_gnn_W"]).then_inc(loaded, 16)
            for w in range(0, W, 5):
                sp.wait_ge(t_ready, w + 5)
                sp.dma_start(nodes(t_table)[:, w:w + 5, :], tmp[:, w:w + 5, :]).then_inc(stored, 16)
            sp.wait_ge(stored, 16 * (W // 5))

        @block.vector
        def _(dve):
            v, link = nc.vector, make_link(dve, chain)
            dve.wait_ge(loaded, 16 * (G + 1))
            link(v.tensor_tensor(part[:, 0, :, :], part[:, 0, :, :], part[:, 1, :, :], ALU.add))
            link(v.tensor_tensor(part[:, 2, :, :], part[:, 2, :, :], part[:, 3, :, :], ALU.add))
            link(v.tensor_tensor(part[:, 0, :, :], part[:, 0, :, :], part[:, 2, :, :], ALU.add))
            link(v.scalar_tensor_tensor(tmp[:, :, :], part[:, 0, :, :], 0.0, m.x[:, :, :], ALU.max, ALU.add))
            layer_norm(nc, dve, link, tmp[:, :, :], m.x[:, :, :], part[:, 0, :, :], stats, EPS, var_ready, std_ready, 1)
            dve.sem_inc(x_ready, 1)
            for w in range(W):
                dve.wait_ge(h_done, w + 1)
                v.tensor_copy(m.h[:, w, :], hb[w % 4][0:Q, 0:D]).then_inc(h_read, 1)

        @block.scalar
        def _(act):
            std_of(nc, act, stats, var_ready, std_ready, 1)
            turn_windows_act(nc, act, m, xt, tb, turned, copied)
            for w in range(W):
                act.wait_ge(h_read, w + 1)
                nc.scalar.activation(tmp[:, w, :], m.h[:, w, :], ACT.Copy, scale=m.deg_rsqrt[:, w:w + 1]).then_inc(t_ready, 1)

        @block.tensor
        def _(pe):
            pe.wait_ge(x_ready, 1)
            turn_windows_pe(nc, pe, m, m.x, tb, turned, copied)
            pe.wait_ge(copied, TG)
            pe.wait_ge(loaded, 16 * (G + 1))
            for w in range(W):
                if w >= 4:
                    pe.wait_ge(h_read, w - 3)
                nc.tensor.matmul(hb[w % 4][0:Q, 0:D], xt[:, w, :], w1[:, :], start=True, stop=True).then_inc(h_done, 1)


STEPS = PAIRS // (2 * G)
POOL_HEADS = 2
WG = 2 * G


def windows(nc, m, engine, at, n):
    _, values = nc.values_load_multi_w_load_instructions(
        m.pair_win_i[0:1, bass.ds(at, n)], engines=[engine], min_val=0, max_val=W - 1, skip_runtime_bounds_check_because="a pair's window is a count of 24 comparisons")
    return values


class PairLoop:

    def __init__(self, nc, m, ctx, table, width=D, hot_dt=F32, slots=2):
        sb, sem, _ = scope(nc, ctx)
        self.nc, self.m, self.table = nc, m, table
        self.slots, self.steps = slots, PAIRS // (slots * G)
        self.idx = sb("idx", [P, slots, G], U32)
        self.got = sb("got", [P, slots, G, width])
        self.hot = sb("hot", [P, 2, G, Q], hot_dt)
        self.copied, self.hot_ready, self.tick = sem("idx_copied"), sem("hot_ready"), sem("pool_tick")
        self.come = m.come.pop()

    def gathers(self, pool, wait_free):
        def gather(b):
            for j in range(G):
                pool.indirect_dma_start(out=self.got[:, b, j, :], out_offset=None, in_=self.table[:, :],
                                        in_offset=bass.IndirectOffsetOnAxis(ap=self.idx[:, b, j:j + 1], axis=0)
                                        ).then_inc(self.come[b], 16)

        for b in range(self.slots):
            pool.wait_ge(self.copied, b + 1)
            gather(b)
        with pool.Fori(0, self.steps) as i:
            for b in range(self.slots):
                g = self.slots * i + b
                pool.wait_ge(self.copied, g + (self.slots + 1)).then_inc(self.tick, 1)
                wait_free(i, b, g)
                gather(b)
        for b in range(self.slots):
            pool.wait_ge(self.come[b], 16 * G * (self.steps + 1))

    def first_rows(self, dve):
        for b in range(self.slots):
            self.nc.vector.tensor_copy(self.idx[:, b, :], self.m.pair_src[:, b * G:(b + 1) * G]).then_inc(self.copied, 1)

    def one_hots(self, at, b):
        v, m = self.nc.vector, self.m
        cols = slice(at, at + G) if isinstance(at, int) else bass.ds(at, G)
        v.tensor_tensor(self.hot[:, b, :, :], bc_last(m.pair_dst[:, cols], Q), bc_mid(m.iota[:, 0:Q], G),
                        ALU.is_equal).then_inc(self.hot_ready, 1)

    def next_rows(self, dve, at, b, seen):
        cols = slice(at, at + G) if isinstance(at, int) else bass.ds(at, G)
        dve.wait_ge(self.come[b], 64 * seen)
        self.nc.vector.tensor_copy(self.idx[:, b, :], self.m.pair_src[:, cols]).then_inc(self.copied, 1)


def put_aside(nc, block, loop, aside, kept_rows, first):
    @block.sync
    def _(sp):
        with sp.Fori(0, loop.steps) as i:
            for b in range(loop.slots):
                sp.wait_ge(loop.come[b], 64 * i + 64)
                sp.dma_start(kept_rows[bass.ds(loop.slots * i + b, 1), :, :].rearrange("a l (j d) -> (a l) j d", j=G),
                             loop.got[:, b, :, first:first + D]).then_inc(aside[b], 16)
        for b in range(loop.slots):
            sp.wait_ge(aside[b], 16 * loop.steps)


def clear_banks(t, zeros, sums, stop):
    for k in range(8):
        last = t.matmul(sums[0:Q, k * 512:(k + 1) * 512], zeros[:, 0:Q], zeros[:, :], start=not stop, stop=stop)
    return last


def gcn_sums(nc, m, table):
    with ExitStack() as ctx:
        sb, sem, bank = scope(nc, ctx)
        loop = PairLoop(nc, m, ctx, table)
        zeros = sb("zeros", [P, 512], BF16)
        sums = bank("sums", (P, 8 * 512))
        used, zeroed, done = sem("used"), sem("zeroed"), sem("all_summed")
        block = ctx.enter_context(nc.Block())

        @block.gpsimd
        def _(pool):
            loop.gathers(pool, lambda i, b, g: pool.wait_ge(used, g + 1).then_inc(loop.tick, 1))

        @block.vector
        def _(dve):
            nc.vector.memset(zeros[:, :], 0.0).then_inc(zeroed, 1)
            loop.first_rows(dve)
            for b in range(2):
                loop.one_hots(b * G, b)
            with dve.Fori(0, STEPS) as i:
                for b in range(2):
                    g, at = 2 * i + b, i * (2 * G) + b * G
                    loop.next_rows(dve, at + 2 * G, b, i + 1)
                    dve.wait_ge(used, g + 1)
                    loop.one_hots(at + 2 * G, b)
            dve.wait_ge(done, 1)
            nc.vector.tensor_copy(m.agg[:, :, :].rearrange("q w d -> q (w d)"), sums[0:Q, 0:W * D])

        @block.tensor
        def _(pe):
            t = nc.tensor
            pe.wait_ge(zeroed, 1)
            clear_banks(t, zeros, sums, False)
            with pe.Fori(0, STEPS) as i:
                for b in range(2):
                    g, at = 2 * i + b, i * (2 * G) + b * G
                    ws = windows(nc, m, ENG.PE, at, G)
                    pe.wait_ge(loop.hot_ready, g + 1)
                    pe.wait_ge(loop.come[b], 64 * i + 64)
                    for j in range(G):
                        last = t.matmul(sums[0:Q, bass.ds(ws[j] * D, D)], loop.hot[:, b, j, :], loop.got[:, b, j, :],
                                        start=False, stop=False)
                    last.then_inc(used, 1)
            clear_banks(t, zeros, sums, True).then_inc(done, 1)


def three_parts(pool, parts, a, left, zero, chain, g, ready):
    pool.tensor_tensor(parts[:, :, 0, :], a, zero, ALU.add).then_inc(chain, 1)
    pool.wait_ge(chain, 3 * g + 1)
    pool.tensor_tensor(left, a, parts[:, :, 0, :], ALU.subtract).then_inc(chain, 1)
    pool.wait_ge(chain, 3 * g + 2)
    pool.tensor_tensor(parts[:, :, 1, :], left, zero, ALU.add).then_inc(chain, 1)
    pool.wait_ge(chain, 3 * g + 3)
    pool.tensor_tensor(parts[:, :, 2, :], left, parts[:, :, 1, :], ALU.subtract).then_inc(ready, 1)


def conv_sums(nc, m, v_rows):
    with ExitStack() as ctx:
        sb, sem, bank = scope(nc, ctx)
        zeros = sb("zeros", [P, 512], BF16)
        rows = sb("rows", [P, 2, WG, D])
        hot = sb("hot", [P, 2, WG, Q])
        msg = sb("msg", [P, 2, WG, D])
        wts = sb("wts", [P, 2, WG, H])
        hot_b, wts3 = sb("hot_b", [P, 2, WG, Q], BF16), sb("wts3", [P, 2, WG, 3, H], BF16)
        left, zero = sb("left", [P, 2, WG, H]), sb("zero", [P, WG, H])
        sums = bank("sums", (P, 8 * 512))
        dens = 7 * 512
        used, zeroed, done, hot_ready, wts_ready, msg_ready = (sem(n) for n in (
            "used", "zeroed", "all_summed", "hot_ready", "wts_ready", "msg_ready"))
        hot_b_ready, parts_ready, chain, zero_ready = (sem(n) for n in ("hot_b_ready", "parts_ready", "parts_chain", "zero_ready"))
        come = [sem("come0"), sem("come1")]
        steps = PAIRS // (2 * WG)
        block = ctx.enter_context(nc.Block())

        @block.sync
        def _(sp):
            with sp.Fori(0, steps) as i:
                for b in range(2):
                    sp.wait_ge(msg_ready, 2 * i + (b + 1))
                    sp.dma_start(rows[:, b, :, :].rearrange("l (a j) d -> l a (j d)", a=2),
                                 v_rows[bass.ds(i * 4 + 2 * b, 2), :, :].rearrange("a l n -> l a n")).then_inc(come[b], 16)

        @block.gpsimd
        def _(pool):
            pool.memset(zero[:, :, :], 0.0).then_inc(zero_ready, 1)
            pool.wait_ge(zero_ready, 1)
            with pool.Fori(0, steps) as i:
                for b in range(2):
                    g = 2 * i + b
                    pool.wait_ge(wts_ready, g + 1)
                    three_parts(pool, wts3[:, b, :, :, :], wts[:, b, :, :], left[:, b, :, :], zero[:, :, :], chain, g, parts_ready)

        @block.scalar
        def _(act):
            with act.Fori(0, steps) as i:
                for b in range(2):
                    act.wait_ge(hot_ready, 2 * i + (b + 1))
                    nc.scalar.copy(hot_b[:, b, :, :], hot[:, b, :, :]).then_inc(hot_b_ready, 1)

        @block.vector
        def _(dve):
            v = nc.vector
            v.memset(zeros[:, :], 0.0).then_inc(zeroed, 1)
            dve.sem_inc(msg_ready, 2)
            with dve.Fori(0, steps) as i:
                for b in range(2):
                    g, cols = 2 * i + b, bass.ds(i * (2 * WG) + b * WG, WG)
                    dve.wait_ge(used, g + 1)
                    v.tensor_copy(wts[:, b, :, :], m.small[:, cols, 0:H]).then_inc(wts_ready, 1)
                    v.tensor_tensor(hot[:, b, :, :], bc_last(m.pair_dst[:, cols], Q), bc_mid(m.iota[:, 0:Q], WG),
                                    ALU.is_equal).then_inc(hot_ready, 1)
                    dve.wait_ge(wts_ready, g + 1)
                    dve.wait_ge(come[b], 16 * i + 16)
                    v.tensor_tensor(msg[:, b, :, :].rearrange("p j (h c) -> p (j h) c", h=H),
                                    rows[:, b, :, :].rearrange("p j (h c) -> p (j h) c", h=H),
                                    bc_last(wts[:, b, :, :].rearrange("p j h -> p (j h)"), C), ALU.mult).then_inc(msg_ready, 1)
            dve.wait_ge(done, 1)
            v.tensor_copy(m.sums[:, :, :].rearrange("q w d -> q (w d)"), sums[0:Q, 0:W * D])
            v.reduce_sum(m.dens[:, :, :], sums[0:Q, dens:dens + W * 3 * H].rearrange("q (w k h) -> q w h k", k=3, h=H), AX)

        @block.tensor
        def _(pe):
            t = nc.tensor
            pe.sem_inc(used, 2)
            pe.wait_ge(zeroed, 1)
            clear_banks(t, zeros, sums, False)
            for _ in range(16):
                t.matmul(sums[0:Q, 7 * 512:8 * 512], zeros[:, 0:Q], zeros[:, :], start=False, stop=False)
            with pe.Fori(0, steps) as i:
                for b in range(2):
                    g, at = 2 * i + b, i * (2 * WG) + b * WG
                    ws = windows(nc, m, ENG.PE, at, WG)
                    pe.wait_ge(hot_ready, g + 1)
                    pe.wait_ge(msg_ready, g + 3)
                    pe.wait_ge(hot_b_ready, g + 1)
                    pe.wait_ge(parts_ready, g + 1)
                    for j in range(WG):
                        t.matmul(sums[0:Q, bass.ds(ws[j] * D, D)], hot[:, b, j, :], msg[:, b, j, :], start=False, stop=False)
                        last = t.matmul(sums[0:Q, bass.ds(ws[j] * (3 * H) + dens, 3 * H)], hot_b[:, b, j, :],
                                        wts3[:, b, j, :, :].rearrange("p k h -> p (k h)"),
                                        start=False, stop=False)
                    last.then_inc(used, 1)
            clear_banks(t, zeros, sums, True).then_inc(done, 1)


def gat_sums(nc, m, x_rows):
    with ExitStack() as ctx:
        sb, sem, bank = scope(nc, ctx)
        rows, hot = sb("rows", [P, 2, G, D]), sb("hot", [P, 2, G, Q])
        wts = sb("wts", [P, 2, G, 2 * H])
        msg = sb("msg", [P, 2, G, H * D])
        hot_b, wts3 = sb("hot_b", [P, 2, G, Q], BF16), sb("wts3", [P, 2, G, 3, 2 * H], BF16)
        left, zero = sb("left", [P, 2, G, 2 * H]), sb("zero", [P, G, 2 * H])
        sums = [bank(f"sums{j}", (P, 2 * 512)) for j in range(G)]
        wts_ready, hot_ready, first_heads_ready, heads_ready, summed, read = (sem(n) for n in (
            "wts_ready", "hot_ready", "first_heads_ready", "heads_ready", "summed", "sums_read"))
        parts_ready, chain, hot_b_ready, zero_ready = (sem(n) for n in ("parts_ready", "parts_chain", "hot_b_ready", "zero_ready"))
        come = [sem("come0"), sem("come1")]
        block = ctx.enter_context(nc.Block())

        @block.sync
        def _(sp):
            with sp.Fori(0, STEPS) as i:
                for b in range(2):
                    g = 2 * i + b
                    sp.wait_ge(first_heads_ready, g + 1)
                    sp.wait_ge(heads_ready, 4 * g + 4)
                    sp.dma_start(rows[:, b, :, :].rearrange("l j d -> l (j d)"),
                                 x_rows[bass.ds(g, 1), :, :].rearrange("a l n -> (a l) n")).then_inc(come[b], 16)

        @block.gpsimd
        def _(pool):
            pool.sem_inc(first_heads_ready, 2)
            pool.memset(zero[:, :, :], 0.0).then_inc(zero_ready, 1)
            pool.wait_ge(zero_ready, 1)
            with pool.Fori(0, STEPS) as i:
                for b in range(2):
                    g = 2 * i + b
                    pool.wait_ge(wts_ready, g + 1)
                    pool.wait_ge(come[b], 16 * i + 16)
                    for h in range(POOL_HEADS):
                        last = pool.tensor_tensor(msg[:, b, :, h * D:(h + 1) * D], rows[:, b, :, :],
                                                  wts[:, b, :, h:h + 1].broadcast_to([P, G, D]), ALU.mult)
                    last.then_inc(first_heads_ready, 1)
                    three_parts(pool, wts3[:, b, :, :, :], wts[:, b, :, :], left[:, b, :, :], zero[:, :, :], chain, g, parts_ready)

        @block.scalar
        def _(act):
            act.sem_inc(heads_ready, 2 * G)
            with act.Fori(0, STEPS) as i:
                for b in range(2):
                    g = 2 * i + b
                    act.wait_ge(wts_ready, g + 1)
                    act.wait_ge(hot_ready, g + 1)
                    nc.scalar.copy(hot_b[:, b, :, :], hot[:, b, :, :]).then_inc(hot_b_ready, 1)
                    act.wait_ge(come[b], 16 * i + 16)
                    for j in range(G):
                        for h in range(POOL_HEADS, H):
                            last = nc.scalar.activation(msg[:, b, j, h * D:(h + 1) * D], rows[:, b, j, :], ACT.Copy,
                                                        scale=wts[:, b, j, h:h + 1])
                        last.then_inc(heads_ready, 1)

        @block.vector
        def _(dve):
            v = nc.vector
            dve.sem_inc(read, G)

            def weights(at, b, g):
                dve.wait_ge(summed, 4 * g + 4)
                cols = slice(at, at + G) if isinstance(at, int) else bass.ds(at, G)
                v.tensor_copy(wts[:, b, :, :], m.small[:, cols, :]).then_inc(wts_ready, 1)
                v.tensor_tensor(hot[:, b, :, :], bc_last(m.pair_dst[:, cols], Q), bc_mid(m.iota[:, 0:Q], G),
                                ALU.is_equal).then_inc(hot_ready, 1)

            weights(0, 0, 0)
            weights(G, 1, 1)
            with dve.Fori(0, STEPS) as i:
                for b in range(2):
                    g, at = 2 * i + b, i * (2 * G) + b * G
                    ws = windows(nc, m, ENG.DVE, at, G)
                    for j in range(G):
                        if j == G - 1:
                            weights(at + 2 * G, b, g + 2)
                        row = m.acc[:, bass.ds(ws[j], 1), :].rearrange("q o d -> q (o d)")
                        dve.wait_ge(summed, 4 * g + (j + 9))
                        dve.wait_ge(read, 4 * g + (j + 4))
                        v.tensor_tensor(row, row, sums[j][0:Q, 0:H * D + 6 * H], ALU.add).then_inc(read, 1)

        @block.tensor
        def _(pe):
            pe.sem_inc(summed, 2 * G)
            t = nc.tensor
            with pe.Fori(0, STEPS) as i:
                for b in range(2):
                    g = 2 * i + b
                    pe.wait_ge(hot_ready, g + 1)
                    pe.wait_ge(first_heads_ready, g + 3)
                    for j in range(G):
                        pe.wait_ge(heads_ready, 4 * g + (j + 9))
                        pe.wait_ge(read, 4 * g + (j + 1))
                        t.matmul(sums[j][0:Q, 0:H * D], hot[:, b, j, :], msg[:, b, j, :], start=True, stop=True)
                        if j == 0:
                            pe.wait_ge(hot_b_ready, g + 1)
                            pe.wait_ge(parts_ready, g + 1)
                        t.matmul(sums[j][0:Q, H * D:H * D + 6 * H], hot_b[:, b, j, :], wts3[:, b, j, :, :].rearrange("p k h -> p (k h)"),
                                 start=True, stop=True).then_inc(summed, 1)


def batch_norm(nc, m, ins, x_table):
    with ExitStack() as ctx:
        sb, sem, bank = scope(nc, ctx)
        o, sq, stats = sb("gcn_out", [Q, W, D]), sb("gcn_sq", [Q, W, D]), sb("stats2", [Q, 2, W])
        vec = sb("gcn_vec", [P, 3, D])
        mean, rstd = sb("bn_mean", [Q, D]), sb("bn_rstd", [Q, D])
        ones = sb("ones_q", [Q, Q])
        sums = [bank("bn_sum"), bank("bn_sq")]
        loaded, chain, ready, summed, var_ready, std_ready, out_ready, stored = (sem(n) for n in (
            "loaded2", "chain2", "bn_ready", "bn_summed", "var2", "std2", "x2_ready", "stored2"))
        weights = sem("gat_weights")
        block = ctx.enter_context(nc.Block())

        @block.sync
        def _(sp):
            for k, name in enumerate(("L1_gnn_b", "L1_gnn_gamma", "L1_gnn_beta")):
                sp.dma_start(vec[:, k, :], row_bc(ins[name], P)).then_inc(loaded, 16)
            sp.dma_start(m.gat_wr[:, :], ins["L2_gnn_W_r"]).then_inc(weights, 16)
            sp.dma_start(m.gat_wl[:, :], ins["L2_gnn_W_l"]).then_inc(weights, 16)
            sp.dma_start(m.att[:, :], row_bc(ins["L2_gnn_att"].rearrange("h d -> (h d)"), P)).then_inc(weights, 16)
            for k, name in enumerate(("L2_gnn_b_l", "L2_gnn_b_r")):
                sp.dma_start(m.gat_bias[:, k, :], row_bc(ins[name], P)).then_inc(weights, 16)
            sp.wait_ge(weights, 80)
            sp.wait_ge(out_ready, 1)
            sp.dma_start(nodes(x_table)[:, :, 0:D], m.x[:, :, :]).then_inc(stored, 16)
            sp.wait_ge(stored, 16)

        @block.tensor
        def _(pe):
            for k, a in enumerate((o, sq)):
                for w in range(W):
                    if w % 5 == 0:
                        pe.wait_ge(ready, 5 * k + w // 5 + 1)
                    last = nc.tensor.matmul(sums[k][0:Q, 0:D], ones[:, :], a[:, w, :], start=(w == 0), stop=(w == W - 1))
                last.then_inc(summed, 1)

        @block.scalar
        def _(act):
            act.wait_ge(var_ready, 1)
            nc.scalar.activation(rstd[:, :], rstd[:, :], ACT.Sqrt).then_inc(std_ready, 1)
            std_of(nc, act, stats, var_ready, std_ready, 2)

        @block.vector
        def _(dve):
            v, link = nc.vector, make_link(dve, chain)
            link(v.memset(ones[:, :], 1.0))
            dve.wait_ge(loaded, 48)
            link(v.tensor_tensor(o[:, :, :], m.agg[:, :, :], bc_last(m.deg_rsqrt[:, :], D), ALU.mult))
            link(v.tensor_tensor(sq[:, :, :], m.h[:, :, :], bc_last(m.deg_inv[:, :], D), ALU.mult))
            link(v.tensor_tensor(o[:, :, :], o[:, :, :], sq[:, :, :], ALU.add))
            link(v.tensor_tensor(o[:, :, :], o[:, :, :], bc_mid(vec[0:Q, 0, :], W), ALU.add))
            for w in range(0, W, 5):
                a = o[:, w:w + 5, :]
                v.scalar_tensor_tensor(a, a, 0.01, a, ALU.mult, ALU.max).then_inc(ready, 1)
            dve.wait_ge(summed, 1)
            link(v.tensor_scalar(mean[:, :], sums[0][0:Q, 0:D], 1.0 / N, None, ALU.mult))
            link(v.tensor_tensor(o[:, :, :], o[:, :, :], bc_mid(mean[:, :], W), ALU.subtract))
            for w in range(0, W, 5):
                v.tensor_tensor(sq[:, w:w + 5, :], o[:, w:w + 5, :], o[:, w:w + 5, :], ALU.mult).then_inc(ready, 1)
            dve.wait_ge(summed, 2)
            v.tensor_scalar(rstd[:, :], sums[1][0:Q, 0:D], 1.0 / N, EPS, ALU.mult, ALU.add).then_inc(var_ready, 1)
            dve.wait_ge(std_ready, 1)
            link(v.reciprocal(rstd[:, :], rstd[:, :]))
            link(v.tensor_tensor(rstd[:, :], rstd[:, :], vec[0:Q, 1, :], ALU.mult))
            link(v.tensor_tensor(o[:, :, :], o[:, :, :], bc_mid(rstd[:, :], W), ALU.mult))
            link(v.tensor_tensor(o[:, :, :], o[:, :, :], bc_mid(vec[0:Q, 2, :], W), ALU.add))
            link(v.tensor_tensor(o[:, :, :], o[:, :, :], m.x[:, :, :], ALU.add))
            layer_norm(nc, dve, link, o[:, :, :], m.x[:, :, :], sq[:, :, :], stats, EPS, var_ready, std_ready, 2)
            dve.sem_inc(out_ready, 1)


def gat_nodes(nc, m, ins, x_table):
    with ExitStack() as ctx:
        sb, sem, bank = scope(nc, ctx)
        wr, bias, z = m.gat_wr, m.gat_bias, sb("z_self", [Q, 2, H * D])
        wide, junk = sb("wide", [P, H * D]), sb("junk", [Q, H, D])
        w_lin, b_lin = sb("w_lin", [D, 2, H]), sb("b_lin", [P, H])
        lin, kink = sb("lin", [Q, W, 2, H]), sb("kink", [Q, W, H])
        rest = sb("rest", [Q, 3, H * D])
        xt = sb("xt3", [P, W, Q])
        tb = [bank(f"g_t{i}") for i in range(2)]
        lb, rb = [bank(f"g_l{i}") for i in range(2)], [bank(f"g_r{i}") for i in range(2)]
        nb = bank("g_lin")
        turned, copied, done, zed, scored, w_ready, lin_done, lin_ready, chain, stored = (sem(n) for n in (
            "t3", "c3", "lr_done", "z_ready", "scored", "w_lin_ready", "lin_done", "lin_ready", "chain3", "stored3"))
        part0, part1, part2, less0, xr_ready = sem("part0"), sem("part1"), sem("part2"), sem("less0"), sem("xr_ready")
        block = ctx.enter_context(nc.Block())

        @block.sync
        def _(sp):
            sp.wait_ge(lin_ready, 1)
            sp.dma_start(nodes(x_table)[:, :, D:D + H], lin[:, :, 0, :]).then_inc(stored, 16)
            sp.wait_ge(stored, 16)

        @block.tensor
        def _(pe):
            turn_windows_pe(nc, pe, m, m.x, tb, turned, copied)
            pe.wait_ge(copied, TG)
            pe.wait_ge(w_ready, 1)
            for w in range(W):
                last = nc.tensor.matmul(nb[0:Q, w * 2 * H:(w + 1) * 2 * H], xt[:, w, :],
                                        w_lin[:, :, :].rearrange("d k h -> d (k h)"), start=True, stop=True)
            last.then_inc(lin_done, 1)
            for w in range(W):
                if w >= 2:
                    pe.wait_ge(zed, w - 1)
                nc.tensor.matmul(lb[w % 2][0:Q, :], xt[:, w, :], m.gat_wl[:, :], start=True, stop=True)
                nc.tensor.matmul(rb[w % 2][0:Q, :], xt[:, w, :], wr[:, :], start=True, stop=True).then_inc(done, 1)

        @block.scalar
        def _(act):
            turn_windows_act(nc, act, m, xt, tb, turned, copied)
            for w in range(W + 1):
                if w < W:
                    act.wait_ge(xr_ready, w + 1)
                    nc.scalar.copy(m.xr3[:, w, 0, :], rest[:, w % 3, :]).then_inc(part0, 1)
                if w:
                    act.wait_ge(less0, w)
                    nc.scalar.copy(m.xr3[:, w - 1, 1, :], rest[:, (w - 1) % 3, :]).then_inc(part1, 1)

        @block.gpsimd
        def _(pool):
            for w in range(W + 1):
                if w < W:
                    r = rest[:, w % 3, :]
                    pool.wait_ge(part0, w + 1)
                    pool.wait_ge(zed, w + 1)
                    pool.tensor_tensor(r, r, m.xr3[:, w, 0, :], ALU.subtract).then_inc(less0, 1)
                if w:
                    pool.wait_ge(less0, w)
                    pool.wait_ge(part1, w)
                    pool.tensor_tensor(m.xr3[:, w - 1, 2, :], rest[:, (w - 1) % 3, :], m.xr3[:, w - 1, 1, :],
                                       ALU.subtract).then_inc(part2, 1)

        @block.vector
        def _(dve):
            v, link = nc.vector, make_link(dve, chain)
            link(v.tensor_tensor(bias[:, 0, :], bias[:, 0, :], bias[:, 1, :], ALU.add))
            for out, a in ((w_lin[:, 0, :], m.gat_wl[:, :]), (w_lin[:, 1, :], wr[:, :]), (b_lin[:, :], bias[:, 0, :])):
                link(v.tensor_tensor(wide[:, :], a, m.att[:, :], ALU.mult))
                link(v.reduce_sum(out, wide[:, :].rearrange("q (h d) -> q h d", h=H), AX))
                link(v.tensor_scalar(out, out, 0.2, None, ALU.mult))
            dve.sem_inc(w_ready, 1)
            link(v.tensor_scalar(m.att[:, :], m.att[:, :], 0.8, None, ALU.mult))
            dve.wait_ge(lin_done, 1)
            link(v.tensor_copy(lin[:, :, :, :].rearrange("q w k h -> q (w k h)"), nb[0:Q, 0:W * 2 * H]))
            dve.sem_inc(lin_ready, 1)
            link(v.tensor_tensor(lin[:, :, 1, :], lin[:, :, 1, :], bc_mid(b_lin[0:Q, :], W), ALU.add))
            link(v.tensor_tensor(m.self_score[:, :, :], lin[:, :, 0, :], lin[:, :, 1, :], ALU.add))
            for k in range(3):
                link(v.tensor_copy(m.lin3[:, :, k, :], lin[:, :, 1, :]))
                if k < 2:
                    link(v.tensor_tensor(lin[:, :, 1, :], lin[:, :, 1, :], m.lin3[:, :, k, :], ALU.subtract))
            for w in range(W):
                dve.wait_ge(done, w + 1)
                if w >= 3:
                    dve.wait_ge(part2, w - 2)
                v.tensor_tensor(rest[:, w % 3, :], rb[w % 2][0:Q, :], bias[0:Q, 0, :], ALU.add).then_inc(xr_ready, 1)
                dve.wait_ge(xr_ready, w + 1)
                v.tensor_tensor(z[:, w % 2, :], lb[w % 2][0:Q, :], rest[:, w % 3, :], ALU.add).then_inc(zed, 1)
                dve.wait_ge(zed, w + 1)
                if w:
                    dve.wait_ge(scored, w)
                for h in range(H):
                    last = v.scalar_tensor_tensor(junk[:, h, :], z[:, w % 2, h * D:(h + 1) * D], 0.0,
                                                  m.att[0:Q, h * D:(h + 1) * D], ALU.max, ALU.mult,
                                                  accum_out=kink[:, w, h:h + 1])
                last.then_inc(scored, 1)
            dve.wait_ge(scored, W)
            v.tensor_tensor(m.self_score[:, :, :], m.self_score[:, :, :], kink[:, :, :], ALU.add)


def gat_scores(nc, m, x_table, x_rows):
    with ExitStack() as ctx:
        sb, sem, bank = scope(nc, ctx)
        loop = PairLoop(nc, m, ctx, x_table, width=D + H, hot_dt=BF16, slots=4)
        got, hot = loop.got, loop.hot
        got_t, hot_t = sb("got_t", [P, 2, G, P]), sb("hot_t", [Q, 2, G, P], BF16)
        junk = sb("junk", [P, G, H, D])
        score, src_lin = sb("score", [P, 2, G, H]), sb("src_lin", [P, 2, G, H])
        got_b, hot_b = bank("got_b"), bank("hot_b", (P, 1024), BF16)
        z = [bank(f"z{j}") for j in range(G)]
        lin = [bank(f"lin{b}", (P, G, 3, H)) for b in range(2)]
        turned, copied_t, z_done, z_read, lin_kept, summed, out = (sem(n) for n in (
            "turned", "copied_t", "z_done", "z_read", "lin_kept", "summed", "alpha_out"))
        aside = [sem(f"aside{b}") for b in range(4)]
        block = ctx.enter_context(nc.Block())

        put_aside(nc, block, loop, aside, x_rows, 0)

        @block.gpsimd
        def _(pool):
            def wait_free(i, b, g):
                pool.wait_ge(turned, g + 1).then_inc(loop.tick, 1)
                pool.wait_ge(lin_kept, g + 1).then_inc(loop.tick, 1)
                pool.wait_ge(aside[b], 16 * i + 16).then_inc(loop.tick, 1)

            loop.gathers(pool, wait_free)

        @block.vector
        def _(dve):
            v = nc.vector
            dve.sem_inc(z_read, G)
            dve.sem_inc(out, 2)
            loop.first_rows(dve)
            for b in range(2):
                loop.one_hots(b * G, b)
            with dve.Fori(0, loop.steps) as i:
                for slot in range(4):
                    g, at, b = 4 * i + slot, i * (4 * G) + slot * G, slot % 2
                    loop.next_rows(dve, at + 4 * G, slot, i + 1)
                    v.tensor_copy(src_lin[:, b, :, :], got[:, slot, :, D:D + H]).then_inc(lin_kept, 1)
                    dve.wait_ge(turned, g + 1)
                    loop.one_hots(at + 2 * G, b)
                    for j in range(G):
                        dve.wait_ge(z_done, 4 * g + (j + 1))
                        dve.wait_ge(z_read, 4 * g + (j + 1))
                        for h in range(H):
                            last = v.scalar_tensor_tensor(junk[:, j, h, :], z[j][:, h * D:(h + 1) * D], 0.0,
                                                          m.att[:, h * D:(h + 1) * D], ALU.max, ALU.mult,
                                                          accum_out=score[:, b, j, h:h + 1])
                        last.then_inc(z_read, 1)
                    v.reduce_sum(m.alpha[:, :, bass.ds(at, G)], lin[b][:, :, :, :].rearrange("p j k h -> p h j k"), AX
                                 ).then_inc(summed, 1)
                    dve.wait_ge(z_read, 4 * g + 2 * G)
                    v.tensor_tensor(score[:, b, :, :], score[:, b, :, :], src_lin[:, b, :, :], ALU.add).then_inc(summed, 1)
                    dve.wait_ge(summed, 2 * g + 2)
                    v.tensor_tensor(m.alpha[:, :, bass.ds(at, G)], m.alpha[:, :, bass.ds(at, G)],
                                    score[:, b, :, :].rearrange("p j h -> p h j"), ALU.add).then_inc(out, 1)

        @block.scalar
        def _(act):
            s = nc.scalar
            act.sem_inc(copied_t, 1)

            def copy(b, g):
                act.wait_ge(turned, g + 1)
                s.copy(got_t[:, b, :, :].rearrange("p j e -> p (j e)"), got_b[:, :])
                s.copy(hot_t[:, b, :, :].rearrange("p j e -> p (j e)"), hot_b[0:Q, 0:G * P]).then_inc(copied_t, 1)

            copy(0, 0)
            with act.Fori(0, STEPS) as i:
                for b in range(2):
                    copy(1 - b, 2 * i + (b + 1))

        @block.tensor
        def _(pe):
            t = nc.tensor

            def turn(slot, g, seen):
                b = slot % 2
                pe.wait_ge(loop.hot_ready, g + 1)
                pe.wait_ge(loop.come[slot], 64 * seen)
                pe.wait_ge(copied_t, g + 1)
                for j in range(G):
                    t.transpose(got_b[:, j * P:(j + 1) * P], got[:, slot, j, 0:D], m.ident[:, :])
                for j in range(G):
                    last = t.transpose(hot_b[0:Q, j * P:(j + 1) * P], hot[:, b, j, :], m.ident_b[:, :])
                last.then_inc(turned, 1)

            turn(0, 0, 1)
            with pe.Fori(0, loop.steps) as i:
                for slot in range(4):
                    g, at, b = 4 * i + slot, i * (4 * G) + slot * G, slot % 2
                    ws = windows(nc, m, ENG.PE, at, G)
                    turn((slot + 1) % 4, g + 1, i + 1 + slot // 3)
                    pe.wait_ge(copied_t, g + 2)
                    pe.wait_ge(out, g + 1)
                    for j in range(G):
                        pe.wait_ge(z_read, 4 * g + (j + 1))
                        t.matmul(z[j][:, :], got_t[:, b, j, :], m.gat_wl[:, :], start=True, stop=False)
                        t.matmul(lin[b][:, j, :, :], hot_t[:, b, j, :],
                                 m.lin3[:, bass.ds(ws[j], 1), :, :].rearrange("q o k h -> q (o k h)"), start=True, stop=True)
                        for k in range(3):
                            last = t.matmul(z[j][:, :], hot_t[:, b, j, :],
                                            m.xr3[:, bass.ds(ws[j], 1), k, :].rearrange("q o d -> q (o d)"),
                                            start=False, stop=(k == 2))
                        last.then_inc(z_done, 1)


def gat_finish(nc, m, ins):
    with ExitStack() as ctx:
        sb, sem, bank = scope(nc, ctx)
        edge, own, inv = (sb(n, [Q, W, H]) for n in ("edge_w", "self_w", "inv_w"))
        tails = sb("tails5", [Q, W, 2 * H])
        tmp, stats = sb("tmp5", [Q, W, D]), sb("stats5", [Q, 2, W])
        vec = sb("vec5", [P, 3, D])
        bl = sb("bl5", [P, H * D])
        at = sb("agg_t", [P, 2, H, Q])
        tb, ob = [bank(f"a_t{i}") for i in range(2)], [bank(f"a_o{i}") for i in range(2)]
        shares, scaled = sem("shares_ready"), sem("scaled")
        loaded, chain, shifted, exped, ready, turned, copied, done, read, var_ready, std_ready = (sem(n) for n in (
            "loaded5", "chain5", "shifted5", "exped5", "ready5", "t5", "c5", "o5", "r5", "var5", "std5"))
        block = ctx.enter_context(nc.Block())

        @block.sync
        def _(sp):
            for k, name in enumerate(("L2_gnn_gat_bias", "L2_gnn_ln_g", "L2_gnn_ln_b")):
                sp.dma_start(vec[:, k, :], row_bc(ins[name], P)).then_inc(loaded, 16)
            sp.dma_start(bl[:, :], row_bc(ins["L2_gnn_b_l"], P)).then_inc(loaded, 16)
            sp.wait_ge(loaded, 64)

        @block.scalar
        def _(act):
            act.wait_ge(shifted, 1)
            nc.scalar.activation(edge[:, :, :], edge[:, :, :], ACT.Exp)
            nc.scalar.activation(own[:, :, :], own[:, :, :], ACT.Exp).then_inc(exped, 1)

            def scale(w):
                for h in range(H):
                    a = m.acc[:, w, h * D:(h + 1) * D]
                    last = nc.scalar.activation(a, a, ACT.Copy, scale=edge[:, w, h:h + 1])
                last.then_inc(scaled, 1)

            act.wait_ge(shares, 1)
            scale(0)
            scale(1)
            for w in range(W):
                if w + 2 < W:
                    scale(w + 2)
                act.wait_ge(turned, w + 1)
                nc.scalar.copy(at[:, w % 2, :, :].rearrange("p h q -> p (h q)"), tb[w % 2][:, 0:H * Q]).then_inc(copied, 1)
            std_of(nc, act, stats, var_ready, std_ready, 1)

        @block.tensor
        def _(pe):
            def turn(w):
                pe.wait_ge(ready, w + 1)
                if w >= 2:
                    pe.wait_ge(copied, w - 1)
                for h in range(H):
                    last = nc.tensor.transpose(tb[w % 2][:, h * Q:(h + 1) * Q], m.acc[:, w, h * D:(h + 1) * D], m.ident[0:Q, 0:Q])
                last.then_inc(turned, 1)

            turn(0)
            for w in range(W):
                if w + 1 < W:
                    turn(w + 1)
                pe.wait_ge(copied, w + 1)
                if w >= 2:
                    pe.wait_ge(read, w - 1)
                for h in range(H):
                    last = nc.tensor.matmul(ob[w % 2][0:Q, 0:D], at[:, w % 2, h, :], m.gat_wl[:, h * D:(h + 1) * D],
                                            start=(h == 0), stop=(h == H - 1))
                last.then_inc(done, 1)

        @block.vector
        def _(dve):
            v, link = nc.vector, make_link(dve, chain)
            link(v.reduce_sum(tails[:, :, :], m.acc[:, :, H * D:].rearrange("q w (k e) -> q w e k", k=3), AX))
            den, emax = tails[:, :, 0:H], tails[:, :, H:2 * H]
            link(v.tensor_scalar(edge[:, :, :], den, 0.0, None, ALU.is_gt))
            link(v.tensor_scalar(edge[:, :, :], edge[:, :, :], 1.0, BIG, ALU.subtract, ALU.mult))
            link(v.tensor_tensor(edge[:, :, :], edge[:, :, :], emax, ALU.add))
            link(v.tensor_tensor(inv[:, :, :], edge[:, :, :], m.self_score[:, :, :], ALU.max))
            link(v.tensor_tensor(edge[:, :, :], edge[:, :, :], inv[:, :, :], ALU.subtract))
            link(v.tensor_tensor(own[:, :, :], m.self_score[:, :, :], inv[:, :, :], ALU.subtract))
            dve.sem_inc(shifted, 1)
            dve.wait_ge(exped, 1)
            link(v.tensor_tensor(inv[:, :, :], den, edge[:, :, :], ALU.mult))
            link(v.tensor_tensor(inv[:, :, :], inv[:, :, :], own[:, :, :], ALU.add))
            link(v.tensor_scalar(inv[:, :, :], inv[:, :, :], 1e-16, None, ALU.add))
            link(v.reciprocal(inv[:, :, :], inv[:, :, :]))
            link(v.tensor_scalar(inv[:, :, :], inv[:, :, :], 1.0 / H, None, ALU.mult))
            link(v.tensor_tensor(edge[:, :, :], edge[:, :, :], inv[:, :, :], ALU.mult))
            link(v.tensor_tensor(own[:, :, :], own[:, :, :], inv[:, :, :], ALU.mult))
            dve.sem_inc(shares, 1)
            dve.wait_ge(loaded, 64)
            for h in range(H):
                link(v.scalar_tensor_tensor(vec[:, 0, :], bl[:, h * D:(h + 1) * D], 1.0 / H, vec[:, 0, :], ALU.mult, ALU.add))
            link(v.tensor_tensor(tmp[:, :, :], m.x[:, :, :], bc_mid(vec[0:Q, 0, :], W), ALU.add))

            def out(w):
                dve.wait_ge(done, w + 1)
                v.tensor_tensor(tmp[:, w, :], tmp[:, w, :], ob[w % 2][0:Q, 0:D], ALU.add).then_inc(read, 1)

            for w in range(W):
                dve.wait_ge(scaled, w + 1)
                for h in range(H):
                    a = m.acc[:, w, h * D:(h + 1) * D]
                    last = v.scalar_tensor_tensor(a, m.x[:, w, :], own[:, w, h:h + 1], a, ALU.mult, ALU.add)
                last.then_inc(ready, 1)
                if w >= 3:
                    out(w - 3)
            for w in range(W - 3, W):
                out(w)
            dve.wait_ge(read, W)
            layer_norm(nc, dve, link, tmp[:, :, :], m.h[:, :, :], m.acc[:, :, 0:D], stats, EPS, var_ready, std_ready, 1)
            link(v.tensor_tensor(m.h[:, :, :], m.h[:, :, :], bc_mid(vec[0:Q, 1, :], W), ALU.mult))
            link(v.tensor_tensor(m.h[:, :, :], m.h[:, :, :], bc_mid(vec[0:Q, 2, :], W), ALU.add))


def feed_forward(nc, m, ins):
    with ExitStack() as ctx:
        sb, sem, bank = scope(nc, ctx)
        w1, w2 = sb("ff_w1", [D, 2 * D]), sb("ff_w2", [D, 2, D])
        b1, b2 = sb("ff_b1", [D, 2]), sb("ff_b2", [P, D])
        ht, ut = sb("ht", [P, W, Q]), sb("ut", [P, 2, W, Q])
        stats = sb("stats6", [Q, 2, W])
        tb, ub = ([bank(f"f_{k}{i}") for i in range(2)] for k in "tu")
        ob = [bank(f"f_o{i}") for i in range(4)]
        loaded, chain, turned, copied, u_done, u_read, o_done, o_read, var_ready, std_ready, leaky = (sem(n) for n in (
            "loaded6", "chain6", "t6", "c6", "u6", "ur6", "o6", "or6", "var6", "std6", "leaky6"))
        block = ctx.enter_context(nc.Block())
        tmp = m.acc[:, :, 0:D]

        @block.sync
        def _(sp):
            sp.dma_start(w1[:, :], ins["L2_gnn_W1"]).then_inc(loaded, 16)
            sp.dma_start(w2[:, :, :], ins["L2_gnn_W2"].rearrange("(c f) d -> f c d", c=2)).then_inc(loaded, 16)
            sp.dma_start(b1[:, :], ins["L2_gnn_b1"].rearrange("(c f) -> f c", c=2), allow_slow_non_contiguous=True).then_inc(loaded, 16)
            sp.dma_start(b2[:, :], row_bc(ins["L2_gnn_b2"], P)).then_inc(loaded, 16)
            sp.wait_ge(loaded, 64)

        @block.tensor
        def _(pe):
            turn_windows_pe(nc, pe, m, m.h, tb, turned, copied)
            pe.wait_ge(copied, TG)
            pe.wait_ge(loaded, 64)
            for g in range(TG):
                k = min(4, W - 4 * g)
                for c in range(2):
                    if g:
                        pe.wait_ge(u_read, 2 * (g - 1) + c + 1)
                    nc.tensor.matmul(ub[c][:, 0:k * Q], w1[:, c * D:(c + 1) * D],
                                     ht[:, 4 * g:4 * g + k, :].rearrange("d w q -> d (w q)"), start=True, stop=True).then_inc(u_done, 1)
            pe.wait_ge(leaky, 2 * TG)
            for w in range(W):
                if w >= 4:
                    pe.wait_ge(o_read, w - 3)
                for c in range(2):
                    last = nc.tensor.matmul(ob[w % 4][0:Q, 0:D], ut[:, c, w, :], w2[:, c, :], start=(c == 0), stop=(c == 1))
                last.then_inc(o_done, 1)

        @block.scalar
        def _(act):
            turn_windows_act(nc, act, m, ht, tb, turned, copied)
            act.wait_ge(loaded, 64)
            for g in range(TG):
                k = min(4, W - 4 * g)
                for c in range(2):
                    act.wait_ge(u_done, 2 * g + c + 1)
                    nc.scalar.activation(ut[:, c, 4 * g:4 * g + k, :].rearrange("d w q -> d (w q)"), ub[c][:, 0:k * Q],
                                         ACT.Identity, bias=b1[:, c:c + 1]).then_inc(u_read, 1)
            std_of(nc, act, stats, var_ready, std_ready, 1)

        @block.vector
        def _(dve):
            v, link = nc.vector, make_link(dve, chain)
            dve.wait_ge(loaded, 64)
            link(v.tensor_tensor(tmp, m.h[:, :, :], bc_mid(b2[0:Q, :], W), ALU.add))
            link(v.tensor_tensor(tmp, tmp, m.x[:, :, :], ALU.add))
            for n in range(2 * TG):
                dve.wait_ge(u_read, n + 1)
                u = ut[:, n % 2, 4 * (n // 2):min(4 * (n // 2) + 4, W), :]
                v.scalar_tensor_tensor(u, u, 0.2, u, ALU.mult, ALU.max).then_inc(leaky, 1)
            for w in range(W):
                dve.wait_ge(o_done, w + 1)
                v.tensor_tensor(m.acc[:, w, 0:D], m.acc[:, w, 0:D], ob[w % 4][0:Q, 0:D], ALU.add).then_inc(o_read, 1)
            dve.wait_ge(o_read, W)
            layer_norm(nc, dve, link, tmp, m.x[:, :, :], m.acc[:, :, D:2 * D], stats, EPS, var_ready, std_ready, 1)


def conv_nodes(nc, m, ins, n, src, kv_table):
    with ExitStack() as ctx:
        sb, sem, bank = scope(nc, ctx)
        w4, b4 = sb("w4", [D, 4, D]), sb("b4", [P, 4, D])
        xt = sb("xt7", [P, W, Q])
        tb, ob = [bank(f"q_t{i}") for i in range(2)], [bank(f"q_o{i}") for i in range(4)]
        loaded, turned, copied, done, read, stored = (sem(x) for x in ("loaded7", "t7", "c7", "o7", "r7", "stored7"))
        block = ctx.enter_context(nc.Block())

        @block.sync
        def _(sp):
            for k, x in enumerate("qkvs"):
                sp.dma_start(w4[:, k, :], ins[f"L3_gnn_W{x}{n}"]).then_inc(loaded, 16)
                sp.dma_start(b4[:, k, :], row_bc(ins[f"L3_gnn_b{x}{n}"], P)).then_inc(loaded, 16)
            for w in range(0, W, 5):
                sp.wait_ge(read, w + 5)
                sp.dma_start(nodes(kv_table)[:, w:w + 5, :], m.acc[:, w:w + 5, D:3 * D]).then_inc(stored, 16)
            sp.wait_ge(stored, 16 * (W // 5))

        @block.tensor
        def _(pe):
            turn_windows_pe(nc, pe, m, src, tb, turned, copied)
            pe.wait_ge(copied, TG)
            pe.wait_ge(loaded, 128)
            for w in range(W):
                if w >= 4:
                    pe.wait_ge(read, w - 3)
                nc.tensor.matmul(ob[w % 4][0:Q, :], xt[:, w, :], w4[:, :, :].rearrange("d k c -> d (k c)"),
                                 start=True, stop=True).then_inc(done, 1)

        @block.scalar
        def _(act):
            turn_windows_act(nc, act, m, xt, tb, turned, copied)

        @block.vector
        def _(dve):
            dve.wait_ge(loaded, 128)
            for w in range(W):
                dve.wait_ge(done, w + 1)
                nc.vector.tensor_tensor(m.acc[:, w, 0:4 * D], ob[w % 4][0:Q, :], b4[0:Q, :, :].rearrange("q k c -> q (k c)"),
                                        ALU.add).then_inc(read, 1)


def conv_scores(nc, m, kv_table, v_rows):
    with ExitStack() as ctx:
        sb, sem, bank = scope(nc, ctx)
        loop = PairLoop(nc, m, ctx, kv_table, width=2 * D, slots=4)
        got, hot = loop.got, loop.hot
        hot_t = sb("hot_t", [Q, 2, G, P])
        prod, score = sb("prod", [P, 2, G, D]), sb("score", [P, 2, G, H])
        hot_b = [bank(f"hot_b{i}") for i in range(2)]
        q_b = [bank(f"q_b{i}") for i in range(2)]
        turned, copied_t, q_done, out, chain, used = (sem(n) for n in (
            "turned", "copied_t", "q_done", "alpha_out", "chain8", "used"))
        aside = [sem(f"aside{b}") for b in range(4)]
        block = ctx.enter_context(nc.Block())

        put_aside(nc, block, loop, aside, v_rows, D)

        @block.gpsimd
        def _(pool):
            def wait_free(i, b, g):
                pool.wait_ge(used, g + 3).then_inc(loop.tick, 1)
                pool.wait_ge(aside[b], 16 * i + 16).then_inc(loop.tick, 1)

            loop.gathers(pool, wait_free)

        @block.vector
        def _(dve):
            v = nc.vector
            dve.sem_inc(used, 2)
            loop.first_rows(dve)
            for b in range(2):
                loop.one_hots(b * G, b)
            with dve.Fori(0, loop.steps) as i:
                for slot in range(4):
                    g, at, b = 4 * i + slot, i * (4 * G) + slot * G, slot % 2
                    loop.next_rows(dve, at + 4 * G, slot, i + 1)
                    dve.wait_ge(turned, g + 1)
                    loop.one_hots(at + 2 * G, b)
                    dve.wait_ge(q_done, g + 1)
                    v.tensor_tensor(prod[:, b, :, :], q_b[b][:, :].rearrange("p (j d) -> p j d", j=G),
                                    got[:, slot, :, 0:D], ALU.mult).then_inc(used, 1)
                    dve.wait_ge(used, g + 3)
                    v.reduce_sum(score[:, b, :, :], prod[:, b, :, :].rearrange("p j (h c) -> p j h c", h=H), AX).then_inc(chain, 1)
                    dve.wait_ge(chain, g + 1)
                    v.tensor_scalar(m.alpha[:, :, bass.ds(at, G)], score[:, b, :, :].rearrange("p j h -> p h j"),
                                    float(C) ** -0.5, None, ALU.mult).then_inc(out, 1)

        @block.scalar
        def _(act):
            def copy(b, g):
                act.wait_ge(turned, g + 1)
                nc.scalar.copy(hot_t[:, b, :, :].rearrange("p j e -> p (j e)"), hot_b[b][0:Q, :]).then_inc(copied_t, 1)

            copy(0, 0)
            with act.Fori(0, STEPS) as i:
                for b in range(2):
                    copy(1 - b, 2 * i + (b + 1))

        @block.tensor
        def _(pe):
            t = nc.tensor

            def turn(b, g):
                pe.wait_ge(loop.hot_ready, g + 1)
                for j in range(G):
                    last = t.transpose(hot_b[b][0:Q, j * P:(j + 1) * P], hot[:, b, j, :], m.ident[:, :])
                last.then_inc(turned, 1)

            turn(0, 0)
            with pe.Fori(0, STEPS) as i:
                for b in range(2):
                    g, at = 2 * i + b, i * (2 * G) + b * G
                    ws = windows(nc, m, ENG.PE, at, G)
                    turn(1 - b, g + 1)
                    pe.wait_ge(copied_t, g + 1)
                    pe.wait_ge(used, g + 1)
                    for j in range(G):
                        w = ws[j]
                        last = t.matmul(q_b[b][:, j * P:(j + 1) * P], hot_t[:, b, j, :],
                                        m.acc[:, bass.ds(w, 1), 0:D].rearrange("q o d -> q (o d)"), start=True, stop=True)
                    last.then_inc(q_done, 1)


def conv_finish(nc, m, last_layer, out):
    with ExitStack() as ctx:
        sb, sem, _ = scope(nc, ctx)
        inv = sb("inv9", [Q, W, H])
        tmp, stats = sb("tmp9", [Q, W, D]), sb("stats9", [Q, 2, W])
        chain, var_ready, std_ready, ready, stored = (sem(n) for n in ("chain9", "var9", "std9", "ready9", "stored9"))
        block = ctx.enter_context(nc.Block())

        if last_layer:
            @block.sync
            def _(sp):
                sp.wait_ge(ready, 1)
                sp.dma_start(nodes(out), m.h[:, :, :]).then_inc(stored, 16)
                sp.wait_ge(stored, 16)

            @block.scalar
            def _(act):
                std_of(nc, act, stats, var_ready, std_ready, 1)

        @block.vector
        def _(dve):
            v, link = nc.vector, make_link(dve, chain)
            link(v.tensor_scalar(inv[:, :, :], m.dens[:, :, :], 1e-30, None, ALU.max))
            link(v.reciprocal(inv[:, :, :], inv[:, :, :]))
            link(v.tensor_tensor(tmp[:, :, :].rearrange("q w (h c) -> q w h c", h=H),
                                 m.sums[:, :, :].rearrange("q w (h c) -> q w h c", h=H),
                                 inv[:, :, :].unsqueeze(3).broadcast_to([Q, W, H, C]), ALU.mult))
            link(v.tensor_tensor(tmp[:, :, :], tmp[:, :, :], m.acc[:, :, 3 * D:4 * D], ALU.add))
            if not last_layer:
                link(v.tensor_scalar(m.h[:, :, :], tmp[:, :, :], 0.0, None, ALU.max))
            else:
                link(v.tensor_tensor(tmp[:, :, :], tmp[:, :, :], m.x[:, :, :], ALU.add))
                layer_norm(nc, dve, link, tmp[:, :, :], m.h[:, :, :], m.acc[:, :, 0:D], stats, EPS, var_ready, std_ready, 1)
                dve.sem_inc(ready, 1)


def build(nc, ins, out):
    with ExitStack() as ctx:
        m = Mem()
        sb, sem, _ = scope(nc, ctx)
        common(m, sb)
        m.come = [[sem(f"come{n}_{b}") for b in range(4)] for n in range(5)]
        m.added = [sem(f"added{j}") for j in range(G)]
        y_table = nc.dram_tensor("y_table", [R * N, D], F32, kind="Internal").ap()
        tables = [nc.dram_tensor(f"agg{j}", [ACCROWS, D], F32, kind="Internal").ap() for j in range(G)]
        t_table = nc.dram_tensor("t_table", [N, D], F32, kind="Internal").ap()
        x_table = nc.dram_tensor("x_table", [N, D + H], F32, kind="Internal").ap()
        kv_table = nc.dram_tensor("kv_table", [N, 2 * D], F32, kind="Internal").ap()
        y_rows = nc.dram_tensor("y_rows", [TILES // G, P, G * D], F32, kind="Internal").ap()
        x_rows, v_rows = (nc.dram_tensor(n, [PAIRS // G, P, G * D], F32, kind="Internal").ap() for n in ("x_rows", "v_rows"))
        setup_phase(nc, m, ins)
        relation_rows(nc, m, ins, y_table)
        fetch_and_count(nc, m, y_table, y_rows)
        relation_edges(nc, m, y_rows, tables)
        m.self_score = sb("self_score", [Q, W, H])
        m.gat_wl, m.att = sb("gat_wl", [D, H * D]), sb("att", [P, H * D])
        m.gat_wr, m.gat_bias = sb("gat_wr", [D, H * D]), sb("gat_bias", [P, 2, H * D])
        with ExitStack() as gcn:
            hold, _, _ = scope(nc, gcn)
            m.h, m.agg = hold("gcn_h", [Q, W, D]), hold("gcn_agg", [Q, W, D])
            gcn_nodes(nc, m, ins, tables, t_table)
            gcn_sums(nc, m, t_table)
            batch_norm(nc, m, ins, x_table)
        with ExitStack() as gat:
            hold, _, _ = scope(nc, gat)
            m.xr3, m.lin3 = hold("xr3", [Q, W, 3, H * D], BF16), hold("lin3", [Q, W, 3, H], BF16)
            gat_nodes(nc, m, ins, x_table)
            gat_scores(nc, m, x_table, x_rows)
        m.acc = sb("acc", [Q, W, H * D + 6 * H])
        m.h = sb("h", [Q, W, D])
        segment_softmax(nc, m, m.acc)
        gat_sums(nc, m, x_rows)
        gat_finish(nc, m, ins)
        feed_forward(nc, m, ins)
        m.sums, m.dens = sb("sums", [Q, W, D]), sb("dens", [Q, W, H])
        for n, src in ((1, m.x), (2, m.h)):
            conv_nodes(nc, m, ins, n, src, kv_table)
            conv_scores(nc, m, kv_table, v_rows)
            segment_softmax(nc, m)
            conv_sums(nc, m, v_rows)
            conv_finish(nc, m, n == 2, out)


def kernel(**inputs):
    import numpy as _np
    import concourse.bacc as _bacc
    from concourse import mybir as _mybir
    from concourse.bass_utils import run_bass_kernel_spmd as _run

    nc = _bacc.Bacc("TRN2", target_bir_lowering=False, num_devices=1)
    arrays, args = {}, {}
    for name in inputs:
        a = _np.ascontiguousarray(inputs[name])
        arrays[f"in_{name}_dram"] = a
        args[name] = nc.dram_tensor(f"in_{name}_dram", a.shape, _mybir.dt.from_np(a.dtype), kind="ExternalInput").ap()
    out = nc.dram_tensor("out_0_dram", (N, D), F32, kind="ExternalOutput").ap()
    build(nc, args, out)
    r = _run(nc, [arrays], core_ids=[0])
    return r.results[0]["out_0_dram"]
```
